# Optimizing a Trainium2 kernel written in Bass

```python
import numpy as np
import jax
import jax.numpy as jnp

def _softmax(x, axis=-1):
    return jax.nn.softmax(x, axis=axis)

def _gelu(x):
    return jax.nn.gelu(x, approximate=True)

def _silu(x):
    return jax.nn.silu(x)

def _sigmoid(x):
    return jax.nn.sigmoid(x)

def _layernorm(x, axis=-1, eps=1e-05):
    m = jnp.mean(x, axis=axis, keepdims=True)
    v = jnp.var(x, axis=axis, keepdims=True)
    return (x - m) / jnp.sqrt(v + eps)

def _scatter_add(tgt, idx, src, axis=0):
    return tgt.at[idx].add(src)

def _segment_sum(src, seg, n):
    return jax.ops.segment_sum(src, seg, n)
kernel_name = 'mk_adaln_attn_ffn_d2_seqx_r8_e5ee10'

def setup_inputs(seed: int=0):
    np.random.seed(seed)
    _w = jnp.asarray

    def _rec_inputs():
        import jax
        import jax.numpy as jnp
        _rk = jax.random.key(seed)
        x = -0.000125 + 0.9999 * jax.random.normal(jax.random.fold_in(_rk, 1), (4, 256, 256), jnp.float32)
        _lenS = 256 - jax.random.randint(jax.random.fold_in(_rk, 7), (4,), 0, max(1, 256 // 4) + 1, jnp.int32)
        _lenS2 = 256 - jax.random.randint(jax.random.fold_in(_rk, 8), (4,), 0, max(1, 256 // 4) + 1, jnp.int32)
        fside_BxSxS_0 = -1.52775e-05 + 0.999936 * jax.random.normal(jax.random.fold_in(_rk, 11), (4, 256, 256), jnp.float32)
        cond_512 = -5.03954e-05 + 1.00559 * jax.random.normal(jax.random.fold_in(_rk, 12), (4, 64), jnp.float32)
        return (x, fside_BxSxS_0, cond_512)
    x, fside_BxSxS_0, cond_512 = _rec_inputs()

    def _L0_cond_setup():
        import jax, jax.numpy as jnp
        from jax import lax
        import numpy as np
        B, T, C, TD = (8, 256, 256, 64)

        def _bi_wkv(r, k, v, w, u, time_emb):
            tf = jax.nn.sigmoid(jnp.sum(time_emb, axis=-1))[:, None, None]
            decay = jnp.exp(-jnp.exp(w.astype(jnp.float32)))[None, :] * (0.5 + 0.5 * tf[:, :, 0])
            kf = k.astype(jnp.float32)
            vf = v.astype(jnp.float32)
            ek = jnp.exp(jnp.minimum(kf, 30.0))
            ekv = ek * vf

            def step(carry, x):
                a, b = carry
                ekv_t, ek_t = x
                a = a * decay + ekv_t
                b = b * decay + ek_t
                return ((a, b), (a, b))
            ekv_t = jnp.swapaxes(ekv, 0, 1)
            ek_t = jnp.swapaxes(ek, 0, 1)
            init = (jnp.zeros_like(decay), jnp.zeros_like(decay))
            _, (nf, df) = lax.scan(step, init, (ekv_t, ek_t))
            _, (nb, db) = lax.scan(step, init, (ekv_t, ek_t), reverse=True)
            nf = jnp.swapaxes(nf, 0, 1)
            df = jnp.swapaxes(df, 0, 1)
            nb = jnp.swapaxes(nb, 0, 1)
            db = jnp.swapaxes(db, 0, 1)
            euk = jnp.exp(jnp.minimum(u.astype(jnp.float32)[None, None, :] + kf, 30.0))
            num = nf + nb - ekv + euk * vf
            den = df + db - ek + euk
            base = jax.nn.sigmoid(r.astype(jnp.float32)) * (num / jnp.maximum(den, 1e-08))
            out = base * (0.8 + 0.2 * tf)
            return out.astype(r.dtype)
        key = jax.random.key(seed)
        ks = jax.random.split(key, 6)
        return {'r': jax.random.normal(ks[0], (B, T, C), dtype=jnp.float32), 'k': jax.random.normal(ks[1], (B, T, C), dtype=jnp.float32), 'v': jax.random.normal(ks[2], (B, T, C), dtype=jnp.float32), 'w': jax.random.normal(ks[3], (C,), dtype=jnp.float32), 'u': jax.random.normal(ks[4], (C,), dtype=jnp.float32), 'time_emb': jax.random.normal(ks[5], (B, TD), dtype=jnp.float32)}
    _L0_cond_all = _L0_cond_setup()
    _L0_cond_in = {k: v for k, v in _L0_cond_all.items() if k in ('w', 'u')}
    del _L0_cond_all

    def _L0_attn_setup():
        import jax, jax.numpy as jnp
        import numpy as np
        import math
        H = 16
        DN = 128
        DR = 64
        DV = 128
        ROPE_BASE = 10000.0

        def _rope_cos_sin(seq_len, dim, dtype):
            inv_freq = 1.0 / ROPE_BASE ** (jnp.arange(0, dim, 2, dtype=jnp.float32) / dim)
            t = jnp.arange(seq_len, dtype=jnp.float32)
            freqs = t[:, None] * inv_freq[None, :]
            return (jnp.cos(freqs).astype(dtype), jnp.sin(freqs).astype(dtype))

        def _apply_rope(x, cos, sin):
            half = x.shape[-1] // 2
            x1, x2 = (x[..., :half], x[..., half:])
            c = cos[None, :, None, :]
            s = sin[None, :, None, :]
            return jnp.concatenate([x1 * c - x2 * s, x1 * s + x2 * c], axis=-1)
        key = jax.random.key(seed)
        ks = jax.random.split(key, 5)
        hidden = 256
        B, S = (1, 256)
        q_size = H * (DN + DR)
        v_size = H * DV
        std = 0.02
        return {'hidden_states': jax.random.normal(ks[0], (B, S, hidden), jnp.float32), 'Wq': jax.random.normal(ks[1], (q_size, hidden), jnp.float32) * std, 'Wk': jax.random.normal(ks[2], (q_size, hidden), jnp.float32) * std, 'Wv': jax.random.normal(ks[3], (v_size, hidden), jnp.float32) * std, 'Wo': jax.random.normal(ks[4], (hidden, v_size), jnp.float32) * std}
    _L0_attn_all = _L0_attn_setup()
    _L0_attn_in = {k: v for k, v in _L0_attn_all.items() if k in ('Wq', 'Wk', 'Wv', 'Wo')}
    del _L0_attn_all

    def _L0_cond2_setup():
        import jax, jax.numpy as jnp
        from jax import lax
        import numpy as np
        B, T, C, TD = (8, 256, 256, 64)

        def _bi_wkv(r, k, v, w, u, time_emb):
            tf = jax.nn.sigmoid(jnp.sum(time_emb, axis=-1))[:, None, None]
            decay = jnp.exp(-jnp.exp(w.astype(jnp.float32)))[None, :] * (0.5 + 0.5 * tf[:, :, 0])
            kf = k.astype(jnp.float32)
            vf = v.astype(jnp.float32)
            ek = jnp.exp(jnp.minimum(kf, 30.0))
            ekv = ek * vf

            def step(carry, x):
                a, b = carry
                ekv_t, ek_t = x
                a = a * decay + ekv_t
                b = b * decay + ek_t
                return ((a, b), (a, b))
            ekv_t = jnp.swapaxes(ekv, 0, 1)
            ek_t = jnp.swapaxes(ek, 0, 1)
            init = (jnp.zeros_like(decay), jnp.zeros_like(decay))
            _, (nf, df) = lax.scan(step, init, (ekv_t, ek_t))
            _, (nb, db) = lax.scan(step, init, (ekv_t, ek_t), reverse=True)
            nf = jnp.swapaxes(nf, 0, 1)
            df = jnp.swapaxes(df, 0, 1)
            nb = jnp.swapaxes(nb, 0, 1)
            db = jnp.swapaxes(db, 0, 1)
            euk = jnp.exp(jnp.minimum(u.astype(jnp.float32)[None, None, :] + kf, 30.0))
            num = nf + nb - ekv + euk * vf
            den = df + db - ek + euk
            base = jax.nn.sigmoid(r.astype(jnp.float32)) * (num / jnp.maximum(den, 1e-08))
            out = base * (0.8 + 0.2 * tf)
            return out.astype(r.dtype)
        key = jax.random.key(seed)
        ks = jax.random.split(key, 6)
        return {'r': jax.random.normal(ks[0], (B, T, C), dtype=jnp.float32), 'k': jax.random.normal(ks[1], (B, T, C), dtype=jnp.float32), 'v': jax.random.normal(ks[2], (B, T, C), dtype=jnp.float32), 'w': jax.random.normal(ks[3], (C,), dtype=jnp.float32), 'u': jax.random.normal(ks[4], (C,), dtype=jnp.float32), 'time_emb': jax.random.normal(ks[5], (B, TD), dtype=jnp.float32)}
    _L0_cond2_all = _L0_cond2_setup()
    _L0_cond2_in = {k: v for k, v in _L0_cond2_all.items() if k in ('w', 'u')}
    del _L0_cond2_all

    def _L0_ffn_setup():
        import jax, jax.numpy as jnp
        import numpy as np
        B, S, D, F = (4, 256, 256, 1024)
        EPS = 1e-05

        def activation_quant(x):
            scale = 127.0 / jnp.clip(jnp.max(jnp.abs(x), axis=-1, keepdims=True), EPS, None)
            return jnp.clip(jnp.round(x * scale), -128.0, 127.0) / scale

        def weight_quant(w):
            scale = 1.0 / jnp.clip(jnp.mean(jnp.abs(w)), EPS, None)
            return jnp.clip(jnp.round(w * scale), -1.0, 1.0) / scale

        def bitlinear(x, w, b):
            xq = activation_quant(x)
            wq = weight_quant(w)
            return jnp.einsum('bsd,fd->bsf', xq, wq) + b

        def layernorm(x, gamma, beta):
            mu = jnp.mean(x, axis=-1, keepdims=True)
            var = jnp.var(x, axis=-1, keepdims=True)
            return (x - mu) * jax.lax.rsqrt(var + EPS) * gamma + beta
        key = jax.random.key(seed)
        ks = jax.random.split(key, 7)
        return {'x': jax.random.normal(ks[0], (B, S, D), dtype=jnp.float32), 'w1': jax.random.normal(ks[1], (F, D), dtype=jnp.float32) * D ** (-0.5), 'b1': jax.random.normal(ks[2], (F,), dtype=jnp.float32) * 0.01, 'gamma': jnp.ones((F,), dtype=jnp.float32), 'beta': jnp.zeros((F,), dtype=jnp.float32), 'w2': jax.random.normal(ks[3], (D, F), dtype=jnp.float32) * F ** (-0.5), 'b2': jax.random.normal(ks[4], (D,), dtype=jnp.float32) * 0.01}
    _L0_ffn_all = _L0_ffn_setup()
    _L0_ffn_in = {k: v for k, v in _L0_ffn_all.items() if k in ('w1', 'b1', 'gamma', 'beta', 'w2', 'b2')}
    del _L0_ffn_all

    def _L1_cond_setup():
        import jax, jax.numpy as jnp
        from jax import lax
        import numpy as np
        B, T, C, TD = (8, 256, 256, 64)

        def _bi_wkv(r, k, v, w, u, time_emb):
            tf = jax.nn.sigmoid(jnp.sum(time_emb, axis=-1))[:, None, None]
            decay = jnp.exp(-jnp.exp(w.astype(jnp.float32)))[None, :] * (0.5 + 0.5 * tf[:, :, 0])
            kf = k.astype(jnp.float32)
            vf = v.astype(jnp.float32)
            ek = jnp.exp(jnp.minimum(kf, 30.0))
            ekv = ek * vf

            def step(carry, x):
                a, b = carry
                ekv_t, ek_t = x
                a = a * decay + ekv_t
                b = b * decay + ek_t
                return ((a, b), (a, b))
            ekv_t = jnp.swapaxes(ekv, 0, 1)
            ek_t = jnp.swapaxes(ek, 0, 1)
            init = (jnp.zeros_like(decay), jnp.zeros_like(decay))
            _, (nf, df) = lax.scan(step, init, (ekv_t, ek_t))
            _, (nb, db) = lax.scan(step, init, (ekv_t, ek_t), reverse=True)
            nf = jnp.swapaxes(nf, 0, 1)
            df = jnp.swapaxes(df, 0, 1)
            nb = jnp.swapaxes(nb, 0, 1)
            db = jnp.swapaxes(db, 0, 1)
            euk = jnp.exp(jnp.minimum(u.astype(jnp.float32)[None, None, :] + kf, 30.0))
            num = nf + nb - ekv + euk * vf
            den = df + db - ek + euk
            base = jax.nn.sigmoid(r.astype(jnp.float32)) * (num / jnp.maximum(den, 1e-08))
            out = base * (0.8 + 0.2 * tf)
            return out.astype(r.dtype)
        key = jax.random.key(seed)
        ks = jax.random.split(key, 6)
        return {'r': jax.random.normal(ks[0], (B, T, C), dtype=jnp.float32), 'k': jax.random.normal(ks[1], (B, T, C), dtype=jnp.float32), 'v': jax.random.normal(ks[2], (B, T, C), dtype=jnp.float32), 'w': jax.random.normal(ks[3], (C,), dtype=jnp.float32), 'u': jax.random.normal(ks[4], (C,), dtype=jnp.float32), 'time_emb': jax.random.normal(ks[5], (B, TD), dtype=jnp.float32)}
    _L1_cond_all = _L1_cond_setup()
    _L1_cond_in = {k: v for k, v in _L1_cond_all.items() if k in ('w', 'u')}
    del _L1_cond_all

    def _L1_attn_setup():
        import jax, jax.numpy as jnp
        import numpy as np
        B, S, HID = (1, 256, 256)
        H, NOPE, ROPE, VDIM = (16, 128, 64, 128)
        QR, KVR = (192, 64)
        IH, ID = (16, 128)
        TOPK = 64
        THETA = 10000.0
        EPS = 1e-06
        SCALE = (NOPE + ROPE) ** (-0.5)
        NEG = -1000000000.0

        def _cos_sin(s, dim, dtype):
            inv = 1.0 / THETA ** (np.arange(0, dim, 2, dtype=np.float32) / dim)
            t = np.arange(s, dtype=np.float32)
            f = np.outer(t, inv)
            emb = np.concatenate([f, f], -1)
            return (jnp.asarray(np.cos(emb), dtype), jnp.asarray(np.sin(emb), dtype))

        def _rope(x, cos, sin):
            x1, x2 = jnp.split(x, 2, axis=-1)
            rot = jnp.concatenate([-x2, x1], axis=-1)
            return x * cos[None, :, None, :] + rot * sin[None, :, None, :]

        def _rmsnorm(x, w):
            v = jnp.mean(x.astype(jnp.float32) ** 2, -1, keepdims=True)
            return (x.astype(jnp.float32) * jax.lax.rsqrt(v + EPS)).astype(x.dtype) * w

        def _layernorm(x, w, b):
            m = jnp.mean(x, -1, keepdims=True)
            v = jnp.var(x, -1, keepdims=True)
            return (x - m) * jax.lax.rsqrt(v + EPS) * w + b
        key = jax.random.key(seed)
        ks = jax.random.split(key, 12)
        g = lambda k, shp: jax.random.normal(k, shp, jnp.float32) * 0.02
        return {'hidden_states': jax.random.normal(ks[0], (B, S, HID), jnp.float32), 'q_a_w': g(ks[1], (QR, HID)), 'q_a_ln_w': jnp.ones((QR,), jnp.float32), 'q_b_w': g(ks[2], (H * (NOPE + ROPE), QR)), 'kv_a_w': g(ks[3], (KVR + ROPE, HID)), 'kv_a_ln_w': jnp.ones((KVR,), jnp.float32), 'kv_b_w': g(ks[4], (H * (NOPE + VDIM), KVR)), 'o_w': g(ks[5], (HID, H * VDIM)), 'idx_wq_b_w': g(ks[6], (IH * ID, QR)), 'idx_wk_w': g(ks[7], (ID, HID)), 'idx_kn_w': jnp.ones((ID,), jnp.float32), 'idx_kn_b': jnp.zeros((ID,), jnp.float32), 'idx_wproj_w': g(ks[8], (IH, HID))}
    _L1_attn_all = _L1_attn_setup()
    _L1_attn_in = {k: v for k, v in _L1_attn_all.items() if k in ('q_a_w', 'q_a_ln_w', 'q_b_w', 'kv_a_w', 'kv_a_ln_w', 'kv_b_w', 'o_w', 'idx_wq_b_w', 'idx_wk_w', 'idx_kn_w', 'idx_kn_b', 'idx_wproj_w')}
    del _L1_attn_all

    def _L1_cond2_setup():
        import jax, jax.numpy as jnp
        from jax import lax
        import numpy as np
        B, T, C, TD = (8, 256, 256, 64)

        def _bi_wkv(r, k, v, w, u, time_emb):
            tf = jax.nn.sigmoid(jnp.sum(time_emb, axis=-1))[:, None, None]
            decay = jnp.exp(-jnp.exp(w.astype(jnp.float32)))[None, :] * (0.5 + 0.5 * tf[:, :, 0])
            kf = k.astype(jnp.float32)
            vf = v.astype(jnp.float32)
            ek = jnp.exp(jnp.minimum(kf, 30.0))
            ekv = ek * vf

            def step(carry, x):
                a, b = carry
                ekv_t, ek_t = x
                a = a * decay + ekv_t
                b = b * decay + ek_t
                return ((a, b), (a, b))
            ekv_t = jnp.swapaxes(ekv, 0, 1)
            ek_t = jnp.swapaxes(ek, 0, 1)
            init = (jnp.zeros_like(decay), jnp.zeros_like(decay))
            _, (nf, df) = lax.scan(step, init, (ekv_t, ek_t))
            _, (nb, db) = lax.scan(step, init, (ekv_t, ek_t), reverse=True)
            nf = jnp.swapaxes(nf, 0, 1)
            df = jnp.swapaxes(df, 0, 1)
            nb = jnp.swapaxes(nb, 0, 1)
            db = jnp.swapaxes(db, 0, 1)
            euk = jnp.exp(jnp.minimum(u.astype(jnp.float32)[None, None, :] + kf, 30.0))
            num = nf + nb - ekv + euk * vf
            den = df + db - ek + euk
            base = jax.nn.sigmoid(r.astype(jnp.float32)) * (num / jnp.maximum(den, 1e-08))
            out = base * (0.8 + 0.2 * tf)
            return out.astype(r.dtype)
        key = jax.random.key(seed)
        ks = jax.random.split(key, 6)
        return {'r': jax.random.normal(ks[0], (B, T, C), dtype=jnp.float32), 'k': jax.random.normal(ks[1], (B, T, C), dtype=jnp.float32), 'v': jax.random.normal(ks[2], (B, T, C), dtype=jnp.float32), 'w': jax.random.normal(ks[3], (C,), dtype=jnp.float32), 'u': jax.random.normal(ks[4], (C,), dtype=jnp.float32), 'time_emb': jax.random.normal(ks[5], (B, TD), dtype=jnp.float32)}
    _L1_cond2_all = _L1_cond2_setup()
    _L1_cond2_in = {k: v for k, v in _L1_cond2_all.items() if k in ('w', 'u')}
    del _L1_cond2_all

    def _L1_ffn_setup():
        import jax, jax.numpy as jnp
        import numpy as np
        D_MODEL = 256
        D_EXPERT = 1024
        EPS = 1e-08

        def ternary_quant(w):
            scale = jnp.mean(jnp.abs(w)) + EPS
            q = jnp.clip(jnp.round(w / scale), -1.0, 1.0) * scale
            return w + jax.lax.stop_gradient(q - w)
        key = jax.random.key(seed)
        k_x, k_up, k_gate, k_down = jax.random.split(key, 4)
        std_in = 1.0 / np.sqrt(D_MODEL)
        std_exp = 1.0 / np.sqrt(D_EXPERT)
        return {'x': jax.random.normal(k_x, (4, 256, D_MODEL), dtype=jnp.float32), 'W_up': jax.random.normal(k_up, (D_EXPERT, D_MODEL), dtype=jnp.float32) * std_in, 'W_gate': jax.random.normal(k_gate, (D_EXPERT, D_MODEL), dtype=jnp.float32) * std_in, 'W_down': jax.random.normal(k_down, (D_MODEL, D_EXPERT), dtype=jnp.float32) * std_exp}
    _L1_ffn_all = _L1_ffn_setup()
    _L1_ffn_in = {k: v for k, v in _L1_ffn_all.items() if k in ('W_up', 'W_gate', 'W_down')}
    del _L1_ffn_all
    return {'x': x, 'fside_BxSxS_0': fside_BxSxS_0, 'cond_512': cond_512, 'L0_cond_w': _L0_cond_in['w'], 'L0_cond_u': _L0_cond_in['u'], 'L0_attn_Wq': _L0_attn_in['Wq'], 'L0_attn_Wk': _L0_attn_in['Wk'], 'L0_attn_Wv': _L0_attn_in['Wv'], 'L0_attn_Wo': _L0_attn_in['Wo'], 'L0_cond2_w': _L0_cond2_in['w'], 'L0_cond2_u': _L0_cond2_in['u'], 'L0_ffn_w1': _L0_ffn_in['w1'], 'L0_ffn_b1': _L0_ffn_in['b1'], 'L0_ffn_gamma': _L0_ffn_in['gamma'], 'L0_ffn_beta': _L0_ffn_in['beta'], 'L0_ffn_w2': _L0_ffn_in['w2'], 'L0_ffn_b2': _L0_ffn_in['b2'], 'L1_cond_w': _L1_cond_in['w'], 'L1_cond_u': _L1_cond_in['u'], 'L1_attn_q_a_w': _L1_attn_in['q_a_w'], 'L1_attn_q_a_ln_w': _L1_attn_in['q_a_ln_w'], 'L1_attn_q_b_w': _L1_attn_in['q_b_w'], 'L1_attn_kv_a_w': _L1_attn_in['kv_a_w'], 'L1_attn_kv_a_ln_w': _L1_attn_in['kv_a_ln_w'], 'L1_attn_kv_b_w': _L1_attn_in['kv_b_w'], 'L1_attn_o_w': _L1_attn_in['o_w'], 'L1_attn_idx_wq_b_w': _L1_attn_in['idx_wq_b_w'], 'L1_attn_idx_wk_w': _L1_attn_in['idx_wk_w'], 'L1_attn_idx_kn_w': _L1_attn_in['idx_kn_w'], 'L1_attn_idx_kn_b': _L1_attn_in['idx_kn_b'], 'L1_attn_idx_wproj_w': _L1_attn_in['idx_wproj_w'], 'L1_cond2_w': _L1_cond2_in['w'], 'L1_cond2_u': _L1_cond2_in['u'], 'L1_ffn_W_up': _L1_ffn_in['W_up'], 'L1_ffn_W_gate': _L1_ffn_in['W_gate'], 'L1_ffn_W_down': _L1_ffn_in['W_down']}

def reference(x, fside_BxSxS_0, cond_512, L0_cond_w, L0_cond_u, L0_attn_Wq, L0_attn_Wk, L0_attn_Wv, L0_attn_Wo, L0_cond2_w, L0_cond2_u, L0_ffn_w1, L0_ffn_b1, L0_ffn_gamma, L0_ffn_beta, L0_ffn_w2, L0_ffn_b2, L1_cond_w, L1_cond_u, L1_attn_q_a_w, L1_attn_q_a_ln_w, L1_attn_q_b_w, L1_attn_kv_a_w, L1_attn_kv_a_ln_w, L1_attn_kv_b_w, L1_attn_o_w, L1_attn_idx_wq_b_w, L1_attn_idx_wk_w, L1_attn_idx_kn_w, L1_attn_idx_kn_b, L1_attn_idx_wproj_w, L1_cond2_w, L1_cond2_u, L1_ffn_W_up, L1_ffn_W_gate, L1_ffn_W_down):
    import jax
    import jax.numpy as jnp

    def _L0_cond_ref(r, k, v, w, u, time_emb):
        import jax, jax.numpy as jnp
        from jax import lax
        import numpy as np
        B, T, C, TD = (8, 256, 256, 64)

        def _bi_wkv(r, k, v, w, u, time_emb):
            tf = jax.nn.sigmoid(jnp.sum(time_emb, axis=-1))[:, None, None]
            decay = jnp.exp(-jnp.exp(w.astype(jnp.float32)))[None, :] * (0.5 + 0.5 * tf[:, :, 0])
            kf = k.astype(jnp.float32)
            vf = v.astype(jnp.float32)
            ek = jnp.exp(jnp.minimum(kf, 30.0))
            ekv = ek * vf

            def step(carry, x):
                a, b = carry
                ekv_t, ek_t = x
                a = a * decay + ekv_t
                b = b * decay + ek_t
                return ((a, b), (a, b))
            ekv_t = jnp.swapaxes(ekv, 0, 1)
            ek_t = jnp.swapaxes(ek, 0, 1)
            init = (jnp.zeros_like(decay), jnp.zeros_like(decay))
            _, (nf, df) = lax.scan(step, init, (ekv_t, ek_t))
            _, (nb, db) = lax.scan(step, init, (ekv_t, ek_t), reverse=True)
            nf = jnp.swapaxes(nf, 0, 1)
            df = jnp.swapaxes(df, 0, 1)
            nb = jnp.swapaxes(nb, 0, 1)
            db = jnp.swapaxes(db, 0, 1)
            euk = jnp.exp(jnp.minimum(u.astype(jnp.float32)[None, None, :] + kf, 30.0))
            num = nf + nb - ekv + euk * vf
            den = df + db - ek + euk
            base = jax.nn.sigmoid(r.astype(jnp.float32)) * (num / jnp.maximum(den, 1e-08))
            out = base * (0.8 + 0.2 * tf)
            return out.astype(r.dtype)
        return _bi_wkv(r, k, v, w, u, time_emb)

    def _L0_attn_ref(hidden_states, Wq, Wk, Wv, Wo):
        import jax, jax.numpy as jnp
        import numpy as np
        import math
        H = 16
        DN = 128
        DR = 64
        DV = 128
        ROPE_BASE = 10000.0

        def _rope_cos_sin(seq_len, dim, dtype):
            inv_freq = 1.0 / ROPE_BASE ** (jnp.arange(0, dim, 2, dtype=jnp.float32) / dim)
            t = jnp.arange(seq_len, dtype=jnp.float32)
            freqs = t[:, None] * inv_freq[None, :]
            return (jnp.cos(freqs).astype(dtype), jnp.sin(freqs).astype(dtype))

        def _apply_rope(x, cos, sin):
            half = x.shape[-1] // 2
            x1, x2 = (x[..., :half], x[..., half:])
            c = cos[None, :, None, :]
            s = sin[None, :, None, :]
            return jnp.concatenate([x1 * c - x2 * s, x1 * s + x2 * c], axis=-1)
        B, S, _ = hidden_states.shape
        q = hidden_states @ Wq.T
        k = hidden_states @ Wk.T
        v = hidden_states @ Wv.T
        q_nope = q[:, :, :H * DN].reshape(B, S, H, DN)
        q_rope = q[:, :, H * DN:].reshape(B, S, H, DR)
        k_nope = k[:, :, :H * DN].reshape(B, S, H, DN)
        k_rope = k[:, :, H * DN:].reshape(B, S, H, DR)
        v = v.reshape(B, S, H, DV)
        cos, sin = _rope_cos_sin(S, DR, hidden_states.dtype)
        q_rope = _apply_rope(q_rope, cos, sin)
        k_rope = _apply_rope(k_rope, cos, sin)
        scores = jnp.einsum('bqhd,bkhd->bhqk', q_nope, k_nope) / math.sqrt(DN) + jnp.einsum('bqhd,bkhd->bhqk', q_rope, k_rope) / math.sqrt(DR)
        attn = jax.nn.softmax(scores, axis=-1)
        out = jnp.einsum('bhqk,bkhd->bqhd', attn, v)
        out = out.reshape(B, S, H * DV)
        return out @ Wo.T

    def _L0_cond2_ref(r, k, v, w, u, time_emb):
        import jax, jax.numpy as jnp
        from jax import lax
        import numpy as np
        B, T, C, TD = (8, 256, 256, 64)

        def _bi_wkv(r, k, v, w, u, time_emb):
            tf = jax.nn.sigmoid(jnp.sum(time_emb, axis=-1))[:, None, None]
            decay = jnp.exp(-jnp.exp(w.astype(jnp.float32)))[None, :] * (0.5 + 0.5 * tf[:, :, 0])
            kf = k.astype(jnp.float32)
            vf = v.astype(jnp.float32)
            ek = jnp.exp(jnp.minimum(kf, 30.0))
            ekv = ek * vf

            def step(carry, x):
                a, b = carry
                ekv_t, ek_t = x
                a = a * decay + ekv_t
                b = b * decay + ek_t
                return ((a, b), (a, b))
            ekv_t = jnp.swapaxes(ekv, 0, 1)
            ek_t = jnp.swapaxes(ek, 0, 1)
            init = (jnp.zeros_like(decay), jnp.zeros_like(decay))
            _, (nf, df) = lax.scan(step, init, (ekv_t, ek_t))
            _, (nb, db) = lax.scan(step, init, (ekv_t, ek_t), reverse=True)
            nf = jnp.swapaxes(nf, 0, 1)
            df = jnp.swapaxes(df, 0, 1)
            nb = jnp.swapaxes(nb, 0, 1)
            db = jnp.swapaxes(db, 0, 1)
            euk = jnp.exp(jnp.minimum(u.astype(jnp.float32)[None, None, :] + kf, 30.0))
            num = nf + nb - ekv + euk * vf
            den = df + db - ek + euk
            base = jax.nn.sigmoid(r.astype(jnp.float32)) * (num / jnp.maximum(den, 1e-08))
            out = base * (0.8 + 0.2 * tf)
            return out.astype(r.dtype)
        return _bi_wkv(r, k, v, w, u, time_emb)

    def _L0_ffn_ref(x, w1, b1, gamma, beta, w2, b2):
        import jax, jax.numpy as jnp
        import numpy as np
        B, S, D, F = (4, 256, 256, 1024)
        EPS = 1e-05

        def activation_quant(x):
            scale = 127.0 / jnp.clip(jnp.max(jnp.abs(x), axis=-1, keepdims=True), EPS, None)
            return jnp.clip(jnp.round(x * scale), -128.0, 127.0) / scale

        def weight_quant(w):
            scale = 1.0 / jnp.clip(jnp.mean(jnp.abs(w)), EPS, None)
            return jnp.clip(jnp.round(w * scale), -1.0, 1.0) / scale

        def bitlinear(x, w, b):
            xq = activation_quant(x)
            wq = weight_quant(w)
            return jnp.einsum('bsd,fd->bsf', xq, wq) + b

        def layernorm(x, gamma, beta):
            mu = jnp.mean(x, axis=-1, keepdims=True)
            var = jnp.var(x, axis=-1, keepdims=True)
            return (x - mu) * jax.lax.rsqrt(var + EPS) * gamma + beta
        h = bitlinear(x, w1, b1)
        h = jax.nn.gelu(h, approximate=False)
        h = layernorm(h, gamma, beta)
        return bitlinear(h, w2, b2)

    def _L1_cond_ref(r, k, v, w, u, time_emb):
        import jax, jax.numpy as jnp
        from jax import lax
        import numpy as np
        B, T, C, TD = (8, 256, 256, 64)

        def _bi_wkv(r, k, v, w, u, time_emb):
            tf = jax.nn.sigmoid(jnp.sum(time_emb, axis=-1))[:, None, None]
            decay = jnp.exp(-jnp.exp(w.astype(jnp.float32)))[None, :] * (0.5 + 0.5 * tf[:, :, 0])
            kf = k.astype(jnp.float32)
            vf = v.astype(jnp.float32)
            ek = jnp.exp(jnp.minimum(kf, 30.0))
            ekv = ek * vf

            def step(carry, x):
                a, b = carry
                ekv_t, ek_t = x
                a = a * decay + ekv_t
                b = b * decay + ek_t
                return ((a, b), (a, b))
            ekv_t = jnp.swapaxes(ekv, 0, 1)
            ek_t = jnp.swapaxes(ek, 0, 1)
            init = (jnp.zeros_like(decay), jnp.zeros_like(decay))
            _, (nf, df) = lax.scan(step, init, (ekv_t, ek_t))
            _, (nb, db) = lax.scan(step, init, (ekv_t, ek_t), reverse=True)
            nf = jnp.swapaxes(nf, 0, 1)
            df = jnp.swapaxes(df, 0, 1)
            nb = jnp.swapaxes(nb, 0, 1)
            db = jnp.swapaxes(db, 0, 1)
            euk = jnp.exp(jnp.minimum(u.astype(jnp.float32)[None, None, :] + kf, 30.0))
            num = nf + nb - ekv + euk * vf
            den = df + db - ek + euk
            base = jax.nn.sigmoid(r.astype(jnp.float32)) * (num / jnp.maximum(den, 1e-08))
            out = base * (0.8 + 0.2 * tf)
            return out.astype(r.dtype)
        return _bi_wkv(r, k, v, w, u, time_emb)

    def _L1_attn_ref(hidden_states, q_a_w, q_a_ln_w, q_b_w, kv_a_w, kv_a_ln_w, kv_b_w, o_w, idx_wq_b_w, idx_wk_w, idx_kn_w, idx_kn_b, idx_wproj_w):
        import jax, jax.numpy as jnp
        import numpy as np
        B, S, HID = (1, 256, 256)
        H, NOPE, ROPE, VDIM = (16, 128, 64, 128)
        QR, KVR = (192, 64)
        IH, ID = (16, 128)
        TOPK = 64
        THETA = 10000.0
        EPS = 1e-06
        SCALE = (NOPE + ROPE) ** (-0.5)
        NEG = -1000000000.0

        def _cos_sin(s, dim, dtype):
            inv = 1.0 / THETA ** (np.arange(0, dim, 2, dtype=np.float32) / dim)
            t = np.arange(s, dtype=np.float32)
            f = np.outer(t, inv)
            emb = np.concatenate([f, f], -1)
            return (jnp.asarray(np.cos(emb), dtype), jnp.asarray(np.sin(emb), dtype))

        def _rope(x, cos, sin):
            x1, x2 = jnp.split(x, 2, axis=-1)
            rot = jnp.concatenate([-x2, x1], axis=-1)
            return x * cos[None, :, None, :] + rot * sin[None, :, None, :]

        def _rmsnorm(x, w):
            v = jnp.mean(x.astype(jnp.float32) ** 2, -1, keepdims=True)
            return (x.astype(jnp.float32) * jax.lax.rsqrt(v + EPS)).astype(x.dtype) * w

        def _layernorm(x, w, b):
            m = jnp.mean(x, -1, keepdims=True)
            v = jnp.var(x, -1, keepdims=True)
            return (x - m) * jax.lax.rsqrt(v + EPS) * w + b
        b, s, _ = hidden_states.shape
        cos, sin = _cos_sin(s, ROPE, hidden_states.dtype)
        qr = _rmsnorm(hidden_states @ q_a_w.T, q_a_ln_w)
        q = (qr @ q_b_w.T).reshape(b, s, H, NOPE + ROPE)
        q_nope, q_pe = (q[..., :NOPE], q[..., NOPE:])
        q_pe = _rope(q_pe, cos, sin)
        ckv = hidden_states @ kv_a_w.T
        c_kv, k_pe = (ckv[..., :KVR], ckv[..., KVR:])
        k_pe = _rope(k_pe[:, :, None, :], cos, sin)
        kv = (_rmsnorm(c_kv, kv_a_ln_w) @ kv_b_w.T).reshape(b, s, H, NOPE + VDIM)
        k_nope, v = (kv[..., :NOPE], kv[..., NOPE:])
        iq = (qr @ idx_wq_b_w.T).reshape(b, s, IH, ID)
        iq = jnp.concatenate([_rope(iq[..., :ROPE], cos, sin), iq[..., ROPE:]], -1)
        ik = _layernorm(hidden_states @ idx_wk_w.T, idx_kn_w, idx_kn_b)
        ik_pe = _rope(ik[:, :, None, :ROPE], cos, sin)[:, :, 0, :]
        ik = jnp.concatenate([ik_pe, ik[..., ROPE:]], -1)
        iw = hidden_states @ idx_wproj_w.T * IH ** (-0.5)
        idx_scores = jnp.einsum('bqh,bhqk->bqk', iw, jax.nn.relu(jnp.einsum('bqhd,bkd->bhqk', iq, ik)))
        causal = jnp.tril(jnp.ones((s, s), bool))
        idx_scores = jnp.where(causal[None], idx_scores, -jnp.inf)
        _, top_idx = jax.lax.top_k(idx_scores, TOPK)
        bi = jnp.arange(b)[:, None, None]
        qi = jnp.arange(s)[None, :, None]
        keep = jnp.zeros((b, s, s), bool).at[bi, qi, top_idx].set(True)
        allowed = keep & causal[None]
        qh = jnp.concatenate([q_nope, q_pe], -1)
        kh = jnp.concatenate([k_nope, jnp.broadcast_to(k_pe, (b, s, H, ROPE))], -1)
        scores = jnp.einsum('bqhd,bkhd->bhqk', qh, kh) * SCALE
        scores = jnp.where(allowed[:, None], scores, NEG)
        attn = jax.nn.softmax(scores, -1)
        out = jnp.einsum('bhqk,bkhd->bqhd', attn, v).reshape(b, s, H * VDIM)
        return out @ o_w.T

    def _L1_cond2_ref(r, k, v, w, u, time_emb):
        import jax, jax.numpy as jnp
        from jax import lax
        import numpy as np
        B, T, C, TD = (8, 256, 256, 64)

        def _bi_wkv(r, k, v, w, u, time_emb):
            tf = jax.nn.sigmoid(jnp.sum(time_emb, axis=-1))[:, None, None]
            decay = jnp.exp(-jnp.exp(w.astype(jnp.float32)))[None, :] * (0.5 + 0.5 * tf[:, :, 0])
            kf = k.astype(jnp.float32)
            vf = v.astype(jnp.float32)
            ek = jnp.exp(jnp.minimum(kf, 30.0))
            ekv = ek * vf

            def step(carry, x):
                a, b = carry
                ekv_t, ek_t = x
                a = a * decay + ekv_t
                b = b * decay + ek_t
                return ((a, b), (a, b))
            ekv_t = jnp.swapaxes(ekv, 0, 1)
            ek_t = jnp.swapaxes(ek, 0, 1)
            init = (jnp.zeros_like(decay), jnp.zeros_like(decay))
            _, (nf, df) = lax.scan(step, init, (ekv_t, ek_t))
            _, (nb, db) = lax.scan(step, init, (ekv_t, ek_t), reverse=True)
            nf = jnp.swapaxes(nf, 0, 1)
            df = jnp.swapaxes(df, 0, 1)
            nb = jnp.swapaxes(nb, 0, 1)
            db = jnp.swapaxes(db, 0, 1)
            euk = jnp.exp(jnp.minimum(u.astype(jnp.float32)[None, None, :] + kf, 30.0))
            num = nf + nb - ekv + euk * vf
            den = df + db - ek + euk
            base = jax.nn.sigmoid(r.astype(jnp.float32)) * (num / jnp.maximum(den, 1e-08))
            out = base * (0.8 + 0.2 * tf)
            return out.astype(r.dtype)
        return _bi_wkv(r, k, v, w, u, time_emb)

    def _L1_ffn_ref(x, W_up, W_gate, W_down):
        import jax, jax.numpy as jnp
        import numpy as np
        D_MODEL = 256
        D_EXPERT = 1024
        EPS = 1e-08

        def ternary_quant(w):
            scale = jnp.mean(jnp.abs(w)) + EPS
            q = jnp.clip(jnp.round(w / scale), -1.0, 1.0) * scale
            return w + jax.lax.stop_gradient(q - w)
        wu = ternary_quant(W_up)
        wg = ternary_quant(W_gate)
        wd = ternary_quant(W_down)
        up = jnp.einsum('bsd,ed->bse', x, wu)
        gate = jnp.einsum('bsd,ed->bse', x, wg)
        hidden = jax.nn.silu(up) * gate
        return jnp.einsum('bse,de->bsd', hidden, wd)
    x = x + _L0_attn_ref(_L0_cond_ref(x, fside_BxSxS_0, fside_BxSxS_0, L0_cond_w, L0_cond_u, cond_512), L0_attn_Wq, L0_attn_Wk, L0_attn_Wv, L0_attn_Wo)
    x = x + _L0_ffn_ref(_L0_cond2_ref(x, fside_BxSxS_0, fside_BxSxS_0, L0_cond2_w, L0_cond2_u, cond_512), L0_ffn_w1, L0_ffn_b1, L0_ffn_gamma, L0_ffn_beta, L0_ffn_w2, L0_ffn_b2)
    x = x + _L1_attn_ref(_L1_cond_ref(x, fside_BxSxS_0, fside_BxSxS_0, L1_cond_w, L1_cond_u, cond_512), L1_attn_q_a_w, L1_attn_q_a_ln_w, L1_attn_q_b_w, L1_attn_kv_a_w, L1_attn_kv_a_ln_w, L1_attn_kv_b_w, L1_attn_o_w, L1_attn_idx_wq_b_w, L1_attn_idx_wk_w, L1_attn_idx_kn_w, L1_attn_idx_kn_b, L1_attn_idx_wproj_w)
    x = x + _L1_ffn_ref(_L1_cond2_ref(x, fside_BxSxS_0, fside_BxSxS_0, L1_cond2_w, L1_cond2_u, cond_512), L1_ffn_W_up, L1_ffn_W_gate, L1_ffn_W_down)
    return x

_drawn_inputs = setup_inputs


def setup_inputs(seed=0):
    import zlib

    import numpy as np

    out = dict(_drawn_inputs(seed))
    spreads = {'L0_ffn_gamma': (1.0, 0.2),
     'L0_ffn_beta': (0.0, 0.1),
     'L1_attn_q_a_ln_w': (1.0, 0.6),
     'L1_attn_kv_a_ln_w': (1.0, 0.6),
     'L1_attn_idx_kn_w': (1.0, 0.6),
     'L1_attn_idx_kn_b': (0.0, 2.0)}
    factors = {'L0_cond_u': 5.224,
     'L0_attn_Wq': 8.0,
     'L0_attn_Wk': 8.0,
     'L0_ffn_b1': 2.778,
     'L0_ffn_b2': 7.12,
     'L1_cond_u': 5.887,
     'L1_attn_q_a_w': 6.191,
     'L1_attn_q_b_w': 21.935,
     'L1_attn_idx_wq_b_w': 22.215,
     'L1_attn_idx_wk_w': 22.78,
     'L1_attn_idx_wproj_w': 22.884,
     'L1_cond2_w': 3.359,
     'L1_cond2_u': 22.031}
    for name, (base, spread) in spreads.items():
        noise = np.random.default_rng([zlib.crc32(name.encode()), seed]).standard_normal(out[name].shape)
        drawn = base * np.exp(spread * noise) if base else spread * noise
        out[name] = jnp.asarray(drawn.astype(out[name].dtype))
    for name, factor in factors.items():
        out[name] = (out[name] * factor).astype(out[name].dtype)
    return out
```

```python
from contextlib import ExitStack

import numpy as np

import concourse.bass as bass
from concourse import mybir

F32 = mybir.dt.float32
F32R = mybir.dt.float32r
BF16 = mybir.dt.bfloat16
ACT = mybir.ActivationFunctionType
ALU = mybir.AluOpType
AX = mybir.AxisListType

P = 128
B, T, C = 4, 256, 256
N = B * T
NT = N // P
KC = C // P
H = 16
PAIRS = H // 2
DN, DR = 128, 64
F = 1024
NF = F // P
QR, KVR = 192, 64
TOPK = 64
HALF = N // 2
MAGIC = 12582912.0
SWAP = [p ^ 16 for p in range(32)]


class Chain:

    def __init__(self, eng, sem):
        self.eng, self.sem, self.n, self.reg, self.k = eng, sem, 0, None, 0

    def did(self, ins):
        ins.then_inc(self.sem, 1)
        self.n += 1
        return ins

    def wait(self):
        self.eng.wait_ge(self.sem, self.n if self.reg is None else self.reg * self.k + self.n)

    def step(self, ins):
        self.did(ins)
        self.wait()

    def loop(self, reg, start, k):
        self.at, self.reg, self.k, self.start = self.n, reg, k, start
        self.n -= start * k

    def close(self, rounds):
        took = self.n + self.start * self.k - self.at
        assert took == self.k, f"the body takes {took} steps"
        self.n, self.reg = self.at + rounds * self.k, None


def pick(t, at, cols):
    if isinstance(at, int):
        return t[:, at, cols]
    return t[:, bass.ds(at, 1), cols].rearrange("p a n -> p (a n)")


def adaln_block(nc, a, out):
    ctx = ExitStack()

    def sem(name):
        return ctx.enter_context(nc.semaphore(name))

    total = nc.sbuf_usable_end
    base0 = (nc.sbuf_base + 63) // 64 * 64

    class Arena:

        def __init__(self, at):
            self.at = at

        def __call__(self, name, shape, dt=F32):
            size = int(np.prod(shape[1:])) * (2 if dt == BF16 else 4)
            t = nc.alloc_sbuf_tensor_at(name, shape, dt, offset=self.at)
            self.at += (size + 63) // 64 * 64
            assert self.at <= total, (name, self.at, total)
            return t

    with ctx:
        keep = Arena(base0)
        gtok = keep("gtok", [P, 3 * KC, NT, P])
        xtok = keep("xtok", [P, NT, C])
        yhi = keep("yhi", [P, KC, N], F32R)
        ylo = keep("ylo", [P, KC, N], F32R)
        ident = keep("ident", [P, P])
        identb = keep("identb", [P, P], BF16)
        ones = keep("ones", [P, P])
        par = keep("par", [P, 2, 4 * KC])
        decay = keep("decay", [P, 4 * KC, B])
        condb = keep("condb", [P, B, 64])
        tf = keep("tf", [P, B])
        dfac = keep("dfac", [P, B])
        gate = keep("gate", [P, B])
        ew = keep("ew", [P, 4 * KC])
        w1q = keep("w1q", [P, KC, F], BF16)
        w2q = keep("w2q", [P, NF, C], BF16)
        wsum = keep("wsum", [P, 8])
        wmean = keep("wmean", [P, 8])
        wrec = keep("wrec", [P, 8])
        half = keep("half", [P, 4])
        clipc = keep("clipc", [P, 2])

        m = Arena(keep.at)
        tabc = m("tabc", [P, HALF])
        tabs = m("tabs", [P, HALF])
        kt = m("kt", [P, KC, N])
        ek = m("ek", [P, KC, N])
        ekv = m("ekv", [P, KC, N])
        gbuf = [m(n, [P, HALF]) for n in ("nf", "nb", "df", "db", "euk", "dd")]
        nb, db = gbuf[1], gbuf[3]
        gg = m("gg", [P, HALF])
        wst, whi, wlo = ([m(f"{n}{x}", [P, KC, 384], F32 if n == "wst" else F32R) for x in range(2)]
                         for n in ("wst", "whi", "wlo"))
        wvst = m("wvst", [P, KC, 256])
        wvhi = m("wvhi", [P, KC, 256], F32R)
        wvlo = m("wvlo", [P, KC, 256], F32R)
        wo = m("wo", [P, H, C])
        at = m.at
        qn, kn, qr, kr = ([m(f"{n}{x}", [P, N]) for x in range(2)] for n in ("qn", "kn", "qr", "kr"))
        v = m("v", [P, NT, 256])
        pr = [m(f"pr{x}", [P, 2, T]) for x in range(2)]
        pt = [m(f"pt{x}", [P, 2, T]) for x in range(2)]
        rt1 = [m(f"rt{x}", [P, HALF]) for x in range(2)]
        rsh = [m(f"rsh{x}", [P, HALF]) for x in range(2)]
        ot = m("ot", [P, 2, N])
        negm = [m(f"negm{x}", [P, 2]) for x in range(2)]
        sums = [m(f"sums{x}", [P, 2]) for x in range(2)]
        rsum = [m(f"rsum{x}", [P, 2]) for x in range(2)]
        pre = Arena(at)
        xt = pre("xt", [P, KC, N])
        g0 = pre("g0", [P, KC, N])
        y32 = pre("y32", [P, KC, N])
        gbuf2 = [pre(n + "2", [P, HALF]) for n in ("nf", "nb", "df", "db", "euk", "dd")]
        assert pre.at <= total

        def gate_buffers(gu, prologue=False):
            return gbuf2 if prologue and gu % 2 else gbuf

        R0 = keep.at
        e = Arena(R0 + 4096)
        wtern = [e(f"wtern{x}", [P, 2048]) for x in range(2)]
        wround = e("wround", [P, 2048])
        b1b, gamb, betb = (e(n, [P, F]) for n in ("b1b", "gamb", "betb"))
        b2b = e("b2b", [P, C])
        assert e.at <= R0 + 42 * 1024
        k2 = Arena(R0 + 42 * 1024)
        kct = k2("kct", [P, N])
        ikt = k2("ikt", [P, N])
        vl = k2("vl", [P, NT, KVR])
        iw = k2("iw", [P, NT, H])
        wabs = k2("wabs", [P, 2, H * KVR])
        wvo = k2("wvo", [P, PAIRS, C])
        at2 = k2.at
        hw = Arena(at2)("hw", [P, H, 576])
        q2 = Arena(at2)
        qrhi = q2("qrhi", [P, 2, N], F32R)
        qrlo = q2("qrlo", [P, 2, N], F32R)
        e = Arena(hw_end := at2 + H * 576 * 4)
        sga = e("sga", [P, NT, C])
        y = [e(f"y{x}", [P, C]) for x in range(2)]
        yq = [e(f"yq{x}", [P, C], BF16) for x in range(2)]
        yqt = [e(f"yqt{x}", [P, KC, P], BF16) for x in range(2)]
        hb = [e(f"hb{x}", [P, F]) for x in range(2)]
        hq = [e(f"hq{x}", [P, F], BF16) for x in range(2)]
        hqt = [e(f"hqt{x}", [P, NF, P], BF16) for x in range(2)]
        xb = [e(f"xb{x}", [P, C]) for x in range(2)]
        sm = [e(f"sm{x}", [P, 64]) for x in range(4)]
        e = Arena(hw_end)
        wfst = Arena(R0)("wfst", [P, KC, 464])
        f_ = Arena(R0 + 4096)
        wfhi = f_("wfhi", [P, KC, 464], F32R)
        wflo = f_("wflo", [P, KC, 464], F32R)
        ropec, ropes = (f_(n, [P, 2, DR]) for n in ("ropec", "ropes"))
        ikw, ikb = (f_(n, [P, P]) for n in ("ikw", "ikb"))
        kvw = f_("kvw", [P, KVR])
        lnw = f_("lnw", [P, 2])
        fy = [f_(f"fy{x}", [P, C]) for x in range(2)]
        fsg = [f_(f"fsg{x}", [P, C]) for x in range(2)]
        fyhi = [f_(f"fyhi{x}", [P, KC, P], F32R) for x in range(2)]
        fylo = [f_(f"fylo{x}", [P, KC, P], F32R) for x in range(2)]
        junk = f_("junk", [P, 256])
        fp = [f_(f"fp{x}", [P, 464]) for x in range(2)]
        ki = [f_(f"ki{x}", [P, 256]) for x in range(2)]
        qrs = [f_(f"qrs{x}", [P, QR]) for x in range(2)]
        rp = f_("rp", [P, 4, DR])
        fs = [f_(f"fs{x}", [P, 32]) for x in range(2)]
        assert f_.at <= R0 + 32 * 1024, f_.at - R0

        i1 = Arena(R0 + 32 * 1024)
        tabc1, tabs1 = (i1(n, [P, HALF]) for n in ("tabc1", "tabs1"))
        wi = [i1(f"wi{x}", [P, 2, P]) for x in range(2)]
        wihi = [i1(f"wihi{x}", [P, 2, P], F32R) for x in range(2)]
        wilo = [i1(f"wilo{x}", [P, 2, P], F32R) for x in range(2)]
        assert i1.at <= R0 + 42 * 1024, i1.at - R0
        i1 = Arena(R0)
        tabc2, tabs2 = (i1(n, [P, HALF]) for n in ("tabc2", "tabs2"))
        it1 = [i1(f"it{x}", [P, HALF]) for x in range(2)]
        ish = [i1(f"ish{x}", [P, HALF]) for x in range(2)]
        acc = i1("acc", [P, NT, T])
        ust = i1("ust", [P, 2048])
        assert i1.at <= R0 + 32 * 1024, i1.at - R0
        i2 = Arena(q2.at)
        iq = [i2(f"iq{x}", [P, N]) for x in range(2)]
        rl = [i2(f"rl{x}", [P, 384]) for x in range(4)]
        top8 = i2("top8", [P, NT, 8])
        biasb = i2("biasb", [P, NT, T], BF16)
        causb = i2("causb", [P, 2, T], BF16)
        p1 = [i2(f"p1{x}", [P, 384]) for x in range(2)]
        pt1 = [i2(f"pt1{x}", [P, 384]) for x in range(2)]
        ot1 = i2("ot1", [P, N])
        negm1 = [i2(f"negm1{x}", [P, 2]) for x in range(2)]
        sums1 = [i2(f"sums1{x}", [P, 2]) for x in range(2)]
        rsum1 = [i2(f"rsum1{x}", [P, 2]) for x in range(2)]
        wt = [i2(f"wt{k}", [P, 2048], F32R) for k in range(3)]
        uround = i2("uround", [P, 2048])

        j1 = Arena(R0)
        jsg = j1("jsg", [P, NT, C])
        jy = j1("jy", [P, NT, C])
        silu = [j1(f"silu{x}", [P, HALF]) for x in range(2)]
        h32 = [j1(f"h32{x}", [P, HALF]) for x in range(2)]
        xo = [j1(f"xo{x}", [P, C]) for x in range(2)]
        j2 = Arena(R0 + 48 * 1024)
        hhi = j2("hhi", [P, NF, HALF], F32R)
        hlo = j2("hlo", [P, NF, HALF], F32R)
        assert j2.at <= i2.at - 4 * 8192 and j1.at <= R0 + 48 * 1024

        ps = [ctx.enter_context(nc.psum_tensor(f"ps{i}", [P, 512], F32)) for i in range(8)]
        chunk_bank, score_bank, turn_bank, pv_bank = ps[0:2], ps[2:4], ps[4], ps[5:7]

        iscore = ps[2:6]
        out_bank = ps[7]
        up_bank, gate_bank, down_bank = ps[0:2], ps[2:4], ps[4:6]
        qturn = [ps[x][:, 0:C // 2].bitcast(BF16) for x in range(2)]
        turn2 = ps[2][:, :].bitcast(BF16)
        ffn1 = [[ps[3], ps[4]], [ps[5], ps[6]]]
        ffn2 = [ps[7], ps[7]]
        fturn, fproj, fout = ps[0:2], ps[2:4], ps[4:6]

        in_k, in_x, in_par, in_tab, in_wo = (sem("in_" + n) for n in ("k", "x", "par", "tab", "wo"))
        in_w = [sem(f"in_w{x}") for x in range(2)]
        in_wv = sem("in_wv")
        dch, ach = sem("vector_steps"), sem("scalar_steps")
        pch = sem("pool_steps")
        s_kmin, s_ukmin = sem("min_k_ready"), sem("min_uk_ready")
        s_const, s_ek, s_decay, s_tf = (sem(n) for n in ("constants_ready", "ek_ready", "decay_ready", "tf_steps"))
        s_euk, s_scan, s_dd, s_sums, s_gg, s_gused = (sem(n) for n in (
            "euk_ready", "scans_ready", "dd_ready", "gate_sums_ready", "gg_ready", "gg_used"))
        s_sig, s_y, s_yhi, s_ylo = (sem(n) for n in ("sig_x_ready", "y_ready", "yhi_ready", "ylo_ready"))
        s_whi, s_wlo, s_wused = sem("w_upper_ready"), sem("w_lower_ready"), sem("w_used")
        s_wvhi, s_wvlo, s_wvused = sem("wv_upper_ready"), sem("wv_lower_ready"), sem("wv_used")
        s_chunk, s_free = sem("chunk_ready"), [sem(f"chunk_bank{x}_free") for x in range(2)]
        s_qk, s_rope, s_v = sem("qk_ready"), sem("rope_ready"), sem("v_ready")
        s_shuf, s_t2 = sem("rope_swapped"), sem("rope_sin_ready")
        s_scores, s_negmax, s_exp, s_norm = (sem(n) for n in ("scores_ready", "negmax_ready", "exp_ready", "probs_ready"))
        s_turn, s_pt, s_pv, s_o = (sem(n) for n in ("probs_turned", "pt_ready", "pv_ready", "o_ready"))
        s_x1 = sem("x1_added")
        s_gtok = sem("gtok_ready")
        s_rev = sem("backward_sources_copied")
        s_out = sem("stored")
        s_pause = sem("pause")
        phase = sem("phase_done")
        in_e, in_hw, in_f, in_i, in_i2 = (sem("in_" + n) for n in ("e", "hw", "f", "i", "i2"))
        in_t0 = [sem(f"in_tern{k}") for k in range(2)]
        s_abs, s_tot, s_wscale, s_round, s_tern = (sem(n) for n in (
            "weight_abs", "weight_total", "weight_scale", "weight_rounded", "weight_ternary"))
        e_sig, e_scale, e_qm, e_q, e_qt, e_qtc, e_h, e_hb, e_gelu, e_ve, e_rstd, e_nm, e_z, e_beta = (sem("e_" + n) for n in (
            "sig", "scale", "scaled", "quant", "turned", "turned_copied", "h", "h_biased", "gelu", "variance", "rstd",
            "mean_rstd", "normed", "affine"))
        e_scale2, e_qm2, e_q2, e_qt2, e_qtc2, e_y2, e_xb, e_x2 = (sem("e2_" + n) for n in (
            "scale", "scaled", "quant", "turned", "turned_copied", "y", "xb", "x2"))
        s_hw, s_hwc = sem("latent_products"), sem("latent_products_copied")
        f_w, f_wlo, f_sig, f_y, f_yt, f_hi, f_lo, f_p, f_sq, f_bn, f_rstd, f_qrs, f_ki, f_vl, f_t, f_hi2, f_pc, f_free = (sem("f_" + n) for n in (
            "w_upper", "w_lower", "sig", "y", "y_turned", "y_upper", "y_lower", "projected", "squares", "variance", "rstd",
            "qr_scaled", "keys", "latents", "turned", "qr_upper", "projected_copied", "act_copies"))

        in_q = [sem(f"in_q{x}") for x in range(2)]
        q_abs, q_whi, q_wlo, q_wused, q_chunk, q_front, q_ready, q_scores = (sem("q_" + n) for n in (
            "absorbed_staged", "w_upper", "w_lower", "w_used", "projected", "rope_front", "ready", "scores"))
        i_init, i_relu, i_acc, a_bias = sem("i_acc_initial"), sem("i_relu"), sem("i_accumulated"), sem("a_bias_ready")
        a_negmax, a_exp, a_norm, a_turn, a_pt, a_pv, a_o, a_out, a_x = (sem("a_" + n) for n in (
            "negmax", "exp", "probs", "turned", "pt", "pv", "o", "out", "x3"))
        in_u = sem("in_u")
        j_clip = sem("j_clipped")
        j_abs, j_tot, j_scale, j_round, j_tern = (sem("j_" + n) for n in ("abs", "total", "scale", "rounded", "ternary"))
        j_sig, j_y, j_yt, j_hi, j_lo, j_proj, j_silu, j_h, j_hhi, j_hlo, j_down, j_x = (sem("j_" + n) for n in (
            "sig", "y", "y_turned", "y_upper", "y_lower", "projected", "silu", "h", "h_upper", "h_lower", "down", "x"))
        j_out = [sem(f"j_stored{x}") for x in range(2)]

        block = ctx.enter_context(nc.Block())

        def barrier(eng, k):
            eng.drain().then_inc(phase, 1)
            eng.wait_ge(phase, 5 * k)

        def skewed(eng, body, chain=None, k=0):
            for t in range(4):
                body(t, t % 2, lambda d, t=t: 0 <= t - d < NT)
            with eng.Fori(2, 4) as i:
                if chain:
                    chain.loop(i, 2, k)
                for x in range(2):
                    body(i * 2 + x, x, lambda d: True)
                if chain:
                    chain.close(2)
            for t in range(NT, NT + 3):
                body(t, t % 2, lambda d, t=t: 0 <= t - d < NT)

        def chunks(g, last):
            qk = [[("r", 0), ("r", 1)], [("q", 0), ("k", 0)], [("q", 1), ("k", 1)], []]
            gc = [("g", 0)] if g else []
            first = [list(x) for x in qk]
            first[3] += gc
            second = [list(x) if not last else [] for x in qk]
            second[3] += gc
            for s in range(1, 4):
                second[s].append(("o", s - 1))
            tail = [[] if last else [("v", s)] for s in range(4)]
            tail[3].append(("o", 3))
            return [(first, [[]] * 4), (second, tail)]

        def numbered(g, last):
            n, places = 0, {}
            for h, (front, tail) in enumerate(chunks(g, last)):
                for s in range(4):
                    for kind, w in front[s] + tail[s]:
                        places[h, kind, w] = n
                        n += 1
            return places, n

        PG, NG = numbered(True, False)
        P6, N6 = numbered(False, False)
        P7, N7 = numbered(False, True)
        FIRST = 10
        NGATED = 6
        assert NG % 2 == 0 and N6 % 2 == 0 and FIRST % 2 == 0

        def chunk_at(i, h, kind, w):
            if not isinstance(i, int):
                return i * NG + (FIRST + PG[h, kind, w])
            if i < NGATED:
                return FIRST + i * NG + PG[h, kind, w]
            return FIRST + NGATED * NG + ((P6[h, kind, w]) if i == 6 else N6 + P7[h, kind, w])

        def bank_at(i, h, kind, w):
            return (PG if not isinstance(i, int) or i < NGATED else P6 if i == 6 else P7)[h, kind, w] % 2

        def uses_at(i, h, kind, w):
            if not isinstance(i, int):
                return i * (NG // 2) + (FIRST + PG[h, kind, w]) // 2
            return chunk_at(i, h, kind, w) // 2

        def pairs(eng, body, chain=None, k=0):
            with eng.Fori(0, NGATED) as i:
                if chain:
                    chain.loop(i, 0, k)
                body(i, True, False)
                if chain:
                    chain.close(NGATED)
            body(6, False, False)
            body(7, False, True)

        @block.sync
        def _(sp):
            sp.dma_start(par[:, :, :], a["par"]).then_inc(in_par, 16)
            sp.dma_start(condb[:, :, :], a["cond"]).then_inc(in_par, 16)
            sp.dma_start(kt[:, :, :], a["kt"]).then_inc(in_k, 16)
            sp.dma_start(xt[:, :, :], a["xt"]).then_inc(in_x, 16)
            for x in range(2):
                sp.dma_start(wst[x][:, :, :], a["wqk0"][x]).then_inc(in_w[x], 16)
            sp.dma_start(wvst[:, :, :], a["wv0"][0]).then_inc(in_wv, 16)
            sp.dma_start(tabc[:, :], a["tabc0"]).then_inc(in_tab, 16)
            sp.dma_start(tabs[:, :], a["tabs0"]).then_inc(in_tab, 16)
            sp.dma_start(wo[:, :, :], a["wo0"]).then_inc(in_wo, 16)
            sp.dma_start(xtok[:, :, :], a["xtok"]).then_inc(in_wo, 16)
            with sp.Fori(0, PAIRS - 1) as i:
                sp.wait_ge(s_whi, i * 2 + 1)
                sp.wait_ge(s_wlo, i * 2 + 1)
                sp.dma_start(wst[0][:, :, :], a["wqk0"][bass.ds(i * 2 + 2, 1), :, :, :].rearrange("a p k n -> (a p) k n")).then_inc(in_w[0], 16)
                sp.wait_ge(s_wvhi, i + 1)
                sp.wait_ge(s_wvlo, i + 1)
                sp.dma_start(wvst[:, :, :], a["wv0"][bass.ds(i + 1, 1), :, :, :].rearrange("a p k n -> (a p) k n")).then_inc(in_wv, 16)
                sp.wait_ge(s_whi, i * 2 + 2)
                sp.wait_ge(s_wlo, i * 2 + 2)
                sp.dma_start(wst[1][:, :, :], a["wqk0"][bass.ds(i * 2 + 3, 1), :, :, :].rearrange("a p k n -> (a p) k n")).then_inc(in_w[1], 16)
            sp.wait_ge(s_gused, 2 * NGATED + 1)
            sp.wait_ge(s_rev, 2 * NGATED + 1)
            for k in range(2):
                sp.dma_start(wtern[k][:, :], a["w12"][k]).then_inc(in_t0[k], 16)
            for t, n in ((b1b, "b1"), (gamb, "gamma"), (betb, "beta"), (b2b, "b2")):
                sp.dma_start(t[:, :], a[n]).then_inc(in_e, 16)
            barrier(sp, 1)
            sp.dma_start(wfst[:, :, :], a["wf"]).then_inc(in_f, 16)
            for t, n in ((ropec, "ropec"), (ropes, "ropes")):
                sp.dma_start(t[:, :, :], a[n]).then_inc(in_f, 16)
            for t, n in ((ikw, "ikw"), (ikb, "ikb"), (kvw, "kvw"), (lnw, "lnw")):
                sp.dma_start(t[:, :], a[n]).then_inc(in_f, 16)
            sp.dma_start(hw[:, :, :], a["hw"]).then_inc(in_hw, 16)
            barrier(sp, 2)
            for t, n in ((tabc1, "tabc1"), (tabs1, "tabs1")):
                sp.dma_start(t[:, :], a[n]).then_inc(in_i, 16)
            for x in range(2):
                sp.dma_start(wi[x][:, :, :], a["wi"][x]).then_inc(in_q[x], 16)
            barrier(sp, 3)
            for t, n in ((tabc2, "tabc2"), (tabs2, "tabs2")):
                sp.dma_start(t[:, :], a[n]).then_inc(in_i2, 16)
            sp.dma_start(ust[:, :], a["w3"][0]).then_inc(in_u, 16)
            with sp.Fori(0, PAIRS - 1) as i:
                for x in range(2):
                    sp.wait_ge(q_wlo, i * 2 + (x + 1))
                    sp.dma_start(wi[x][:, :, :], a["wi"][bass.ds(i * 2 + (2 + x), 1), :, :, :].rearrange("a p k n -> (a p) k n")).then_inc(in_q[x], 16)
            def attention_weights(i):
                for x in range(2):
                    sp.wait_ge(q_wlo, i * 2 + (H - 1 + x))
                    src = a["wq1"][i * 2 + x] if isinstance(i, int) else a["wq1"][bass.ds(i * 2 + x, 1), :, :, :].rearrange("a p k n -> (a p) k n")
                    sp.dma_start(wi[x][:, :, KVR:P], src).then_inc(in_q[x], 16)

            attention_weights(0)
            for k in range(1, 3):
                sp.wait_ge(j_round, k)
                sp.dma_start(ust[:, :], a["w3"][k]).then_inc(in_u, 16)
            with sp.Fori(1, PAIRS) as i:
                attention_weights(i)
            barrier(sp, 4)
            for x in range(2):
                sp.sem_inc(j_out[x], 16)
            with sp.Fori(0, 2) as n:
                for j in range(4):
                    sp.wait_ge(j_x, n * 4 + (j + 1))
                    sp.dma_start(out[:, bass.ds(n * 4 + j, 1), :].rearrange("p a c -> p (a c)"), xo[j % 2][:, :]).then_inc(j_out[j % 2], 16)
            for x in range(2):
                sp.wait_ge(j_out[x], 16 + 16 * NT // 2)

        @block.gpsimd
        def _(gp):
            ch = Chain(gp, pch)
            for t, val in ((ident, 0.0), (identb, 0.0), (ones, 1.0), (half, -0.5)):
                ch.did(gp.memset(t[:, :], val))
            ch.did(gp.memset(clipc[:, 0:1], 1.0 - MAGIC))
            ch.did(gp.memset(clipc[:, 1:2], 2.0))
            ch.wait()
            for t in (ident, identb):
                gp.affine_select(out=t[:, :], in_=t[:, :], compare_op=ALU.not_equal, fill=1.0, base=0,
                                 pattern=[[-1, P]], channel_multiplier=1).then_inc(s_const, 1)

            def gate_sums(gu, kcols, prologue=False):
                nf, nb, df, db, euk, dd = gate_buffers(gu, prologue)
                gp.wait_ge(s_scan, gu + 1)
                ch.did(gp.tensor_tensor(nf[:, :], nf[:, :], nb[:, :], ALU.add))
                ch.did(gp.tensor_tensor(df[:, :], df[:, :], db[:, :], ALU.add))
                gp.wait_ge(s_dd, gu + 1)
                ch.wait()
                ch.step(gp.tensor_tensor(nb[:, :], dd[:, :], kcols, ALU.mult))
                ch.did(gp.tensor_tensor(nf[:, :], nf[:, :], nb[:, :], ALU.add))
                gp.tensor_tensor(df[:, :], df[:, :], dd[:, :], ALU.add).then_inc(s_sums, 1)

            def split_w(x, hd):
                gp.wait_ge(s_whi, hd + 1)
                gp.tensor_tensor(wlo[x][:, :, :], wst[x][:, :, :], whi[x][:, :, :].bitcast(F32), ALU.subtract).then_inc(s_wlo, 1)

            def split_wv(i):
                gp.wait_ge(s_wvhi, i + 1)
                gp.tensor_tensor(wvlo[:, :, :], wvst[:, :, :], wvhi[:, :, :].bitcast(F32), ALU.subtract).then_inc(s_wvlo, 1)

            def rope_sin(rn):
                for w in range(2):
                    gp.wait_ge(s_shuf, rn + w + 1)
                    gp.tensor_tensor(rsh[w][:, :], rsh[w][:, :], tabs[:, :], ALU.mult).then_inc(s_t2, 1)

            gp.wait_ge(in_k, 16)
            for c in range(KC):
                for bh in range(2):
                    gate_sums(2 * c + bh, kt[:, c, bh * HALF:(bh + 1) * HALF], True)
            split_w(0, 0)
            split_wv(0)
            split_w(1, 1)
            gp.wait_ge(in_tab, 32)
            rope_sin(0)

            def body(i, g, last):
                rope_sin(i * 4 + 2)
                if g:
                    gate_sums(i * 2 + 4, pick(kt, i % 2, slice(0, HALF)))
                if not last:
                    split_w(0, i * 2 + 2)
                    split_wv(i + 1)
                    rope_sin(i * 4 + 4)
                if g:
                    gate_sums(i * 2 + 5, pick(kt, i % 2, slice(HALF, N)))
                if not last:
                    split_w(1, i * 2 + 3)

            pairs(gp, body, ch, 8)
            barrier(gp, 1)
            ch.step(gp.memset(wabs[QR - P:P, 1, :], 0.0))
            gp.wait_ge(in_e, 64)

            def steps(t, x, on):
                if on(1):
                    gp.wait_ge(e_ve, t)
                    gp.tensor_tensor(sm[1 - x][:, 9:10], sm[1 - x][:, 8:9], half[:, 0:1], ALU.pow).then_inc(e_rstd, 1)
                if on(2):
                    gp.tensor_tensor(xb[x][:, :], pick(xtok, t - 2, slice(0, C)), b2b[:, :], ALU.add).then_inc(e_xb, 1)
                if on(1):
                    gp.wait_ge(e_z, t)
                    ch.step(gp.tensor_tensor(hb[1 - x][:, :], hb[1 - x][:, :], gamb[:, :], ALU.mult))
                    gp.tensor_tensor(hb[1 - x][:, :], hb[1 - x][:, :], betb[:, :], ALU.add).then_inc(e_beta, 1)

            skewed(gp, steps, ch, 2)
            gp.wait_ge(f_w, 1)
            gp.tensor_tensor(wflo[:, :, :], wfst[:, :, :], wfhi[:, :, :].bitcast(F32), ALU.subtract).then_inc(f_wlo, 1)
            barrier(gp, 2)

            def fsteps(t, x, on):
                if on(1):
                    gp.wait_ge(f_bn, t)
                    gp.tensor_tensor(fs[1 - x][:, 12:15], fs[1 - x][:, 8:11], half[:, 0:3], ALU.pow).then_inc(f_rstd, 1)

            skewed(gp, fsteps)
            barrier(gp, 3)
            ch.did(gp.memset(acc[:, :, :], 0.0))
            ch.did(gp.memset(causb[:, :, :], 0.0))
            ch.wait()
            for qt in range(2):
                gp.affine_select(out=acc[:, qt::2, :], in_=acc[:, qt::2, :], compare_op=ALU.is_ge, fill=-3e38, base=qt * P,
                                 pattern=[[0, B], [-1, T]], channel_multiplier=1).then_inc(i_init, 1)
                gp.affine_select(out=causb[:, qt, :], in_=causb[:, qt, :], compare_op=ALU.is_ge, fill=-1e9, base=qt * P,
                                 pattern=[[-1, T]], channel_multiplier=1).then_inc(i_init, 1)

            def split_q(n, x):
                gp.wait_ge(q_whi, n + 1)
                gp.tensor_tensor(wilo[x][:, :, :], wi[x][:, :, :], wihi[x][:, :, :].bitcast(F32), ALU.subtract).then_inc(q_wlo, 1)

            def rope_q(n, x, w, tab, first=False):
                gp.wait_ge(q_front, (n * 4) + (2 * w + 2))
                ch.step(gp.tensor_tensor(ish[w][:, :], ish[w][:, :], tab[:, :], ALU.mult))
                if not first:
                    gp.wait_ge(q_scores, (n * 4) - 3)
                gp.tensor_tensor(iq[x][:, w * HALF:(w + 1) * HALF], ish[w][:, :], it1[w][:, :], ALU.add).then_inc(q_ready, 1)

            split_q(0, 0)
            split_q(1, 1)
            gp.wait_ge(in_i, 32)
            for w in range(2):
                rope_q(0, 0, w, tabs1, True)

            def heads(base, tab, i, last):
                for h in range(2):
                    n = i * 2 + (base + h)
                    if base == 0:
                        split_q(n + 2, h)
                    if not (last and h):
                        for w in range(2):
                            rope_q(n + 1, 1 - h, w, tab)
                    if base and not last:
                        split_q(n + 2, h)

            with gp.Fori(0, PAIRS - 1) as i:
                ch.loop(i, 0, 4)
                heads(0, tabs1, i, False)
                ch.close(PAIRS - 1)
            for w in range(2):
                rope_q(H - 1, 1, w, tabs1)
            split_q(H, 0)
            split_q(H + 1, 1)
            gp.wait_ge(in_i2, 32)
            for w in range(2):
                rope_q(H, 0, w, tabs2)
            for k in range(3):
                gp.wait_ge(j_clip, 2 * k + 2)
                gp.tensor_scalar(wt[k][:, :], uround[:, :], -1.0, 1.0, ALU.mult, ALU.add).then_inc(j_tern, 1)
            with gp.Fori(0, PAIRS - 1) as i:
                ch.loop(i, 0, 4)
                heads(H, tabs2, i, False)
                ch.close(PAIRS - 1)
            heads(H, tabs2, PAIRS - 1, True)
            barrier(gp, 4)
            with gp.Fori(0, 2) as n:
                for f in range(NF):
                    gp.wait_ge(j_hhi, n * NF + (f + 1))
                    gp.tensor_tensor(hlo[:, f, :], h32[f % 2][:, :], hhi[:, f, :].bitcast(F32), ALU.subtract).then_inc(j_hlo, 1)

        @block.scalar
        def _(act):
            act.wait_ge(in_par, 32)
            act.activation(ew[:, :], par[:, 0, :], ACT.Exp).then_inc(ach, 1)
            act.wait_ge(ach, 1)
            act.activation(ew[:, :], ew[:, :], ACT.Exp, scale=-1.0).then_inc(s_decay, 1)
            act.wait_ge(s_tf, 1)
            act.activation(tf[:, :], tf[:, :], ACT.Exp, scale=-1.0).then_inc(s_tf, 1)
            for c in range(KC):
                act.wait_ge(s_kmin, c + 1)
                act.activation(ek[:, c, :], ek[:, c, :], ACT.Exp).then_inc(s_ek, 1)

            def gate_exp(gu, prologue=False):
                euk = gate_buffers(gu, prologue)[4]
                act.wait_ge(s_ukmin, gu + 1)
                act.activation(euk[:, :], euk[:, :], ACT.Exp).then_inc(s_euk, 1)

            def split_w(x, hd):
                act.wait_ge(in_w[x], (hd - x) * 8 + 16)
                act.wait_ge(s_wused, hd + 1)
                act.activation(whi[x][:, :, :], wst[x][:, :, :], ACT.Copy).then_inc(s_whi, 1)

            def split_wv(i):
                act.wait_ge(in_wv, i * 16 + 16)
                act.wait_ge(s_wvused, i + 1)
                act.activation(wvhi[:, :, :], wvst[:, :, :], ACT.Copy).then_inc(s_wvhi, 1)

            def copy_chunk(g, bank, dst, done, scale=1.0, src=None):
                act.wait_ge(s_chunk, g + 1)
                src = chunk_bank[bank][:, :] if src is None else src
                act.activation(dst, src, ACT.Copy, scale=scale).then_inc(done, 1)
                act.drain().then_inc(s_free[bank], 1)

            QS = DN ** -0.5

            def qkv_chunk(g, bank, x, kind, w):
                if kind == "q":
                    copy_chunk(g, bank, qn[x][:, w * HALF:(w + 1) * HALF], s_qk, QS)
                elif kind == "k":
                    copy_chunk(g, bank, kn[x][:, w * HALF:(w + 1) * HALF], s_qk)
                else:
                    copy_chunk(g, bank, v[:, 2 * w:2 * w + 2, :].rearrange("p a b -> p (a b)"), s_v)

            def exps(u, par_):
                act.wait_ge(s_negmax, u + 1)
                for q in range(2):
                    last = act.activation(pr[par_][:, q, :], score_bank[par_][:, q * T:(q + 1) * T], ACT.Exp,
                                          bias=negm[par_][:, q:q + 1], accum_out=sums[par_][:, q:q + 1])
                last.then_inc(s_exp, 1)

            for c in range(KC):
                for bh in range(2):
                    gate_exp(2 * c + bh, True)
            act.sem_inc(s_wused, 2)
            act.sem_inc(s_wvused, 1)
            split_w(0, 0)
            split_wv(0)
            split_w(1, 1)
            act.wait_ge(in_x, 16)
            act.activation(xt[:, :, :], xt[:, :, :], ACT.Sigmoid).then_inc(s_sig, 1)
            for c in range(KC):
                act.wait_ge(s_y, 4 * c + 4)
                act.activation(yhi[:, c, :], y32[:, c, :], ACT.Copy).then_inc(s_yhi, 1)
            for s, (kind, w) in enumerate((("r", 0), ("r", 1), ("q", 0), ("k", 0), ("q", 1), ("k", 1),
                                           ("v", 0), ("v", 1), ("v", 2), ("v", 3))):
                if kind != "r":
                    qkv_chunk(s, s % 2, 0, kind, w)
            exps(0, 0)

            def gate_copy(gu, ci, bh):
                act.wait_ge(s_sums, gu)
                for src, r in ((ekv, nb), (ek, db)):
                    act.activation(r[:, :], pick(src, ci, slice(bh * HALF, (bh + 1) * HALF)), ACT.Copy)
                act.drain().then_inc(s_rev, 1)

            gate_copy(4, 0, 0)

            def body(i, g, last):
                for h, (front, tail) in enumerate(chunks(g, last)):
                    for s in range(4):
                        u = i * 8 + (4 * h + s)
                        if not (last and h == 1 and s == 3):
                            exps(u + 1, (s + 1) % 2)
                        if h == 0 and s == 0 and not last:
                            split_w(0, i * 2 + 2)
                            split_wv(i + 1)
                        if h == 1 and s == 1 and not last:
                            split_w(1, i * 2 + 3)
                        if g and s == 0:
                            gate_exp(i * 2 + (4 + h))
                        for kind, w in front[s]:
                            gi, bank = chunk_at(i, h, kind, w), bank_at(i, h, kind, w)
                            if kind in "qk":
                                qkv_chunk(gi, bank, 1 - h, kind, w)
                            if kind == "g":
                                dst = gtok[:, bass.ds(i, 1), 4 * h:4 * h + 4, :].rearrange("p l t n -> p (l t) n")
                                copy_chunk(gi, bank, dst, s_gtok, src=chunk_bank[bank][:, :].rearrange("p (t n) -> p t n", t=4))
                        act.wait_ge(s_pv, u + 1)
                        act.activation(ot[:, h, s * T:(s + 1) * T], pv_bank[s % 2][:, 0:T], ACT.Copy).then_inc(s_o, 1)
                        if g and s == 3:
                            gate_copy(i * 2 + (5 + h), i % 2 if h == 0 else (i + 1) % 2, 1 - h)
                        for kind, w in tail[s]:
                            if kind == "v":
                                qkv_chunk(chunk_at(i, h, kind, w), bank_at(i, h, kind, w), 0, kind, w)

            pairs(act, body)
            for k in range(2):
                act.wait_ge(in_t0[k], 16)
                if k:
                    act.wait_ge(s_abs, k)
                act.activation(wround[:, :], wtern[k][:, :], ACT.Abs, accum_out=wsum[:, k:k + 1]).then_inc(s_abs, 1)
            for k in range(2):
                act.wait_ge(s_wscale, k + 1)
                act.wait_ge(s_abs, 2)
                if k:
                    act.wait_ge(s_tern, k)
                act.activation(wround[:, :], wtern[k][:, :], ACT.Copy, bias=MAGIC, scale=wrec[:, k:k + 1]).then_inc(s_round, 1)
            barrier(act, 1)
            def steps(t, x, on):
                if on(0):
                    act.wait_ge(e_scale, t + 1)
                    act.activation(y[x][:, :], y[x][:, :], ACT.Copy, bias=MAGIC, scale=sm[x][:, 2:3]).then_inc(e_qm, 1)
                if on(1):
                    act.wait_ge(e_hb, t)
                    act.activation(hb[1 - x][:, :], hb[1 - x][:, :], ACT.Gelu).then_inc(e_gelu, 1)
                if on(2):
                    act.wait_ge(e_scale2, t - 1)
                    act.activation(hb[x][:, :], hb[x][:, :], ACT.Copy, bias=MAGIC, scale=sm[x][:, 18:19]).then_inc(e_qm2, 1)
                if on(0):
                    act.wait_ge(e_qt, t + 1)
                    act.activation(yqt[x][:, :, :].rearrange("p a b -> p (a b)"), qturn[x][:, 0:C], ACT.Copy).then_inc(e_qtc, 1)
                if on(2):
                    act.wait_ge(e_qt2, t - 1)
                    act.activation(hqt[x][:, :, :].rearrange("p a b -> p (a b)"), turn2[:, :], ACT.Copy).then_inc(e_qtc2, 1)
                if on(1):
                    act.wait_ge(e_nm, t)
                    act.activation(hb[1 - x][:, :], hb[1 - x][:, :], ACT.Identity, bias=sm[1 - x][:, 10:11],
                                   scale=sm[1 - x][:, 9:10]).then_inc(e_z, 1)

            for t in range(NT):
                act.activation(sga[:, t, :], xtok[:, t, :], ACT.Sigmoid).then_inc(e_sig, 1)
            skewed(act, steps)
            act.wait_ge(in_f, 16 * 7)
            act.activation(wfhi[:, :, :], wfst[:, :, :], ACT.Copy).then_inc(f_w, 1)
            for n in range(8):
                act.wait_ge(s_hw, n + 1)
                bank = ps[n % 2]
                if n < 4:
                    k, g8 = n % 2, n // 2
                    rows = P if k == 0 else QR - P
                    act.activation(wabs[0:rows, k, g8 * 512:(g8 + 1) * 512], bank[0:rows, :], ACT.Copy).then_inc(s_hwc, 1)
                else:
                    act.activation(wvo[:, 2 * (n - 4):2 * (n - 4) + 2, :].rearrange("p a b -> p (a b)"), bank[:, :], ACT.Copy).then_inc(s_hwc, 1)
            barrier(act, 2)

            def fsteps(t, x, on):
                o = 1 - x
                if on(0):
                    act.activation(fsg[x][:, :], pick(xtok, t, slice(0, C)), ACT.Sigmoid).then_inc(f_sig, 1)
                if on(1):
                    act.wait_ge(f_pc, t)
                    act.activation(junk[:, 0:QR], fp[o][:, 0:QR], ACT.Square, accum_out=fs[o][:, 0:1])
                    act.activation(junk[:, QR:QR + KVR], fp[o][:, QR:QR + KVR], ACT.Square, accum_out=fs[o][:, 1:2]).then_inc(f_sq, 1)
                if on(0):
                    act.wait_ge(f_yt, t + 1)
                    act.activation(fyhi[x][:, :, :].rearrange("p a b -> p (a b)"), fturn[x][:, 0:C], ACT.Copy).then_inc(f_hi, 1)
                if on(2):
                    act.wait_ge(f_t, t - 1)
                    cols = bass.ds((t - 2) * P, P)
                    act.activation(ikt[:, cols], fout[x][:, 3 * P:4 * P], ACT.Copy)
                    act.activation(qrhi[:, 0, cols], fout[x][:, 0:P], ACT.Copy, scale=lnw[:, 0:1])
                    act.activation(qrhi[0:QR - P, 1, cols], fout[x][0:QR - P, P:2 * P], ACT.Copy, scale=lnw[0:QR - P, 1:2])
                    act.drain().then_inc(f_hi2, 1)
                if on(1):
                    act.wait_ge(f_rstd, t)
                    act.activation(qrs[o][:, :], fp[o][:, 0:QR], ACT.Copy, scale=fs[o][:, 12:13]).then_inc(f_qrs, 1)
                    act.activation(pick(iw, t - 1, slice(0, H)), fp[o][:, 448:464], ACT.Copy, scale=H ** -0.5).then_inc(f_free, 1)
                    act.wait_ge(f_ki, t)
                    act.activation(pick(vl, t - 1, slice(0, KVR)), ki[o][:, 0:KVR], ACT.Copy).then_inc(f_vl, 1)

            skewed(act, fsteps)
            barrier(act, 3)
            act.sem_inc(i_relu, 4)
            act.sem_inc(q_abs, 1)

            def split_q(n, x):
                act.wait_ge(in_q[x], (n - x) * 8 + 16)
                act.wait_ge(q_wused, n + 1)
                act.activation(wihi[x][:, :, :], wi[x][:, :, :], ACT.Copy).then_inc(q_whi, 1)

            def stage_q(m, x):
                act.wait_ge(in_q[x], (m - x) * 8 + 16 + 8 * H)
                act.wait_ge(q_wlo, m + (H - 1))
                act.activation(wi[x][:, :, 0:KVR], pick_k(wabs, m), ACT.Copy).then_inc(q_abs, 1)
                act.wait_ge(q_abs, m + 2)
                split_q(m + H, x)

            def pick_k(t, m):
                return t[:, :, bass.ds(m * KVR, KVR)] if not isinstance(m, int) else t[:, :, m * KVR:(m + 1) * KVR]

            def relus(n, s):
                act.wait_ge(q_scores, n * 4 + (s + 1))
                act.wait_ge(i_acc, n * 8 + (2 * s + 2))
                act.activation(rl[s][:, :], iscore[s][:, 0:384], ACT.Relu).then_inc(i_relu, 1)

            split_q(0, 0)
            split_q(1, 1)
            with act.Fori(0, PAIRS - 1) as i:
                for h in range(2):
                    n = i * 2 + h
                    split_q(n + 2, h)
                    for s in range(4):
                        relus(n, s)
            def weight_abs(k):
                act.wait_ge(in_u, 16 * k + 16)
                act.activation(wt[k][:, :], ust[:, :], ACT.Abs, accum_out=wsum[:, 2 + k:3 + k]).then_inc(j_abs, 1)

            def weight_round(k):
                act.wait_ge(j_scale, k + 1)
                if k:
                    act.wait_ge(j_tern, k)
                act.activation(uround[:, :], ust[:, :], ACT.Copy, bias=MAGIC, scale=wrec[:, 2 + k:3 + k]).then_inc(j_round, 1)
                act.wait_ge(j_round, k + 1)
                act.activation(uround[:, :], uround[:, :], ACT.Relu, bias=clipc[:, 0:1]).then_inc(j_clip, 1)
                act.wait_ge(j_clip, 2 * k + 1)
                act.activation(uround[:, :], uround[:, :], ACT.Relu, bias=clipc[:, 1:2], scale=-1.0).then_inc(j_clip, 1)

            weight_abs(0)
            for s in range(4):
                relus(H - 2, s)
            stage_q(0, 0)
            for s in range(4):
                relus(H - 1, s)
            stage_q(1, 1)
            for k in range(3):
                if k:
                    weight_abs(k)
                weight_round(k)

            def exps1(u, x):
                act.wait_ge(a_negmax, u + 1)
                for q, cols in enumerate((slice(0, P), slice(P, 384))):
                    last = act.activation(p1[x][:, cols], score_bank[x][:, cols], ACT.Exp, bias=negm1[x][:, q:q + 1],
                                          accum_out=sums1[x][:, q:q + 1])
                    last.then_inc(a_exp, 1)

            exps1(0, 0)

            def turned_copy(u, x):
                act.wait_ge(a_turn, u + 1)
                act.activation(pt1[x][:, :], turn_bank[:, 0:384], ACT.Copy).then_inc(a_pt, 1)

            def out_copy(u, h, s):
                rows = slice(h * 64, h * 64 + 64)
                act.wait_ge(a_pv, u + 1)
                act.activation(ot1[rows, s * T:(s + 1) * T], pv_bank[s % 2][rows, 0:T], ACT.Copy).then_inc(a_o, 1)

            def attention_body(i, first, last):
                for h in range(2):
                    for s in range(4):
                        u = i * 8 + (4 * h + s)
                        if not (last and h == 1 and s == 3):
                            exps1(u + 1, (s + 1) % 2)
                        turned_copy(u, s % 2)
                        if not (first and h == 0 and s == 0):
                            out_copy(u - 1, h if s else 1 - h, (s - 1) % 4)
                        if s == 1 and not last:
                            stage_q(i * 2 + (h + 2), h)

            attention_body(0, True, False)
            with act.Fori(1, PAIRS - 1) as i:
                attention_body(i, False, False)
            attention_body(PAIRS - 1, False, True)
            out_copy(8 * PAIRS - 1, 1, 3)
            barrier(act, 4)
            act.activation(jsg[:, :, :], xtok[:, :, :], ACT.Sigmoid).then_inc(j_sig, 1)
            for g in range(4):
                act.wait_ge(j_yt, g + 1)
                act.activation(yhi[:, :, g * T:(g + 1) * T], ps[g][:, :].rearrange("p (c n) -> p c n", c=KC), ACT.Copy).then_inc(j_hi, 1)
            with act.Fori(0, 2) as n:
                for f in range(NF + 1):
                    if f < NF:
                        act.wait_ge(j_proj, n * NF + (f + 1))
                        act.activation(silu[f % 2][:, :], up_bank[f % 2][:, :], ACT.Silu, scale=wmean[:, 2:3]).then_inc(j_silu, 1)
                    if f > 0:
                        act.wait_ge(j_h, n * NF + f)
                        act.wait_ge(j_down, n * 4 + 1)
                        act.activation(hhi[:, f - 1, :], h32[(f - 1) % 2][:, :], ACT.Copy).then_inc(j_hhi, 1)

        @block.vector
        def _(dve):
            ch = Chain(dve, dch)
            dve.wait_ge(in_k, 16)
            for c in range(KC):
                dve.tensor_scalar(ek[:, c, :], kt[:, c, :], 30.0, None, ALU.min).then_inc(s_kmin, 1)
            dve.wait_ge(in_par, 32)
            dve.tensor_reduce(tf[:, :], condb[:, :, :], AX.X, ALU.add).then_inc(s_tf, 1)
            dve.wait_ge(s_tf, 2)
            ch.step(dve.tensor_scalar(tf[:, :], tf[:, :], 1.0, None, ALU.add))
            ch.step(dve.reciprocal(tf[:, :], tf[:, :]))
            ch.did(dve.tensor_scalar(dfac[:, :], tf[:, :], 0.5, 0.5, ALU.mult, ALU.add))
            ch.did(dve.tensor_scalar(gate[:, :], tf[:, :], 0.2, 0.8, ALU.mult, ALU.add))
            ch.wait()
            dve.wait_ge(s_decay, 1)
            for b in range(B):
                ch.did(dve.tensor_scalar(decay[:, :, b], ew[:, :], dfac[:, b:b + 1], None, ALU.mult))
            for c in range(KC):
                dve.wait_ge(s_ek, c + 1)
                ch.did(dve.tensor_tensor(ekv[:, c, :], ek[:, c, :], kt[:, c, :], ALU.mult))
            ch.wait()

            def cols(t, ci, b, rev):
                s = slice((b + 1) * T - 1, b * T - 1 if b else None, -1) if rev else slice(b * T, (b + 1) * T)
                return pick(t, ci, s)

            def gate_scans(lc, ci, bh, bufs=gbuf):
                nf, nb, df, db, euk, dd = bufs
                for j in range(2):
                    b = 2 * bh + j
                    dk = pick(decay, lc, slice(b, b + 1)).broadcast_to([P, T])
                    fw = slice(j * T, (j + 1) * T)
                    bw = slice((j + 1) * T - 1, j * T - 1 if j else None, -1)
                    for src, f, r in ((ekv, nf, nb), (ek, df, db)):
                        dve.tensor_tensor_scan(f[:, fw], dk, cols(src, ci, b, False), 0.0, ALU.mult, ALU.add)
                        back = cols(src, ci, b, True) if isinstance(ci, int) else r[:, bw]
                        last = dve.tensor_tensor_scan(r[:, bw], dk, back, 0.0, ALU.mult, ALU.add)
                last.then_inc(s_scan, 1)

            def gate_ukmin(lc, ci, bh, bufs=gbuf):
                euk = bufs[4]
                u = par[:, 1, lc:lc + 1] if isinstance(lc, int) else par[:, 1, bass.ds(lc, 1)]
                dve.tensor_scalar(euk[:, :], pick(kt, ci, slice(bh * HALF, (bh + 1) * HALF)), u, 30.0,
                                  ALU.add, ALU.min).then_inc(s_ukmin, 1)

            def gate_dd(gu, ci, bh, bufs=gbuf):
                euk, dd = bufs[4:]
                s = slice(bh * HALF, (bh + 1) * HALF)
                dve.wait_ge(s_euk, gu + 1)
                dve.tensor_tensor(dd[:, :], euk[:, :], pick(ek, ci, s), ALU.subtract).then_inc(s_dd, 1)

            def gate_den(gu, bufs=gbuf):
                df = bufs[2]
                dve.wait_ge(s_sums, gu + 1)
                ch.step(dve.tensor_scalar(df[:, :], df[:, :], 1e-8, None, ALU.max))

            def gate_reciprocal(j, bufs=gbuf):
                df = bufs[2]
                ch.step(dve.reciprocal(df[:, j * T:(j + 1) * T], df[:, j * T:(j + 1) * T]))

            def gate_factor(dst, bufs=gbuf):
                return dve.tensor_tensor(dst, bufs[0][:, :], bufs[2][:, :], ALU.mult)

            for gu in range(2 * KC + 1):
                if gu < 2 * KC:
                    c, bh = divmod(gu, 2)
                    z = gate_buffers(gu, True)
                    gate_ukmin(c, c, bh, z)
                    gate_scans(c, c, bh, z)
                    gate_dd(gu, c, bh, z)
                if gu > 0:
                    c, bh = divmod(gu - 1, 2)
                    z = gate_buffers(gu - 1, True)
                    gate_den(gu - 1, z)
                    gate_reciprocal(0, z)
                    gate_reciprocal(1, z)
                    ch.step(gate_factor(g0[:, c, bh * HALF:(bh + 1) * HALF], z))
            dve.wait_ge(s_sig, 1)
            for c in range(KC):
                for b in range(B):
                    s = slice(b * T, (b + 1) * T)
                    dve.scalar_tensor_tensor(y32[:, c, s], xt[:, c, s], gate[:, b:b + 1], g0[:, c, s],
                                             ALU.mult, ALU.mult).then_inc(s_y, 1)
            for c in range(KC):
                dve.wait_ge(s_yhi, c + 1)
                dve.tensor_tensor(ylo[:, c, :], y32[:, c, :], yhi[:, c, :].bitcast(F32), ALU.subtract).then_inc(s_ylo, 1)

            def rope_front(g, bank, w):
                dve.wait_ge(s_chunk, g + 1)
                dve.tensor_tensor(rt1[w][:, :], chunk_bank[bank][:, :], tabc[:, :], ALU.mult)
                dve.stream_shuffle(rsh[w][:, :], chunk_bank[bank][:, :], SWAP).then_inc(s_shuf, 1)
                dve.drain().then_inc(s_free[bank], 1)

            def rope_back(rn, x, w):
                dve.wait_ge(s_t2, rn + w + 1)
                s = slice(w * HALF, (w + 1) * HALF)
                dve.tensor_tensor(qr[x][0:DR, s], rt1[w][0:DR, :], rsh[w][0:DR, :], ALU.add)
                dve.tensor_tensor(kr[x][0:DR, s], rt1[w][DR:P, :], rsh[w][DR:P, :], ALU.add).then_inc(s_rope, 1)

            def negmax(u, par_):
                dve.wait_ge(s_scores, u + 1)
                dve.tensor_reduce(negm[par_][:, :], score_bank[par_][:, :].rearrange("p (q k) -> p q k", q=2),
                                  AX.X, ALU.max, negate=True).then_inc(s_negmax, 1)

            def normalise(u, par_):
                dve.wait_ge(s_exp, u + 1)
                ch.step(dve.reciprocal(rsum[par_][:, :], sums[par_][:, :]))
                for q in range(2):
                    last = dve.tensor_scalar(pr[par_][:, q, :], pr[par_][:, q, :], rsum[par_][:, q:q + 1], None, ALU.mult)
                last.then_inc(s_norm, 1)

            dve.wait_ge(in_tab, 32)
            rope_front(0, 0, 0)
            rope_front(1, 1, 1)
            rope_back(0, 0, 0)
            rope_back(0, 0, 1)
            negmax(0, 0)
            normalise(0, 0)
            dve.wait_ge(in_wo, 32)

            def body(i, g, last):
                for h, (front, tail) in enumerate(chunks(g, last)):
                    rn = i * 4 + (2 + 2 * h)
                    ropes = ("r", 0) in front[0]
                    for s in range(4):
                        u = i * 8 + (4 * h + s)
                        more = not (last and h == 1 and s == 3)
                        if more:
                            negmax(u + 1, (s + 1) % 2)
                        dve.wait_ge(s_turn, u + 1)
                        dve.tensor_copy(pt[s % 2][:, :, :].rearrange("p a b -> p (a b)"), turn_bank[:, :]).then_inc(s_pt, 1)
                        if ropes and s == 0:
                            rope_front(chunk_at(i, h, "r", 0), bank_at(i, h, "r", 0), 0)
                        if g and s == 2:
                            gate_den(i * 2 + (4 + h))
                            gate_reciprocal(0)
                        if more:
                            normalise(u + 1, (s + 1) % 2)
                        if ropes and s == 0:
                            rope_front(chunk_at(i, h, "r", 1), bank_at(i, h, "r", 1), 1)
                        if ropes and s == 1:
                            rope_back(rn, 1 - h, 0)
                            rope_back(rn, 1 - h, 1)
                        for kind, w in front[s] + tail[s]:
                            if kind == "o":
                                bank = bank_at(i, h, kind, w)
                                dve.wait_ge(s_chunk, chunk_at(i, h, kind, w) + 1)
                                xs = xtok[:, 2 * w:2 * w + 2, :].rearrange("p a b -> p (a b)")
                                dve.tensor_tensor(xs, chunk_bank[bank][:, :], xs, ALU.add).then_inc(s_x1, 1)
                                dve.drain().then_inc(s_free[bank], 1)
                        if g:
                            gu = i * 2 + (4 + h)
                            if s == 0:
                                gate_ukmin(i + 2, i % 2, h)
                                dve.wait_ge(s_rev, i * 2 + (1 + h))
                                gate_scans(i + 2, i % 2, h)
                                gate_dd(gu, i % 2, h)
                            if s == 2:
                                gate_reciprocal(1)
                                dve.wait_ge(s_gused, i * 2 + (1 + h))
                                gate_factor(gg[:, :]).then_inc(s_gg, 1)

            pairs(dve, body, ch, 14)
            for k in range(2):
                dve.wait_ge(s_tot, 1)
                ch.step(dve.tensor_scalar(wmean[:, k:k + 1], ps[7][:, k:k + 1], 1.0 / (C * F), 1e-5, ALU.mult, ALU.max))
                dve.reciprocal(wrec[:, k:k + 1], wmean[:, k:k + 1]).then_inc(s_wscale, 1)
            for k in range(2):
                dve.wait_ge(s_round, k + 1)
                ch.step(dve.tensor_scalar(wround[:, :], wround[:, :], -MAGIC, 1.0, ALU.add, ALU.min))
                dve.tensor_scalar((w1q, w2q)[k][:, :, :].rearrange("p a b -> p (a b)"), wround[:, :], -1.0, None, ALU.max).then_inc(s_tern, 1)
            barrier(dve, 1)
            dve.wait_ge(in_e, 64)

            def quant_scale(src, s_, at, done):
                ch.step(dve.tensor_reduce(s_[:, at:at + 1], src, AX.X, ALU.max, apply_absolute_value=True))
                ch.step(dve.tensor_scalar(s_[:, at + 1:at + 2], s_[:, at:at + 1], 1e-5, 1.0 / 127.0, ALU.max, ALU.mult))
                dve.reciprocal(s_[:, at + 2:at + 3], s_[:, at + 1:at + 2]).then_inc(done, 1)

            def gated(dst, src, t, L, b, n_):
                gcol = gate[:, b:b + 1] if isinstance(b, int) else gate[:, bass.ds(b, 1)]
                fac = gtok[:, 2 * L:2 * L + 2, t:t + 1, :] if isinstance(t, int) else gtok[:, 2 * L:2 * L + 2, bass.ds(t, 1), :]
                return dve.scalar_tensor_tensor(dst.rearrange("p (l n) -> p l n", l=2), src.rearrange("p (l n) -> p l n", l=2), gcol,
                                                fac.rearrange("p l t n -> p l (t n)"), ALU.mult, ALU.mult)

            def tile_batch(t):
                return t // 2

            def steps(t, x, on):
                o = 1 - x
                if on(3):
                    dve.wait_ge(e_y2, t - 2)
                    dve.wait_ge(e_xb, t - 2)
                    ch.wait()
                    dve.scalar_tensor_tensor(pick(xtok, t - 3, slice(0, C)), ffn2[o][:, 0:C], sm[o][:, 19:20], xb[o][:, :],
                                             ALU.mult, ALU.add).then_inc(e_x2, 1)
                if on(0):
                    dve.wait_ge(e_sig, t + 1)
                    ch.step(gated(y[x][:, :], pick(sga, t, slice(0, C)), t, 0, tile_batch(t), 0))
                    quant_scale(y[x][:, :], sm[x], 0, e_scale)
                if on(1):
                    dve.wait_ge(e_h, t)
                    ch.step(dve.tensor_scalar(sm[o][:, 3:4], sm[o][:, 1:2], wmean[:, 0:1], None, ALU.mult))
                    for n in range(2):
                        last = dve.scalar_tensor_tensor(hb[o][:, n * 512:(n + 1) * 512], ffn1[o][n][:, :], sm[o][:, 3:4],
                                                        b1b[:, n * 512:(n + 1) * 512], ALU.mult, ALU.add)
                    last.then_inc(e_hb, 1)
                if on(2):
                    dve.wait_ge(e_beta, t - 1)
                    quant_scale(hb[x][:, :], sm[x], 16, e_scale2)
                if on(0):
                    dve.wait_ge(e_qm, t + 1)
                    dve.tensor_scalar(yq[x][:, :], y[x][:, :], -MAGIC, None, ALU.add).then_inc(e_q, 1)
                if on(1):
                    dve.wait_ge(e_gelu, t)
                    for n in range(2):
                        ch.did(dve.bn_stats(sm[o][:, 32 + 6 * n:38 + 6 * n], hb[o][:, n * 512:(n + 1) * 512]))
                    ch.wait()
                    dve.sem_inc(s_pause, 1)
                    ch.step(dve.bn_aggr(sm[o][:, 6:8], sm[o][:, 32:44]))
                    dve.tensor_scalar(sm[o][:, 8:9], sm[o][:, 7:8], 1e-5, None, ALU.add).then_inc(e_ve, 1)
                if on(2):
                    dve.wait_ge(e_qm2, t - 1)
                    dve.tensor_scalar(hq[x][:, :], hb[x][:, :], -MAGIC, None, ALU.add).then_inc(e_q2, 1)
                    ch.did(dve.tensor_scalar(sm[x][:, 19:20], sm[x][:, 17:18], wmean[:, 1:2], None, ALU.mult))
                if on(1):
                    dve.wait_ge(e_rstd, t)
                    dve.tensor_scalar(sm[o][:, 10:11], sm[o][:, 6:7], sm[o][:, 9:10], -1.0, ALU.mult, ALU.mult).then_inc(e_nm, 1)

            skewed(dve, steps, ch, 2 * 10)
            barrier(dve, 2)
            dve.wait_ge(in_f, 16 * 7)

            def fsteps(t, x, on):
                o = 1 - x
                if on(0):
                    dve.wait_ge(f_sig, t + 1)
                    gated(fy[x][:, :], fsg[x][:, :], t, 1, tile_batch(t), 1).then_inc(f_y, 1)
                if on(1):
                    s_ = fs[o]
                    dve.wait_ge(f_p, t)
                    dve.tensor_copy(fp[o][:, :], fproj[o][:, 0:464]).then_inc(f_pc, 1)
                    dve.wait_ge(f_pc, t)
                    ch.step(dve.bn_stats(s_[:, 16:22], fp[o][:, 320:448]))
                    dve.sem_inc(s_pause, 1)
                    ch.step(dve.bn_aggr(s_[:, 2:4], s_[:, 16:22]))
                    dve.wait_ge(f_sq, t)
                    ch.did(dve.tensor_scalar(s_[:, 8:9], s_[:, 0:1], 1.0 / QR, 1e-6, ALU.mult, ALU.add))
                    ch.did(dve.tensor_scalar(s_[:, 9:10], s_[:, 1:2], 1.0 / KVR, 1e-6, ALU.mult, ALU.add))
                    dve.tensor_scalar(s_[:, 10:11], s_[:, 3:4], 1e-6, None, ALU.add).then_inc(f_bn, 1)
                if on(0):
                    dve.wait_ge(f_hi, t + 1)
                    dve.tensor_tensor(fylo[x][:, :, :].rearrange("p a b -> p (a b)"), fturn[x][:, 0:C],
                                      fyhi[x][:, :, :].rearrange("p a b -> p (a b)").bitcast(F32), ALU.subtract).then_inc(f_lo, 1)
                if on(2):
                    dve.wait_ge(f_hi2, t - 1)
                    cols = bass.ds((t - 2) * P, P)
                    for k, rows in ((0, P), (1, QR - P)):
                        dve.scalar_tensor_tensor(qrlo[0:rows, k, cols], fout[x][0:rows, k * P:(k + 1) * P], lnw[0:rows, k:k + 1],
                                                 qrhi[0:rows, k, cols].bitcast(F32), ALU.mult, ALU.subtract)
                    ch.did(dve.tensor_copy(kct[:, cols], fout[x][:, 2 * P:3 * P]))
                if on(1):
                    s_, k_ = fs[o], ki[o]
                    dve.wait_ge(f_rstd, t)
                    ch.did(dve.tensor_scalar(k_[:, P:2 * P], fp[o][:, 320:448], s_[:, 2:3], s_[:, 14:15], ALU.subtract, ALU.mult))
                    ch.did(dve.tensor_copy(k_[:, KVR:P], fp[o][:, 256:320]))
                    ch.did(dve.scalar_tensor_tensor(k_[:, 0:KVR], fp[o][:, QR:QR + KVR], s_[:, 13:14], kvw[:, :], ALU.mult, ALU.mult))
                    ch.wait()
                    ch.step(dve.tensor_tensor(k_[:, P:2 * P], k_[:, P:2 * P], ikw[:, :], ALU.mult))
                    ch.step(dve.tensor_tensor(k_[:, P:2 * P], k_[:, P:2 * P], ikb[:, :], ALU.add))
                    kv = k_[:, :].rearrange("p (s r g h f) -> p s r g h f", s=2, r=2, g=2, h=2)[:, :, 1, :, :, :]
                    ra, rb = kv[:, :, :, 0, :], kv[:, :, :, 1, :]
                    tab = [tb[:, o, :].rearrange("p (s g f) -> p s g f", s=2, g=2) for tb in (ropec, ropes)]
                    r4 = [rp[:, n, :].rearrange("p (s g f) -> p s g f", s=2, g=2) for n in range(4)]
                    for n, (src, tb) in enumerate(((ra, 0), (rb, 1), (ra, 1), (rb, 0))):
                        ch.did(dve.tensor_tensor(r4[n], src, tab[tb], ALU.mult))
                    ch.wait()
                    dve.tensor_tensor(ra, r4[0], r4[1], ALU.subtract)
                    dve.tensor_tensor(rb, r4[2], r4[3], ALU.add).then_inc(f_ki, 1)

            skewed(dve, fsteps, ch, 2 * 14)
            barrier(dve, 3)
            dve.sem_inc(i_acc, 8)

            def front_q(n, w, tab, first=False):
                dve.wait_ge(q_chunk, n * 2 + (w + 1))
                if not first:
                    dve.wait_ge(q_ready, n * 2 + w - 1)
                dve.tensor_tensor(it1[w][:, :], chunk_bank[w][:, :], tab[:, :], ALU.mult).then_inc(q_front, 1)
                dve.stream_shuffle(ish[w][:, :], chunk_bank[w][:, :], SWAP).then_inc(q_front, 1)

            def accumulate(n, s):
                dve.wait_ge(i_relu, n * 4 + (s + 5))
                dve.wait_ge(i_acc, n * 8 + (2 * s + 2))
                for q, (cols, width) in enumerate(((slice(0, P), P), (slice(P, 384), T))):
                    tt = 2 * s + q
                    wcol = iw[:, tt, n:n + 1] if isinstance(n, int) else iw[:, tt, bass.ds(n, 1)]
                    dve.scalar_tensor_tensor(acc[:, tt, 0:width], rl[s][:, cols], wcol, acc[:, tt, 0:width],
                                             ALU.mult, ALU.add).then_inc(i_acc, 1)

            dve.wait_ge(in_i, 32)
            for w in range(2):
                front_q(0, w, tabc1, True)
            dve.wait_ge(i_init, 4)
            with dve.Fori(0, PAIRS - 1) as i:
                for h in range(2):
                    n = i * 2 + h
                    for s in range(4):
                        if s % 2 == 0:
                            front_q(n + 1, s // 2, tabc1)
                        accumulate(n, s)
            dve.wait_ge(in_i2, 32)
            for h in range(2):
                n = H - 2 + h
                for s in range(4):
                    if s % 2 == 0:
                        front_q(n + 1, s // 2, tabc2 if h else tabc1)
                    accumulate(n, s)
            dve.wait_ge(i_acc, 8 + 8 * H)
            widths = [(P, T)[tt % 2] for tt in range(NT)]
            for r in range(TOPK // 8):
                for tt in range(NT):
                    ch.did(dve.max(top8[:, tt, :], acc[:, tt, 0:widths[tt]]))
                ch.wait()
                for tt in range(NT):
                    ch.did(dve.match_replace(acc[:, tt, 0:widths[tt]], top8[:, tt, :], acc[:, tt, 0:widths[tt]], -3.3e38))
                ch.wait()
                if r % 3 == 0:
                    k = r // 3
                    c0 = slice(2 + k, 3 + k)
                    dve.wait_ge(j_tot, k + 1)
                    ch.step(dve.tensor_scalar(wmean[:, c0], out_bank[:, c0], 1.0 / (C * F), 1e-8, ALU.mult, ALU.add))
                    dve.reciprocal(wrec[:, c0], wmean[:, c0]).then_inc(j_scale, 1)
            for tt in range(NT):
                w_ = widths[tt]
                ch.step(dve.tensor_scalar(biasb[:, tt, 0:w_], acc[:, tt, 0:w_], -3.25e38, -1e9, ALU.is_gt, ALU.mult))
                dve.tensor_tensor(biasb[:, tt, 0:w_], biasb[:, tt, 0:w_], causb[:, tt % 2, 0:w_], ALU.min).then_inc(a_bias, 1)

            def negmax1(u, x):
                dve.wait_ge(q_scores, u + (4 * H + 1))
                for q, cols in enumerate((slice(0, P), slice(P, 384))):
                    last = dve.tensor_reduce(negm1[x][:, q:q + 1], score_bank[x][:, cols], AX.X, ALU.max, negate=True)
                    ch.did(last)
                dve.drain().then_inc(a_negmax, 1)

            def normalise1(u, x):
                dve.wait_ge(a_exp, u * 2 + 2)
                ch.step(dve.reciprocal(rsum1[x][:, :], sums1[x][:, :]))
                for q, cols in enumerate((slice(0, P), slice(P, 384))):
                    dve.tensor_scalar(p1[x][:, cols], p1[x][:, cols], rsum1[x][:, q:q + 1], None, ALU.mult).then_inc(a_norm, 1)

            negmax1(0, 0)
            normalise1(0, 0)

            def add_out(i, w):
                dve.wait_ge(a_out, i * 4 + (w + 1))
                xs = xtok[:, 2 * w:2 * w + 2, :].rearrange("p a b -> p (a b)")
                dve.tensor_tensor(xs, out_bank[:, :], xs, ALU.add).then_inc(a_x, 1)

            def attention_body(i, first, last):
                for h in range(2):
                    n = i * 2 + (H + h)
                    for s in range(4):
                        u = i * 8 + (4 * h + s)
                        if not (last and h == 1 and s == 3):
                            negmax1(u + 1, (s + 1) % 2)
                            normalise1(u + 1, (s + 1) % 2)
                        if s < 2 and not (last and h):
                            front_q(n + 1, s, tabc2)
                        if h == 1 and s >= 2:
                            add_out(i, s - 2)
                        if h == 0 and s < 2 and not first:
                            add_out(i - 1, s + 2)

            attention_body(0, True, False)
            with dve.Fori(1, PAIRS - 1) as i:
                ch.loop(i, 1, 8 * 3)
                attention_body(i, False, False)
                ch.close(PAIRS - 2)
            attention_body(PAIRS - 1, False, True)
            for w in (2, 3):
                add_out(PAIRS - 1, w)
            barrier(dve, 4)
            dve.wait_ge(j_sig, 1)
            for t in range(NT):
                gated(jy[:, t, :], jsg[:, t, :], t, 2, t // 2, 2).then_inc(j_y, 1)
            for g in range(4):
                dve.wait_ge(j_hi, g + 1)
                cols = slice(g * T, (g + 1) * T)
                dve.tensor_tensor(ylo[:, :, cols], ps[g][:, :].rearrange("p (c n) -> p c n", c=KC),
                                  yhi[:, :, cols].bitcast(F32), ALU.subtract).then_inc(j_lo, 1)
            with dve.Fori(0, 2) as n:
                for f in range(NF):
                    dve.wait_ge(j_silu, n * NF + (f + 1))
                    if f >= 2:
                        dve.wait_ge(j_hlo, n * NF + (f - 1))
                    dve.scalar_tensor_tensor(h32[f % 2][:, :], gate_bank[f % 2][:, :], wmean[:, 3:4], silu[f % 2][:, :],
                                             ALU.mult, ALU.mult).then_inc(j_h, 1)
                for j in range(4):
                    t = n * 4 + j
                    dve.wait_ge(j_down, n * 4 + (j + 2))
                    dve.wait_ge(j_out[j % 2], n * 32 + (16 * (j // 2 + 1)))
                    dve.scalar_tensor_tensor(xo[j % 2][:, :], down_bank[j % 2][:, 0:C], wmean[:, 4:5], pick(xtok, t, slice(0, C)),
                                             ALU.mult, ALU.add).then_inc(j_x, 1)

        @block.tensor
        def _(pe):
            pe.sem_inc(s_free[0], 1)
            pe.sem_inc(s_free[1], 1)
            pe.sem_inc(s_gused, 1)
            pe.wait_ge(s_const, 2)
            PASSES = ((whi, yhi), (wlo, yhi), (whi, ylo))

            def project(g, bank, uses, x, kind, w, pair=None):
                pe.wait_ge(s_free[bank], uses + 1)
                out_ = chunk_bank[bank]
                if kind in "qkr":
                    mt = "qkr".index(kind)
                    n = 0
                    for c in range(KC):
                        for wt, yt in PASSES:
                            last = pe.matmul(out_[:, :], wt[x][:, c, mt * P:(mt + 1) * P], yt[:, c, w * HALF:(w + 1) * HALF],
                                             start=(n == 0), stop=(n == 5))
                            n += 1
                elif kind == "v":
                    for j in range(2):
                        tt = 2 * w + j
                        n = 0
                        for c in range(KC):
                            for wt, yt in ((wvhi, yhi), (wvlo, yhi), (wvhi, ylo)):
                                last = pe.matmul(out_[:, j * 256:(j + 1) * 256], yt[:, c, tt * P:(tt + 1) * P], wt[:, c, :],
                                                 start=(n == 0), stop=(n == 5))
                                n += 1
                elif kind == "o":
                    for j in range(2):
                        tt = 2 * w + j
                        for h in range(2):
                            wh = pick(wo, pair * 2 + h, slice(0, C))
                            last = pe.matmul(out_[:, j * 256:(j + 1) * 256], ot[:, h, tt * P:(tt + 1) * P], wh,
                                             start=(h == 0), stop=(h == 1))
                else:
                    for q in range(4):
                        last = pe.transpose(out_[:, q * P:(q + 1) * P], gg[:, q * P:(q + 1) * P], ident[:, :])
                last.then_inc(s_chunk, 1)

            def scores(u, hd, x, b):
                pe.wait_ge(s_qk, hd * 4 + (2 if b < 2 else 4))
                pe.wait_ge(s_rope, hd * 2 + (1 if b < 2 else 2))
                bank = score_bank[b % 2]
                for q in range(2):
                    qs = slice(b * T + q * P, b * T + (q + 1) * P)
                    ks = slice(b * T, (b + 1) * T)
                    pe.matmul(bank[:, q * T:(q + 1) * T], qn[x][:, qs], kn[x][:, ks], start=True, stop=False)
                    last = pe.matmul(bank[:, q * T:(q + 1) * T], qr[x][0:DR, qs], kr[x][0:DR, ks], start=False, stop=True)
                last.then_inc(s_scores, 1)

            def turn(u, par_):
                pe.wait_ge(s_norm, u + 1)
                for k in range(2):
                    for q in range(2):
                        last = pe.transpose(turn_bank[:, k * T + q * P:k * T + (q + 1) * P],
                                            pr[par_][:, q, k * P:(k + 1) * P], ident[:, :])
                last.then_inc(s_turn, 1)

            def pv(u, pair, h, b):
                pe.wait_ge(s_pt, u + 1)
                pe.wait_ge(s_v, pair * 4 + (b + 1))
                for k in range(2):
                    last = pe.matmul(pv_bank[b % 2][:, 0:T], v[:, 2 * b + k, h * DN:(h + 1) * DN],
                                     pt[b % 2][:, k, :], start=(k == 0), stop=(k == 1))
                last.then_inc(s_pv, 1)

            pe.wait_ge(s_ylo, 2)
            pe.wait_ge(s_wlo, 1)
            pe.wait_ge(s_wvlo, 1)
            for s, (kind, w) in enumerate((("r", 0), ("r", 1), ("q", 0), ("k", 0), ("q", 1), ("k", 1),
                                           ("v", 0), ("v", 1), ("v", 2), ("v", 3))):
                project(s, s % 2, s // 2, 0, kind, w)
                if s == 5:
                    pe.drain().then_inc(s_wused, 1)
            pe.drain().then_inc(s_wvused, 1)
            scores(0, 0, 0, 0)

            def body(i, g, last):
                for h, (front, tail) in enumerate(chunks(g, last)):
                    if not (last and h == 1):
                        pe.wait_ge(s_wlo, i * 2 + (2 + h))
                        if h == 1:
                            pe.wait_ge(s_wvlo, i + 2)
                    for s in range(4):
                        u = i * 8 + (4 * h + s)
                        if s < 3:
                            scores(u + 1, i * 2 + h, h, s + 1)
                        elif not (last and h == 1):
                            scores(u + 1, i * 2 + (h + 1), 1 - h, 0)
                        turn(u, s % 2)
                        for kind, w in front[s]:
                            if kind == "o":
                                pe.wait_ge(s_o, i * 8 + (4 + w + 1))
                            if kind == "g":
                                pe.wait_ge(s_gg, i * 2 + (1 + h))
                            project(0, bank_at(i, h, kind, w), uses_at(i, h, kind, w), 1 - h, kind, w, i)
                            if kind == "g":
                                pe.drain().then_inc(s_gused, 1)
                            if (kind, w) == ("k", 1):
                                pe.drain().then_inc(s_wused, 1)
                        pv(u, i, h, s)
                        for kind, w in tail[s]:
                            if kind == "o":
                                pe.wait_ge(s_o, i * 8 + (4 + w + 1))
                            project(0, bank_at(i, h, kind, w), uses_at(i, h, kind, w), 0, kind, w, i)
                            if (kind, w) == ("v", 3):
                                pe.drain().then_inc(s_wvused, 1)

            pairs(pe, body)
            pe.wait_ge(s_abs, 2)
            pe.matmul(ps[7][:, 0:2], ones[:, :], wsum[:, 0:2], start=True, stop=True).then_inc(s_tot, 1)
            barrier(pe, 1)
            def steps(t, x, on):
                if on(0):
                    pe.wait_ge(e_q, t + 1)
                    for c in range(KC):
                        last = pe.transpose(qturn[x][:, c * P:(c + 1) * P], yq[x][:, c * P:(c + 1) * P], identb[:, :])
                    last.then_inc(e_qt, 1)
                if on(2):
                    pe.wait_ge(e_q2, t - 1)
                    for f in range(NF):
                        last = pe.transpose(turn2[:, f * P:(f + 1) * P], hq[x][:, f * P:(f + 1) * P], identb[:, :])
                    last.then_inc(e_qt2, 1)
                if on(0):
                    pe.wait_ge(e_qtc, t + 1)
                    for n in range(2):
                        for c in range(KC):
                            last = pe.matmul(ffn1[x][n][:, :], yqt[x][:, c, :], w1q[:, c, n * 512:(n + 1) * 512], start=(c == 0), stop=(c == 1))
                    last.then_inc(e_h, 1)
                if on(2):
                    pe.wait_ge(e_qtc2, t - 1)
                    for f in range(NF):
                        last = pe.matmul(ffn2[x][:, 0:C], hqt[x][:, f, :], w2q[:, f, :], start=(f == 0), stop=(f == NF - 1))
                    last.then_inc(e_y2, 1)

            skewed(pe, steps)
            pe.wait_ge(in_hw, 16)
            for n in range(8):
                if n >= 2:
                    pe.wait_ge(s_hwc, n - 1)
                bank = ps[n % 2]
                if n < 4:
                    k, g8 = n % 2, n // 2
                    rows = P if k == 0 else QR - P
                    for j in range(8):
                        hd = 8 * g8 + j
                        last = pe.matmul(bank[0:rows, j * 64:(j + 1) * 64], hw[:, hd, k * P:k * P + rows], hw[:, hd, QR:QR + 64],
                                         start=True, stop=True)
                else:
                    for j in range(2):
                        for h in range(2):
                            hd = 4 * (n - 4) + 2 * j + h
                            last = pe.matmul(bank[h * 64:(h + 1) * 64, j * C:(j + 1) * C], hw[:, hd, 256:320], hw[:, hd, 320:576],
                                             start=True, stop=True)
                last.then_inc(s_hw, 1)
            barrier(pe, 2)
            pe.wait_ge(f_wlo, 1)

            def fsteps(t, x, on):
                o = 1 - x
                if on(0):
                    pe.wait_ge(f_y, t + 1)
                    for c in range(KC):
                        last = pe.transpose(fturn[x][:, c * P:(c + 1) * P], fy[x][:, c * P:(c + 1) * P], ident[:, :])
                    last.then_inc(f_yt, 1)
                if on(1):
                    pe.wait_ge(f_qrs, t)
                    pe.wait_ge(f_ki, t)
                    pe.transpose(fout[o][:, 0:P], qrs[o][:, 0:P], ident[:, :])
                    pe.transpose(fout[o][0:QR - P, P:2 * P], qrs[o][:, P:QR], ident[:, :])
                    for j in range(2):
                        last = pe.transpose(fout[o][:, (2 + j) * P:(3 + j) * P], ki[o][:, j * P:(j + 1) * P], ident[:, :])
                    last.then_inc(f_t, 1)
                if on(0):
                    pe.wait_ge(f_lo, t + 1)
                    n = 0
                    for c in range(KC):
                        for yt, wt_ in ((fyhi, wfhi), (fylo, wfhi), (fyhi, wflo)):
                            last = pe.matmul(fproj[x][:, 0:464], yt[x][:, c, :], wt_[:, c, :], start=(n == 0), stop=(n == 5))
                            n += 1
                    last.then_inc(f_p, 1)

            skewed(pe, fsteps)
            barrier(pe, 3)
            pe.sem_inc(q_wused, 2)

            def project_q(n, x, w, first=False):
                pe.wait_ge(q_wlo, n + 1)
                if not first:
                    pe.wait_ge(q_front, n * 4 + (2 * w - 2))
                cols = slice(w * HALF, (w + 1) * HALF)
                k = 0
                for c, rows in ((0, P), (1, QR - P)):
                    for wt_, qt_ in ((wihi, qrhi), (wilo, qrhi), (wihi, qrlo)):
                        last = pe.matmul(chunk_bank[w][:, :], wt_[x][0:rows, c, :], qt_[0:rows, c, cols], start=(k == 0), stop=(k == 5))
                        k += 1
                last.then_inc(q_chunk, 1)
                if w == 1:
                    pe.drain().then_inc(q_wused, 1)

            def index_scores(n, x, s):
                pe.wait_ge(q_ready, n * 2 + (1 if s < 2 else 2))
                pe.wait_ge(i_relu, n * 4 + (s + 1))
                bank = iscore[s]
                pe.matmul(bank[:, 0:P], iq[x][:, s * T:s * T + P], ikt[:, s * T:s * T + P], start=True, stop=True)
                pe.matmul(bank[:, P:384], iq[x][:, s * T + P:(s + 1) * T], ikt[:, s * T:(s + 1) * T], start=True,
                          stop=True).then_inc(q_scores, 1)

            for w in range(2):
                project_q(0, 0, w, True)
            with pe.Fori(0, PAIRS - 1) as i:
                for h in range(2):
                    n = i * 2 + h
                    for s in range(4):
                        if s % 2 == 0:
                            project_q(n + 1, 1 - h, s // 2)
                        index_scores(n, h, s)
            for h in range(2):
                n = H - 2 + h
                for s in range(4):
                    if s % 2 == 0:
                        project_q(n + 1, 1 - h, s // 2)
                    index_scores(n, h, s)

            def scores1(u, n, x, s, first=False):
                pe.wait_ge(q_ready, n * 2 + (1 if s < 2 else 2))
                if first:
                    pe.wait_ge(a_bias, 2 * s + 2)
                bank = score_bank[s % 2]
                for q, (c0, width) in enumerate(((0, P), (P, T))):
                    pe.matmul(bank[:, c0:c0 + width], iq[x][:, s * T + q * P:s * T + (q + 1) * P], kct[:, s * T:s * T + width],
                              start=True, stop=False)
                    last = pe.matmul(bank[:, c0:c0 + width], identb[:, :], biasb[:, 2 * s + q, 0:width], start=False, stop=True)
                last.then_inc(q_scores, 1)

            for k in range(3):
                pe.wait_ge(j_abs, k + 1)
                pe.matmul(out_bank[:, 2 + k:3 + k], ones[:, :], wsum[:, 2 + k:3 + k], start=True, stop=True).then_inc(j_tot, 1)
            scores1(0, H, 0, 0, True)

            def pv1(u, h, s):
                rows = slice(h * 64, h * 64 + 64)
                bank = pv_bank[s % 2]
                pe.matmul(bank[rows, 0:T], vl[:, 2 * s, :], pt1[s % 2][:, 0:T], start=True, stop=False)
                pe.matmul(bank[rows, P:T], vl[:, 2 * s + 1, :], pt1[s % 2][:, T:384], start=False, stop=True).then_inc(a_pv, 1)

            def attention_body(i, first, last):
                for h in range(2):
                    n = i * 2 + (H + h)
                    for s in range(4):
                        u = i * 8 + (4 * h + s)
                        if s < 3:
                            scores1(u + 1, n, h, s + 1, first and h == 0)
                        elif not (last and h == 1):
                            scores1(u + 1, n + 1, 1 - h, 0)
                        pe.wait_ge(a_norm, u * 2 + 2)
                        before = not (first and h == 0 and s == 0)
                        if before:
                            pe.wait_ge(a_pt, u)
                        for c, cols in enumerate((slice(0, P), slice(P, T), slice(T, 384))):
                            t_ = pe.transpose(turn_bank[:, c * P:(c + 1) * P], p1[s % 2][:, cols], ident[:, :])
                        t_.then_inc(a_turn, 1)
                        if s < 2 and not (last and h):
                            project_q(n + 1, 1 - h, s)
                        if h == 1 and s >= 2:
                            project_out(i, s - 2)
                        if h == 0 and s < 2 and not first:
                            project_out(i - 1, s + 2)
                        if before:
                            pv1(u - 1, h if s else 1 - h, (s - 1) % 4)

            def project_out(i, w):
                pe.wait_ge(a_o, i * 8 + (4 + w + 1))
                if not (isinstance(i, int) and i == 0 and w == 0):
                    pe.wait_ge(a_x, i * 4 + w)
                for j in range(2):
                    tt = 2 * w + j
                    last = pe.matmul(out_bank[:, j * C:(j + 1) * C], ot1[:, tt * P:(tt + 1) * P], pick(wvo, i, slice(0, C)),
                                     start=True, stop=True)
                last.then_inc(a_out, 1)

            attention_body(0, True, False)
            with pe.Fori(1, PAIRS - 1) as i:
                attention_body(i, False, False)
            attention_body(PAIRS - 1, False, True)
            pe.wait_ge(a_pt, 8 * PAIRS)
            pv1(8 * PAIRS - 1, 1, 3)
            for w in (2, 3):
                project_out(PAIRS - 1, w)
            barrier(pe, 4)
            for g in range(4):
                for j in range(2):
                    pe.wait_ge(j_y, 2 * g + j + 1)
                    for c in range(KC):
                        last = pe.transpose(ps[g][:, c * T + j * P:c * T + (j + 1) * P], jy[:, 2 * g + j, c * P:(c + 1) * P], ident[:, :])
                last.then_inc(j_yt, 1)
            pe.wait_ge(j_tern, 3)
            pe.wait_ge(j_lo, 4)
            pe.sem_inc(j_down, 1)
            with pe.Fori(0, 2) as n:
                for f in range(NF):
                    if f >= 2:
                        pe.wait_ge(j_h, n * NF + (f - 1))
                    for k, bank in ((0, up_bank), (1, gate_bank)):
                        m = 0
                        for c in range(KC):
                            for yt in (yhi, ylo):
                                last = pe.matmul(bank[f % 2][:, :], wt[k][:, c * F + f * P:c * F + (f + 1) * P],
                                                 yt[:, c, bass.ds(n * HALF, HALF)], start=(m == 0), stop=(m == 3))
                                m += 1
                    last.then_inc(j_proj, 1)
                pe.wait_ge(j_hlo, n * NF + NF)
                for j in range(4):
                    if j >= 2:
                        pe.wait_ge(j_x, n * 4 + (j - 1))
                    m = 0
                    for f in range(NF):
                        for ht in (hhi, hlo):
                            last = pe.matmul(down_bank[j % 2][:, 0:C], ht[:, f, j * P:(j + 1) * P], wt[2][:, f * C:(f + 1) * C],
                                             start=(m == 0), stop=(m == 2 * NF - 1))
                            m += 1
                    last.then_inc(j_down, 1)

_P64 = np.concatenate([np.arange(0, 16), np.arange(32, 48), np.arange(16, 32), np.arange(48, 64)])
_FREQ = np.concatenate([np.arange(0, 16), np.arange(0, 16), np.arange(16, 32), np.arange(16, 32)])
_SIGN = np.concatenate([-np.ones(16), np.ones(16), -np.ones(16), np.ones(16)]).astype(np.float32)


def _angles():
    inv = (1.0 / 10000.0 ** (np.arange(0, 64, 2, dtype=np.float32) / 64)).astype(np.float32)
    f = np.arange(T, dtype=np.float32)[:, None] * inv[None, :]
    return np.cos(f).astype(np.float32), np.sin(f).astype(np.float32)


def _chan(x):
    return np.ascontiguousarray(np.asarray(x).T.reshape(2, P, -1).transpose(1, 0, 2))


def host_arrays(i):
    g = {k: np.asarray(v) for k, v in i.items()}
    r = {}
    x = g["x"].reshape(N, C)
    r["xt"], r["kt"] = _chan(x), _chan(g["fside_BxSxS_0"].reshape(N, C))
    r["xtok"] = np.ascontiguousarray(x.reshape(NT, P, C).transpose(1, 0, 2))
    names = ["L0_cond", "L0_cond2", "L1_cond", "L1_cond2"]
    r["par"] = np.ascontiguousarray(np.stack([np.stack([g[n + s].reshape(2, P) for n in names]) for s in ("_w", "_u")])
                                    .transpose(3, 0, 1, 2).reshape(P, 2, 8))
    r["cond"] = np.ascontiguousarray(np.broadcast_to(g["cond_512"][None], (P, B, 64)))
    wq, wk = g["L0_attn_Wq"], g["L0_attn_Wk"]
    heads = []
    for h in range(H):
        rows = np.concatenate([wq[h * DN:(h + 1) * DN], wk[h * DN:(h + 1) * DN],
                               wq[H * DN + h * DR:H * DN + (h + 1) * DR][_P64],
                               wk[H * DN + h * DR:H * DN + (h + 1) * DR][_P64]])
        heads.append(_chan(rows))
    r["wqk0"] = np.stack(heads)
    r["wv0"] = np.stack([_chan(g["L0_attn_Wv"][p * 256:(p + 1) * 256]) for p in range(PAIRS)])
    r["wo0"] = np.ascontiguousarray(g["L0_attn_Wo"].T.reshape(H, DN, C).transpose(1, 0, 2))
    cos, sin = _angles()
    cr, sr = cos.T[_FREQ], sin.T[_FREQ] * _SIGN[:, None]
    q8 = np.float32(DR ** -0.5)
    r["tabc0"] = np.tile(np.concatenate([cr * q8, cr]), (1, 2)).astype(np.float32)
    r["tabs0"] = np.tile(np.concatenate([sr * q8, sr]), (1, 2)).astype(np.float32)
    r["w12"] = np.stack([_chan(g["L0_ffn_w1"]).reshape(P, 2048),
                         g["L0_ffn_w2"].T.reshape(NF, P, C).transpose(1, 0, 2).reshape(P, 2048)])

    def rows(v):
        return np.ascontiguousarray(np.broadcast_to(v[None], (P,) + v.shape))

    r["b1"], r["gamma"], r["beta"], r["b2"] = (rows(g["L0_ffn_" + n]) for n in ("b1", "gamma", "beta", "b2"))
    qb = g["L1_attn_q_b_w"].reshape(H, DN + DR, QR)
    kvb = g["L1_attn_kv_b_w"].reshape(H, 2 * DN, KVR)
    ow = g["L1_attn_o_w"].T.reshape(H, DN, C)
    r["hw"] = np.ascontiguousarray(np.concatenate([qb[:, :DN], kvb[:, :DN], kvb[:, DN:], ow], axis=2).transpose(1, 0, 2))
    kva, ikw_ = g["L1_attn_kv_a_w"], g["L1_attn_idx_wk_w"]
    order = np.concatenate([np.arange(64, 128), _P64])
    r["wf"] = _chan(np.concatenate([g["L1_attn_q_a_w"], kva[:KVR], kva[KVR:][_P64], ikw_[order], g["L1_attn_idx_wproj_w"]]))
    fc = np.concatenate([np.arange(0, 16), np.arange(16, 32)])
    c4, s4 = (np.tile(v[:, fc], (1, 2)).reshape(2, P, 64).transpose(1, 0, 2) for v in (cos, sin))
    r["ropec"], r["ropes"] = np.ascontiguousarray(c4), np.ascontiguousarray(s4)
    r["ikw"], r["ikb"] = rows(g["L1_attn_idx_kn_w"][order]), rows(g["L1_attn_idx_kn_b"][order])
    r["kvw"] = rows(g["L1_attn_kv_a_ln_w"])
    iqb = g["L1_attn_idx_wq_b_w"].reshape(H, P, QR)[:, order]
    qpe = qb[:, DN:][:, _P64]

    def padded(w):
        z = np.zeros((H, 2 * P, w.shape[1]), np.float32)
        z[:, :QR] = w.transpose(0, 2, 1)
        return np.ascontiguousarray(z.reshape(H, 2, P, -1).transpose(0, 2, 1, 3))

    r["wi"], r["wq1"] = padded(iqb), padded(qpe)
    one, zero = np.ones((DR, T), np.float32), np.zeros((DR, T), np.float32)
    sc = np.float32((DN + DR) ** -0.5)
    tc, ts = np.tile(np.concatenate([one, cr]), (1, 2)), np.tile(np.concatenate([zero, sr]), (1, 2))
    r["tabc1"], r["tabs1"] = tc.astype(np.float32), ts.astype(np.float32)
    r["tabc2"], r["tabs2"] = (tc * sc).astype(np.float32), (ts * sc).astype(np.float32)
    r["w3"] = np.stack([_chan(g["L1_ffn_W_up"]).reshape(P, 2048), _chan(g["L1_ffn_W_gate"]).reshape(P, 2048),
                        g["L1_ffn_W_down"].T.reshape(NF, P, C).transpose(1, 0, 2).reshape(P, 2048)])
    ln = np.zeros(256, np.float32)
    ln[:QR] = g["L1_attn_q_a_ln_w"]
    r["lnw"] = np.ascontiguousarray(ln.reshape(2, P).T)
    return r


def kernel(**inputs):
    import concourse.bacc as bacc
    from concourse.bass_utils import run_bass_kernel_spmd

    arrays = host_arrays(inputs)
    nc = bacc.Bacc("TRN2", target_bir_lowering=False, num_devices=1)
    aps = {k: nc.dram_tensor("in_" + k, v.shape, mybir.dt.from_np(v.dtype), kind="ExternalInput").ap()
           for k, v in arrays.items()}
    out = nc.dram_tensor("out_x", (P, NT, C), F32, kind="ExternalOutput").ap()
    adaln_block(nc, aps, out)
    r = run_bass_kernel_spmd(nc, [{"in_" + k: v for k, v in arrays.items()}], core_ids=[0])
    return r.results[0]["out_x"].transpose(1, 0, 2).reshape(B, T, C)
```

```python
from contextlib import ExitStack

import numpy as np

import concourse.bass as bass
from concourse import mybir

F32 = mybir.dt.float32
F32R = mybir.dt.float32r
BF16 = mybir.dt.bfloat16
ACT = mybir.ActivationFunctionType
ALU = mybir.AluOpType
AX = mybir.AxisListType

P = 128
B, T, C = 4, 256, 256
N = B * T
NT = N // P
KC = C // P
H = 16
PAIRS = H // 2
DN, DR = 128, 64
F = 1024
NF = F // P
QR, KVR = 192, 64
TOPK = 64
HALF = N // 2
MAGIC = 12582912.0
SWAP = [p ^ 16 for p in range(32)]


class Chain:

    def __init__(self, eng, sem):
        self.eng, self.sem, self.n, self.reg, self.k = eng, sem, 0, None, 0

    def did(self, ins):
        ins.then_inc(self.sem, 1)
        self.n += 1
        return ins

    def wait(self):
        self.eng.wait_ge(self.sem, self.n if self.reg is None else self.reg * self.k + self.n)

    def step(self, ins):
        self.did(ins)
        self.wait()

    def loop(self, reg, start, k):
        self.at, self.reg, self.k, self.start = self.n, reg, k, start
        self.n -= start * k

    def close(self, rounds):
        took = self.n + self.start * self.k - self.at
        assert took == self.k, f"the body takes {took} steps"
        self.n, self.reg = self.at + rounds * self.k, None


def pick(t, at, cols):
    if isinstance(at, int):
        return t[:, at, cols]
    return t[:, bass.ds(at, 1), cols].rearrange("p a n -> p (a n)")


def adaln_block(nc, a, out):
    ctx = ExitStack()

    def sem(name):
        return ctx.enter_context(nc.semaphore(name))

    total = nc.sbuf_usable_end
    base0 = (nc.sbuf_base + 63) // 64 * 64

    class Arena:

        def __init__(self, at):
            self.at = at

        def __call__(self, name, shape, dt=F32):
            size = int(np.prod(shape[1:])) * (2 if dt == BF16 else 4)
            t = nc.alloc_sbuf_tensor_at(name, shape, dt, offset=self.at)
            self.at += (size + 31) // 32 * 32
            assert self.at <= total, (name, self.at, total)
            return t

    with ctx:
        keep = Arena(base0)
        gtok = keep("gtok", [P, 3 * KC, NT, P])
        xtok = keep("xtok", [P, NT, C])
        yhi = keep("yhi", [P, KC, N], F32R)
        ylo = keep("ylo", [P, KC, N], F32R)
        ident = keep("ident", [P, P])
        identb = keep("identb", [P, P], BF16)
        par = keep("par", [P, 2, 4 * KC])
        decay = keep("decay", [P, 4 * KC, B])
        tf = keep("tf", [P, B])
        dfac = keep("dfac", [P, B])
        gate = keep("gate", [P, B])
        ew = keep("ew", [P, 4 * KC])
        w1q = keep("w1q", [P, KC, F], BF16)
        w2q = keep("w2q", [P, NF, C], BF16)
        wsum = keep("wsum", [P, 8])
        wmean = keep("wmean", [P, 8])
        wrec = keep("wrec", [P, 8])
        half = keep("half", [P, 4])
        clipc = keep("clipc", [P, 2])

        m = Arena(keep.at)
        tabc = m("tabc", [P, HALF])
        tabs = m("tabs", [P, HALF])
        kt = m("kt", [P, KC, N])
        ek = m("ek", [P, KC, N])
        ekv = m("ekv", [P, KC, N])
        gbuf = [m(n, [P, HALF]) for n in ("nf", "nb", "df", "db", "euk", "dd")]
        nb, db = gbuf[1], gbuf[3]
        gg = m("gg", [P, HALF])
        wst, whi, wlo = ([m(f"{n}{x}", [P, KC, 384], F32 if n == "wst" else F32R) for x in range(2)]
                         for n in ("wst", "whi", "wlo"))
        wvst = m("wvst", [P, KC, 256])
        wvhi = m("wvhi", [P, KC, 256], F32R)
        wvlo = m("wvlo", [P, KC, 256], F32R)
        wo = m("wo", [P, H, C])
        at = m.at
        qn, kn = ([None, m(f"{n}1", [P, N])] for n in ("qn", "kn"))
        qr, kr = ([None, m(f"{n}1", [P, N], F32R)] for n in ("qr", "kr"))
        ot = m("ot", [P, 2, N])
        pt = [m(f"pt{x}", [P, 2, T]) for x in range(2)]
        at_end = m.at
        for n, t, dt in (("qn", qn, F32), ("kn", kn, F32), ("qr", qr, F32R), ("kr", kr, F32R)):
            t[0] = m(f"{n}0", [P, N], dt)
        rlow = m("rlow", [P, N], F32R)
        condb = Arena(m.at)("condb", [P, B, 64])
        v = m("v", [P, NT, 256])
        pr = [m(f"pr{x}", [P, 2, T]) for x in range(2)]
        rt1 = [m(f"rt{x}", [P, HALF]) for x in range(2)]
        rsh = [m(f"rsh{x}", [P, HALF]) for x in range(2)]
        negm = [m(f"negm{x}", [P, 2]) for x in range(2)]
        sums = [m(f"sums{x}", [P, 2]) for x in range(2)]
        rsum = [m(f"rsum{x}", [P, 2]) for x in range(2)]
        pre = Arena(at)
        xt = pre("xt", [P, KC, N])
        y32 = pre("y32", [P, KC, N])
        gbuf2 = [pre(n + "2", [P, HALF]) for n in ("nf", "nb", "df", "db", "euk", "dd")]
        assert pre.at <= at_end

        def gate_buffers(gu, prologue=False):
            return gbuf2 if prologue and gu % 2 else gbuf

        R0 = keep.at
        e = Arena(R0 + 4096)
        wtern = [e(f"wtern{x}", [P, 2048]) for x in range(2)]
        wround = e("wround", [P, 2048])
        b1b, gamb, betb = (e(n, [P, F]) for n in ("b1b", "gamb", "betb"))
        b2b = e("b2b", [P, C])
        ones0 = e("ones0", [P, P])
        assert e.at <= R0 + 42 * 1024
        k2 = Arena(R0 + 42 * 1024)
        kct = k2("kct", [P, N])
        ikt = k2("ikt", [P, N])
        vl = k2("vl", [P, NT, KVR])
        iw = k2("iw", [P, NT, H])
        wabs = k2("wabs", [P, 2, H * KVR])
        wvo = k2("wvo", [P, PAIRS, C])
        at2 = k2.at
        hw = Arena(at2)("hw", [P, H, 576])
        q2 = Arena(at2)
        qrhi = q2("qrhi", [P, 2, N], F32R)
        qrlo = q2("qrlo", [P, 2, N], F32R)
        e = Arena(hw_end := at2 + H * 576 * 4)
        sga = e("sga", [P, NT, C])
        y = [e(f"y{x}", [P, C]) for x in range(2)]
        yq = [e(f"yq{x}", [P, C], BF16) for x in range(2)]
        yqt = [e(f"yqt{x}", [P, KC, P], BF16) for x in range(2)]
        hb = [e(f"hb{x}", [P, F]) for x in range(2)]
        hq = [e(f"hq{x}", [P, F], BF16) for x in range(2)]
        hqt = [e(f"hqt{x}", [P, NF, P], BF16) for x in range(2)]
        xb = [e(f"xb{x}", [P, C]) for x in range(2)]
        sm = [e(f"sm{x}", [P, 64]) for x in range(4)]
        e = Arena(hw_end)
        wfst = Arena(R0)("wfst", [P, KC, 464])
        f_ = Arena(R0 + 4096)
        wfhi = f_("wfhi", [P, KC, 464], F32R)
        wflo = f_("wflo", [P, KC, 464], F32R)
        ropec, ropes = (f_(n, [P, 2, DR]) for n in ("ropec", "ropes"))
        ikw, ikb = (f_(n, [P, P]) for n in ("ikw", "ikb"))
        kvw = f_("kvw", [P, KVR])
        lnw = f_("lnw", [P, 2])
        fy = [f_(f"fy{x}", [P, C]) for x in range(2)]
        fsg = [f_(f"fsg{x}", [P, C]) for x in range(2)]
        fyhi = [f_(f"fyhi{x}", [P, KC, P], F32R) for x in range(2)]
        fylo = [f_(f"fylo{x}", [P, KC, P], F32R) for x in range(2)]
        junk = f_("junk", [P, 256])
        fp = [f_(f"fp{x}", [P, 464]) for x in range(2)]
        ki = [f_(f"ki{x}", [P, 256]) for x in range(2)]
        qrs = [f_(f"qrs{x}", [P, QR]) for x in range(2)]
        rp = f_("rp", [P, 4, DR])
        fs = [f_(f"fs{x}", [P, 32]) for x in range(2)]
        assert f_.at <= R0 + 32 * 1024, f_.at - R0

        i1 = Arena(R0 + 32 * 1024)
        tabc1, tabs1 = (i1(n, [P, HALF]) for n in ("tabc1", "tabs1"))
        wi = [i1(f"wi{x}", [P, 2, P]) for x in range(2)]
        wihi = [i1(f"wihi{x}", [P, 2, P], F32R) for x in range(2)]
        wilo = [i1(f"wilo{x}", [P, 2, P], F32R) for x in range(2)]
        assert i1.at <= R0 + 42 * 1024, i1.at - R0
        i1 = Arena(R0)
        tabc2, tabs2 = (i1(n, [P, HALF]) for n in ("tabc2", "tabs2"))
        it1 = [i1(f"it{x}", [P, HALF]) for x in range(2)]
        ish = [i1(f"ish{x}", [P, HALF]) for x in range(2)]
        acc = i1("acc", [P, NT, T])
        ust = i1("ust", [P, 2048])
        assert i1.at <= R0 + 32 * 1024, i1.at - R0
        i2 = Arena(q2.at)
        iq = [i2(f"iq{x}", [P, N]) for x in range(2)]
        rl = [i2(f"rl{x}", [P, 384]) for x in range(4)]
        top8 = i2("top8", [P, NT, 8])
        biasb = i2("biasb", [P, NT, T], BF16)
        causb = i2("causb", [P, 2, T], BF16)
        p1 = [i2(f"p1{x}", [P, 384]) for x in range(2)]
        pt1 = [i2(f"pt1{x}", [P, 384]) for x in range(2)]
        ot1 = i2("ot1", [P, N])
        negm1 = [i2(f"negm1{x}", [P, 2]) for x in range(2)]
        sums1 = [i2(f"sums1{x}", [P, 2]) for x in range(2)]
        rsum1 = [i2(f"rsum1{x}", [P, 2]) for x in range(2)]
        wt = [i2(f"wt{k}", [P, 2048], F32R) for k in range(3)]
        uround = i2("uround", [P, 2048])
        ones1 = i2("ones1", [P, P])

        j1 = Arena(R0)
        jsg = j1("jsg", [P, NT, C])
        jy = j1("jy", [P, NT, C])
        silu = [j1(f"silu{x}", [P, HALF]) for x in range(2)]
        h32 = [j1(f"h32{x}", [P, HALF]) for x in range(2)]
        xo = [j1(f"xo{x}", [P, 2 * C]) for x in range(2)]
        j2 = Arena(R0 + 48 * 1024)
        hhi = j2("hhi", [P, NF, HALF], F32R)
        hlo = j2("hlo", [P, NF, HALF], F32R)
        assert j2.at <= i2.at - 4 * 8192 - 512 and j1.at <= R0 + 48 * 1024

        ps = [ctx.enter_context(nc.psum_tensor(f"ps{i}", [P, 512], F32)) for i in range(8)]
        chunk_bank, score_bank, turn_bank, pv_bank = ps[0:2], ps[2:4], ps[4], ps[5:7]

        iscore = ps[2:6]
        out_bank = ps[7]
        up_bank, gate_bank, down_bank = ps[0:2], ps[2:4], ps[4:6]
        qturn = [ps[x][:, 0:C // 2].bitcast(BF16) for x in range(2)]
        turn2 = ps[2][:, :].bitcast(BF16)
        ffn1 = [[ps[3], ps[4]], [ps[5], ps[6]]]
        ffn2 = [ps[7], ps[7]]
        fturn, fproj, fout = ps[0:2], ps[2:4], ps[4:6]

        in_k, in_x, in_par, in_tab, in_wo = (sem("in_" + n) for n in ("k", "x", "par", "tab", "wo"))
        in_w = [sem(f"in_w{x}") for x in range(2)]
        in_wv = sem("in_wv")
        dch, ach = sem("vector_steps"), sem("scalar_steps")
        pch = sem("pool_steps")
        s_kmin, s_ukmin = sem("min_k_ready"), sem("min_uk_ready")
        s_const, s_ek, s_decay, s_tf = (sem(n) for n in ("constants_ready", "ek_ready", "decay_ready", "tf_steps"))
        s_euk, s_scan, s_dd, s_sums, s_gg = (sem(n) for n in (
            "euk_ready", "scans_ready", "dd_ready", "gate_sums_ready", "gg_ready"))
        s_sig, s_y, s_yhi, s_ylo = (sem(n) for n in ("sig_x_ready", "y_ready", "yhi_ready", "ylo_ready"))
        s_whi, s_wlo = sem("w_upper_ready"), sem("w_lower_ready")
        s_wvhi, s_wvlo = sem("wv_upper_ready"), sem("wv_lower_ready")
        s_chunk, s_free = sem("chunk_ready"), [sem(f"chunk_bank{x}_free") for x in range(2)]
        s_qk, s_rope, s_v = sem("qk_ready"), sem("rope_ready"), sem("v_ready")
        s_shuf, s_t2 = sem("rope_swapped"), sem("rope_sin_ready")
        s_scores, s_negmax, s_exp, s_norm = (sem(n) for n in ("scores_ready", "negmax_ready", "exp_ready", "probs_ready"))
        s_turn, s_pt, s_pv, s_o = (sem(n) for n in ("probs_turned", "pt_ready", "pv_ready", "o_ready"))
        s_x1 = sem("x1_added")
        s_out_chunk = sem("output_chunk_ready")
        s_rsum, s_rhi, s_ones = sem("rope_summed"), sem("rope_upper"), sem("ones_ready")
        s_gtok = sem("gtok_ready")
        s_rev = sem("backward_sources_copied")
        s_out = sem("stored")
        s_pause = sem("pause")
        phase = sem("phase_done")
        in_e, in_hw, in_f, in_i, in_i2 = (sem("in_" + n) for n in ("e", "hw", "f", "i", "i2"))
        in_t0 = [sem(f"in_tern{k}") for k in range(2)]
        s_abs, s_tot, s_wscale, s_round, s_tern = (sem(n) for n in (
            "weight_abs", "weight_total", "weight_scale", "weight_rounded", "weight_ternary"))
        e_sig, e_scale, e_qm, e_q, e_qt, e_qtc, e_h, e_hb, e_gelu, e_ve, e_rstd, e_nm, e_z, e_beta = (sem("e_" + n) for n in (
            "sig", "scale", "scaled", "quant", "turned", "turned_copied", "h", "h_biased", "gelu", "variance", "rstd",
            "mean_rstd", "normed", "affine"))
        e_scale2, e_qm2, e_q2, e_qt2, e_qtc2, e_y2, e_xb, e_x2 = (sem("e2_" + n) for n in (
            "scale", "scaled", "quant", "turned", "turned_copied", "y", "xb", "x2"))
        s_hw, s_hwc = sem("latent_products"), sem("latent_products_copied")
        f_w, f_wlo, f_sig, f_y, f_yt, f_hi, f_lo, f_p, f_sq, f_bn, f_rstd, f_qrs, f_ki, f_vl, f_t, f_hi2, f_pc, f_free = (sem("f_" + n) for n in (
            "w_upper", "w_lower", "sig", "y", "y_turned", "y_upper", "y_lower", "projected", "squares", "variance", "rstd",
            "qr_scaled", "keys", "latents", "turned", "qr_upper", "projected_copied", "act_copies"))

        in_q = [sem(f"in_q{x}") for x in range(2)]
        q_abs, q_whi, q_wlo, q_chunk, q_front, q_ready, q_scores = (sem("q_" + n) for n in (
            "absorbed_staged", "w_upper", "w_lower", "projected", "rope_front", "ready", "scores"))
        i_init, i_relu, i_acc, a_bias = sem("i_acc_initial"), sem("i_relu"), sem("i_accumulated"), sem("a_bias_ready")
        a_negmax, a_exp, a_norm, a_turn, a_pt, a_pv, a_o, a_out, a_x = (sem("a_" + n) for n in (
            "negmax", "exp", "probs", "turned", "pt", "pv", "o", "out", "x3"))
        in_u = sem("in_u")
        j_clip = sem("j_clipped")
        j_abs, j_tot, j_scale, j_round, j_tern = (sem("j_" + n) for n in ("abs", "total", "scale", "rounded", "ternary"))
        j_sig, j_y, j_yt, j_hi, j_lo, j_proj, j_silu, j_h, j_hhi, j_hlo, j_down, j_x = (sem("j_" + n) for n in (
            "sig", "y", "y_turned", "y_upper", "y_lower", "projected", "silu", "h", "h_upper", "h_lower", "down", "x"))
        j_out = [sem(f"j_stored{x}") for x in range(2)]

        block = ctx.enter_context(nc.Block())

        def barrier(eng, k):
            eng.drain().then_inc(phase, 1)
            eng.wait_ge(phase, 5 * k)

        LAST_OUT = {2: ps[0], 3: ps[1]}
        yturn = [ps[0], ps[1], ps[6], ps[7]]

        LATENT = {2: (0,), 3: (1,), NT: (2, 3, 4, 5), NT + 1: (6, 7)}

        def skewed(eng, body, chain=None, k=0):
            for t in range(4):
                body(t, t % 2, lambda d, t=t: 0 <= t - d < NT)
            with eng.Fori(2, 4) as i:
                if chain:
                    chain.loop(i, 2, k)
                for x in range(2):
                    body(i * 2 + x, x, lambda d: True)
                if chain:
                    chain.close(2)
            for t in range(NT, NT + 3):
                body(t, t % 2, lambda d, t=t: 0 <= t - d < NT)

        def chunks(g, last):
            qk = [[("r", 0), ("r", 1)], [("q", 0), ("k", 0)], [("q", 1), ("k", 1)], []]
            gc = [("g", 0)] if g else []
            first = [list(x) for x in qk]
            first[3] += gc
            second = [list(x) if not last else [] for x in qk]
            second[3] += gc
            for s in range(1, 4):
                second[s].append(("o", s - 1))
            tail = [[] if last else [("v", s)] for s in range(4)]
            tail[3].append(("o", 3))
            return [(first, [[]] * 4), (second, tail)]

        def numbered(g, last):
            n, places = 0, {}
            for h, (front, tail) in enumerate(chunks(g, last)):
                for s in range(4):
                    for kind, w in front[s] + tail[s]:
                        if kind != "o":
                            places[h, kind, w] = n
                            n += 1
            return places, n

        PG, NG = numbered(True, False)
        P6, N6 = numbered(False, False)
        P7, N7 = numbered(False, True)
        FIRST_CHUNKS = (("r", 0), ("q", 0), ("k", 0), ("v", 0), ("v", 1), ("r", 1), ("q", 1), ("k", 1), ("v", 2), ("v", 3))
        FIRST = len(FIRST_CHUNKS)
        NGATED = 6
        assert NG % 2 == 0 and N6 % 2 == 0 and FIRST % 2 == 0

        def chunk_at(i, h, kind, w):
            if not isinstance(i, int):
                return i * NG + (FIRST + PG[h, kind, w])
            if i < NGATED:
                return FIRST + i * NG + PG[h, kind, w]
            return FIRST + NGATED * NG + ((P6[h, kind, w]) if i == 6 else N6 + P7[h, kind, w])

        def bank_at(i, h, kind, w):
            return (PG if not isinstance(i, int) or i < NGATED else P6 if i == 6 else P7)[h, kind, w] % 2

        def uses_at(i, h, kind, w):
            if not isinstance(i, int):
                return i * (NG // 2) + (FIRST + PG[h, kind, w]) // 2
            return chunk_at(i, h, kind, w) // 2

        def pairs(eng, body, chain=None, k=0):
            with eng.Fori(0, NGATED) as i:
                if chain:
                    chain.loop(i, 0, k)
                body(i, True, False)
                if chain:
                    chain.close(NGATED)
            body(6, False, False)
            body(7, False, True)

        @block.sync
        def _(sp):
            sp.dma_start(par[:, :, :], a["par"]).then_inc(in_par, 16)
            sp.dma_start(condb[:, :, :], a["cond"]).then_inc(in_par, 16)
            sp.dma_start(kt[:, :, :], a["kt"]).then_inc(in_k, 16)
            sp.dma_start(xt[:, :, :], a["xt"]).then_inc(in_x, 16)
            for x in range(2):
                sp.dma_start(wst[x][:, :, :], a["wqk0"][x]).then_inc(in_w[x], 16)
            sp.dma_start(wvst[:, :, :], a["wv0"][0]).then_inc(in_wv, 16)
            sp.dma_start(tabc[:, :], a["tabc0"]).then_inc(in_tab, 16)
            sp.dma_start(tabs[:, :], a["tabs0"]).then_inc(in_tab, 16)
            sp.dma_start(wo[:, :, :], a["wo0"]).then_inc(in_wo, 16)
            sp.dma_start(xtok[:, :, :], a["xtok"]).then_inc(in_wo, 16)
            with sp.Fori(0, PAIRS - 1) as i:
                sp.wait_ge(s_whi, i * 2 + 1)
                sp.wait_ge(s_wlo, i * 2 + 1)
                sp.dma_start(wst[0][:, :, :], a["wqk0"][bass.ds(i * 2 + 2, 1), :, :, :].rearrange("a p k n -> (a p) k n")).then_inc(in_w[0], 16)
                sp.wait_ge(s_wvhi, i + 1)
                sp.wait_ge(s_wvlo, i + 1)
                sp.dma_start(wvst[:, :, :], a["wv0"][bass.ds(i + 1, 1), :, :, :].rearrange("a p k n -> (a p) k n")).then_inc(in_wv, 16)
                sp.wait_ge(s_whi, i * 2 + 2)
                sp.wait_ge(s_wlo, i * 2 + 2)
                sp.dma_start(wst[1][:, :, :], a["wqk0"][bass.ds(i * 2 + 3, 1), :, :, :].rearrange("a p k n -> (a p) k n")).then_inc(in_w[1], 16)
            sp.wait_ge(s_gtok, 2 * NGATED + 1)
            sp.wait_ge(s_rev, 2 * NGATED + 1)
            for k in range(2):
                sp.dma_start(wtern[k][:, :], a["w12"][k]).then_inc(in_t0[k], 16)
            for t, n in ((b1b, "b1"), (gamb, "gamma"), (betb, "beta"), (b2b, "b2")):
                sp.dma_start(t[:, :], a[n]).then_inc(in_e, 16)
            barrier(sp, 1)
            sp.dma_start(wfst[:, :, :], a["wf"]).then_inc(in_f, 16)
            for t, n in ((ropec, "ropec"), (ropes, "ropes")):
                sp.dma_start(t[:, :, :], a[n]).then_inc(in_f, 16)
            for t, n in ((ikw, "ikw"), (ikb, "ikb"), (kvw, "kvw"), (lnw, "lnw")):
                sp.dma_start(t[:, :], a[n]).then_inc(in_f, 16)
            sp.dma_start(hw[:, :, :], a["hw"]).then_inc(in_hw, 16)
            barrier(sp, 2)
            for t, n in ((tabc1, "tabc1"), (tabs1, "tabs1")):
                sp.dma_start(t[:, :], a[n]).then_inc(in_i, 16)
            for x in range(2):
                sp.dma_start(wi[x][:, :, :], a["wi"][x]).then_inc(in_q[x], 16)
            barrier(sp, 3)
            for t, n in ((tabc2, "tabc2"), (tabs2, "tabs2")):
                sp.dma_start(t[:, :], a[n]).then_inc(in_i2, 16)
            sp.dma_start(ust[:, :], a["w3"][0]).then_inc(in_u, 16)
            with sp.Fori(0, PAIRS - 1) as i:
                for x in range(2):
                    sp.wait_ge(q_wlo, i * 2 + (x + 1))
                    sp.dma_start(wi[x][:, :, :], a["wi"][bass.ds(i * 2 + (2 + x), 1), :, :, :].rearrange("a p k n -> (a p) k n")).then_inc(in_q[x], 16)
            def attention_weights(i):
                for x in range(2):
                    sp.wait_ge(q_wlo, i * 2 + (H - 1 + x))
                    src = a["wq1"][i * 2 + x] if isinstance(i, int) else a["wq1"][bass.ds(i * 2 + x, 1), :, :, :].rearrange("a p k n -> (a p) k n")
                    sp.dma_start(wi[x][:, :, KVR:P], src).then_inc(in_q[x], 16)

            attention_weights(0)
            for k in range(1, 3):
                sp.wait_ge(j_round, k)
                sp.dma_start(ust[:, :], a["w3"][k]).then_inc(in_u, 16)
            with sp.Fori(1, PAIRS) as i:
                attention_weights(i)
            barrier(sp, 4)
            for x in range(2):
                sp.sem_inc(j_out[x], 16)
            with sp.Fori(0, 2) as n:
                for x in range(2):
                    sp.wait_ge(j_x, n * 2 + (x + 2))
                    sp.dma_start(out[:, bass.ds(n * 4 + 2 * x, 2), :], xo[x][:, :].rearrange("p (t c) -> p t c", t=2)).then_inc(j_out[x], 16)
            for x in range(2):
                sp.wait_ge(j_out[x], 16 + 16 * NT // 4)

        @block.gpsimd
        def _(gp):
            ch = Chain(gp, pch)
            for t, val in ((ident, 0.0), (identb, 0.0), (half, -0.5)):
                ch.did(gp.memset(t[:, :], val))
            ch.did(gp.memset(clipc[:, 0:1], 1.0 - MAGIC))
            ch.did(gp.memset(clipc[:, 1:2], 2.0))
            ch.wait()
            for t in (ident, identb):
                gp.affine_select(out=t[:, :], in_=t[:, :], compare_op=ALU.not_equal, fill=1.0, base=0,
                                 pattern=[[-1, P]], channel_multiplier=1).then_inc(s_const, 1)

            def gate_sums(gu, kcols, prologue=False):
                nf, nb, df, db, euk, dd = gate_buffers(gu, prologue)
                for j in range(2):
                    gp.wait_ge(s_scan, gu * 2 + (j + 1))
                    cols = slice(j * T, (j + 1) * T)
                    ch.did(gp.tensor_tensor(nf[:, cols], nf[:, cols], nb[:, cols], ALU.add))
                    ch.did(gp.tensor_tensor(df[:, cols], df[:, cols], db[:, cols], ALU.add))
                gp.wait_ge(s_dd, gu + 1)
                ch.wait()
                ch.step(gp.tensor_tensor(nb[:, :], dd[:, :], kcols, ALU.mult))
                ch.did(gp.tensor_tensor(nf[:, :], nf[:, :], nb[:, :], ALU.add))
                gp.tensor_tensor(df[:, :], df[:, :], dd[:, :], ALU.add).then_inc(s_sums, 1)

            def split_w(x, hd):
                gp.wait_ge(s_whi, hd + 1)
                gp.tensor_tensor(wlo[x][:, :, :], wst[x][:, :, :], whi[x][:, :, :].bitcast(F32), ALU.subtract).then_inc(s_wlo, 1)

            def split_wv(i):
                gp.wait_ge(s_wvhi, i + 1)
                gp.tensor_tensor(wvlo[:, :, :], wvst[:, :, :], wvhi[:, :, :].bitcast(F32), ALU.subtract).then_inc(s_wvlo, 1)

            def rope_sin(rn):
                for w in range(2):
                    gp.wait_ge(s_shuf, rn + w + 1)
                    gp.tensor_tensor(rsh[w][:, :], rsh[w][:, :], tabs[:, :], ALU.mult).then_inc(s_t2, 1)

            gp.wait_ge(in_k, 16)
            for gu in range(2 * KC):
                bh, c = divmod(gu, KC)
                gate_sums(gu, kt[:, c, bh * HALF:(bh + 1) * HALF], True)
                if gu == 0:
                    split_w(0, 0)
                    split_wv(0)
            gp.wait_ge(in_tab, 32)
            rope_sin(0)
            split_w(1, 1)

            def body(i, g, last):
                if last:
                    gp.wait_ge(s_gtok, 2 * NGATED + 1)
                    gp.memset(ones0[:, :], 1.0).then_inc(s_ones, 1)
                rope_sin(i * 4 + 2)
                if g:
                    gate_sums(i * 2 + 4, pick(kt, i % 2, slice(0, HALF)))
                if not last:
                    split_w(0, i * 2 + 2)
                    split_wv(i + 1)
                    rope_sin(i * 4 + 4)
                if g:
                    gate_sums(i * 2 + 5, pick(kt, i % 2, slice(HALF, N)))
                if not last:
                    split_w(1, i * 2 + 3)

            pairs(gp, body, ch, 12)
            barrier(gp, 1)
            ch.step(gp.memset(wabs[QR - P:P, 1, :], 0.0))
            gp.wait_ge(in_e, 64)

            def steps(t, x, on):
                if on(1):
                    gp.wait_ge(e_ve, t)
                    gp.tensor_tensor(sm[1 - x][:, 9:10], sm[1 - x][:, 8:9], half[:, 0:1], ALU.pow).then_inc(e_rstd, 1)
                if on(2):
                    gp.tensor_tensor(xb[x][:, :], pick(xtok, t - 2, slice(0, C)), b2b[:, :], ALU.add).then_inc(e_xb, 1)
                if on(1):
                    gp.wait_ge(e_z, t)
                    ch.step(gp.tensor_tensor(hb[1 - x][:, :], hb[1 - x][:, :], gamb[:, :], ALU.mult))
                    gp.tensor_tensor(hb[1 - x][:, :], hb[1 - x][:, :], betb[:, :], ALU.add).then_inc(e_beta, 1)

            skewed(gp, steps, ch, 2)
            gp.wait_ge(f_w, 1)
            gp.tensor_tensor(wflo[:, :, :], wfst[:, :, :], wfhi[:, :, :].bitcast(F32), ALU.subtract).then_inc(f_wlo, 1)
            barrier(gp, 2)
            ch.step(gp.memset(causb[:, :, :], 0.0))
            for qt in range(2):
                gp.affine_select(out=causb[:, qt, :], in_=causb[:, qt, :], compare_op=ALU.is_ge, fill=-1e9, base=qt * P,
                                 pattern=[[-1, T]], channel_multiplier=1).then_inc(i_init, 1)
            gp.memset(ones1[:, :], 1.0).then_inc(s_ones, 1)

            def fsteps(t, x, on):
                if on(1):
                    gp.wait_ge(f_bn, t)
                    gp.tensor_tensor(fs[1 - x][:, 12:15], fs[1 - x][:, 8:11], half[:, 0:3], ALU.pow).then_inc(f_rstd, 1)

            skewed(gp, fsteps)

            def split_q(n, x):
                gp.wait_ge(q_whi, n + 1)
                gp.tensor_tensor(wilo[x][:, :, :], wi[x][:, :, :], wihi[x][:, :, :].bitcast(F32), ALU.subtract).then_inc(q_wlo, 1)

            split_q(0, 0)
            split_q(1, 1)
            barrier(gp, 3)
            ch.step(gp.memset(acc[:, :, :], 0.0))
            for qt in range(2):
                gp.affine_select(out=acc[:, qt::2, :], in_=acc[:, qt::2, :], compare_op=ALU.is_ge, fill=-3e38, base=qt * P,
                                 pattern=[[0, B], [-1, T]], channel_multiplier=1).then_inc(i_init, 1)

            def rope_q(n, x, w, tab, first=False):
                gp.wait_ge(q_front, (n * 4) + (2 * w + 2))
                ch.step(gp.tensor_tensor(ish[w][:, :], ish[w][:, :], tab[:, :], ALU.mult))
                if not first:
                    gp.wait_ge(q_scores, (n * 4) - 3)
                gp.tensor_tensor(iq[x][:, w * HALF:(w + 1) * HALF], ish[w][:, :], it1[w][:, :], ALU.add).then_inc(q_ready, 1)

            gp.wait_ge(in_i, 32)
            for w in range(2):
                rope_q(0, 0, w, tabs1, True)

            def heads(base, tab, i, last):
                for h in range(2):
                    n = i * 2 + (base + h)
                    if base == 0:
                        split_q(n + 2, h)
                    if not (last and h):
                        for w in range(2):
                            rope_q(n + 1, 1 - h, w, tab)
                    if base and not last:
                        split_q(n + 2, h)

            with gp.Fori(0, PAIRS - 1) as i:
                ch.loop(i, 0, 4)
                heads(0, tabs1, i, False)
                ch.close(PAIRS - 1)
            for w in range(2):
                rope_q(H - 1, 1, w, tabs1)
            split_q(H, 0)
            split_q(H + 1, 1)
            gp.wait_ge(in_i2, 32)
            for w in range(2):
                rope_q(H, 0, w, tabs2)
            for k in range(3):
                gp.wait_ge(j_clip, 2 * k + 2)
                gp.tensor_scalar(wt[k][:, :], uround[:, :], -1.0, 1.0, ALU.mult, ALU.add).then_inc(j_tern, 1)
            with gp.Fori(0, PAIRS - 1) as i:
                ch.loop(i, 0, 4)
                heads(H, tabs2, i, False)
                ch.close(PAIRS - 1)
            heads(H, tabs2, PAIRS - 1, True)
            gp.drain().then_inc(phase, 1)

        @block.scalar
        def _(act):
            act.wait_ge(in_par, 32)
            act.activation(ew[:, :], par[:, 0, :], ACT.Exp).then_inc(ach, 1)
            act.wait_ge(ach, 1)
            act.activation(ew[:, :], ew[:, :], ACT.Exp, scale=-1.0).then_inc(s_decay, 1)
            act.wait_ge(s_tf, 1)
            act.activation(tf[:, :], tf[:, :], ACT.Exp, scale=-1.0).then_inc(s_tf, 1)
            for c in range(KC):
                act.wait_ge(s_kmin, c + 1)
                act.activation(ek[:, c, :], ek[:, c, :], ACT.Exp).then_inc(s_ek, 1)

            def gate_exp(gu, prologue=False):
                euk = gate_buffers(gu, prologue)[4]
                act.wait_ge(s_ukmin, gu + 1)
                act.activation(euk[:, :], euk[:, :], ACT.Exp).then_inc(s_euk, 1)

            def split_w(x, hd):
                act.wait_ge(in_w[x], (hd - x) * 8 + 16)
                act.activation(whi[x][:, :, :], wst[x][:, :, :], ACT.Copy).then_inc(s_whi, 1)

            def split_wv(i):
                act.wait_ge(in_wv, i * 16 + 16)
                act.activation(wvhi[:, :, :], wvst[:, :, :], ACT.Copy).then_inc(s_wvhi, 1)

            def copy_chunk(g, bank, dst, done, scale=1.0, src=None):
                act.wait_ge(s_chunk, g + 1)
                src = chunk_bank[bank][:, :] if src is None else src
                act.activation(dst, src, ACT.Copy, scale=scale).then_inc(done, 1)
                act.drain().then_inc(s_free[bank], 1)

            QS = DN ** -0.5

            def qkv_chunk(g, bank, x, kind, w):
                if kind == "q":
                    copy_chunk(g, bank, qn[x][:, w * HALF:(w + 1) * HALF], s_qk, QS)
                elif kind == "k":
                    copy_chunk(g, bank, kn[x][:, w * HALF:(w + 1) * HALF], s_qk)
                else:
                    copy_chunk(g, bank, v[:, 2 * w:2 * w + 2, :].rearrange("p a b -> p (a b)"), s_v)

            def rope_upper(rn, x, w):
                act.wait_ge(s_rsum, rn + w + 1)
                s = slice(w * HALF, (w + 1) * HALF)
                lo, hi = slice(0, DR), slice(DR, P)
                act.activation(qr[x][lo, s], rt1[w][lo, :], ACT.Copy)
                act.activation(kr[x][hi, s], rt1[w][hi, :], ACT.Copy)
                if x == 0:
                    act.activation(qr[x][hi, s], rt1[w][lo, :], ACT.Copy)
                else:
                    act.activation(kr[x][lo, s], rt1[w][hi, :], ACT.Copy)
                act.drain().then_inc(s_rhi, 1)

            def exps(u, par_):
                act.wait_ge(s_negmax, u + 1)
                for q in range(2):
                    last = act.activation(pr[par_][:, q, :], score_bank[par_][:, q * T:(q + 1) * T], ACT.Exp,
                                          bias=negm[par_][:, q:q + 1], accum_out=sums[par_][:, q:q + 1])
                last.then_inc(s_exp, 1)

            def upper_y(gu):
                bh, c = divmod(gu, KC)
                cols = slice(bh * HALF, (bh + 1) * HALF)
                act.wait_ge(s_y, gu + 1)
                act.activation(yhi[:, c, cols], y32[:, c, cols], ACT.Copy).then_inc(s_yhi, 1)

            def first_chunk(n):
                kind, w = FIRST_CHUNKS[n]
                if kind != "r":
                    qkv_chunk(n, n % 2, 0, kind, w)

            gate_exp(0, True)
            act.sem_inc(s_pt, 1)
            split_w(0, 0)
            split_wv(0)
            gate_exp(1, True)
            act.wait_ge(in_x, 16)
            act.activation(xt[:, :, :], xt[:, :, :], ACT.Sigmoid).then_inc(s_sig, 1)
            upper_y(0)
            gate_exp(2, True)
            upper_y(1)
            gate_exp(3, True)
            for n in range(3):
                first_chunk(n)
            upper_y(2)
            first_chunk(3)
            first_chunk(4)
            upper_y(3)
            split_w(1, 1)
            rope_upper(0, 0, 0)
            for n in range(5, FIRST):
                first_chunk(n)
                if n == 7:
                    rope_upper(0, 0, 1)
                    exps(0, 0)

            def gate_copy(gu, ci, bh):
                act.wait_ge(s_sums, gu)
                for src, r in ((ekv, nb), (ek, db)):
                    act.activation(r[:, :], pick(src, ci, slice(bh * HALF, (bh + 1) * HALF)), ACT.Copy)
                act.drain().then_inc(s_rev, 1)

            gate_copy(4, 0, 0)

            def evict(i, h, kind, w):
                if kind in "ro":
                    return
                gi, bank = chunk_at(i, h, kind, w), bank_at(i, h, kind, w)
                if kind in "qk":
                    qkv_chunk(gi, bank, 1 - h, kind, w)
                elif kind == "v":
                    qkv_chunk(gi, bank, 0, kind, w)
                elif kind == "g":
                    dst = gtok[:, bass.ds(i, 1), 4 * h:4 * h + 4, :].rearrange("p l t n -> p (l t) n")
                    copy_chunk(gi, bank, dst, s_gtok, src=chunk_bank[bank][:, :].rearrange("p (t n) -> p t n", t=4))

            def ternary_abs(k):
                act.wait_ge(in_t0[k], 16)
                if k:
                    act.wait_ge(s_abs, k)
                act.activation(wround[:, :], wtern[k][:, :], ACT.Abs, accum_out=wsum[:, k:k + 1]).then_inc(s_abs, 1)

            def ternary_round(k):
                act.wait_ge(s_wscale, k + 1)
                act.wait_ge(s_abs, 2)
                if k:
                    act.wait_ge(s_tern, k)
                act.activation(wround[:, :], wtern[k][:, :], ACT.Copy, bias=MAGIC, scale=wrec[:, k:k + 1]).then_inc(s_round, 1)

            def body(i, g, last):
                for h, (front, tail) in enumerate(chunks(g, last)):
                    for s in range(4):
                        if s == 2 and not g:
                            (ternary_round if last else ternary_abs)(h)
                        u = i * 8 + (4 * h + s)
                        act.wait_ge(s_turn, u + 1)
                        act.activation(pt[s % 2][:, :, :].rearrange("p a b -> p (a b)"), turn_bank[:, :], ACT.Copy).then_inc(s_pt, 1)
                        if not (last and h == 1 and s == 3):
                            exps(u + 1, (s + 1) % 2)
                        if g and s == 0:
                            gate_exp(i * 2 + (4 + h))
                        for kind, w in front[s]:
                            evict(i, h, kind, w)
                        if s in (1, 2) and not (last and h == 1):
                            rope_upper(i * 4 + (2 + 2 * h), 1 - h, s - 1)
                        act.wait_ge(s_pv, u + 1)
                        act.activation(ot[:, h, s * T:(s + 1) * T], pv_bank[s % 2][:, 0:T], ACT.Copy).then_inc(s_o, 1)
                        if h == 0 and s == 0 and not last:
                            split_w(0, i * 2 + 2)
                            split_wv(i + 1)
                        if h == 1 and s == 1 and not last:
                            split_w(1, i * 2 + 3)
                        for kind, w in tail[s]:
                            evict(i, h, kind, w)
                        if g and s == 3:
                            gate_copy(i * 2 + (5 + h), i % 2 if h == 0 else (i + 1) % 2, 1 - h)

            pairs(act, body)
            barrier(act, 1)
            def latent_copy(n):
                act.wait_ge(s_hw, n + 1)
                bank = ps[n % 2]
                if n < 4:
                    k, g8 = n % 2, n // 2
                    rows = P if k == 0 else QR - P
                    act.activation(wabs[0:rows, k, g8 * 512:(g8 + 1) * 512], bank[0:rows, :], ACT.Copy).then_inc(s_hwc, 1)
                else:
                    act.activation(wvo[:, 2 * (n - 4):2 * (n - 4) + 2, :].rearrange("p a b -> p (a b)"), bank[:, :], ACT.Copy).then_inc(s_hwc, 1)

            def steps(t, x, on):
                if isinstance(t, int) and t == NT:
                    act.wait_ge(in_f, 16 * 7)
                    act.activation(wfhi[:, :, :], wfst[:, :, :], ACT.Copy).then_inc(f_w, 1)
                if on(0):
                    act.wait_ge(e_scale, t + 1)
                    act.activation(y[x][:, :], y[x][:, :], ACT.Copy, bias=MAGIC, scale=sm[x][:, 2:3]).then_inc(e_qm, 1)
                if on(1):
                    act.wait_ge(e_hb, t)
                    act.activation(hb[1 - x][:, :], hb[1 - x][:, :], ACT.Gelu).then_inc(e_gelu, 1)
                if on(0):
                    act.wait_ge(e_qt, t + 1)
                    act.activation(yqt[x][:, :, :].rearrange("p a b -> p (a b)"), qturn[x][:, 0:C], ACT.Copy).then_inc(e_qtc, 1)
                if on(1):
                    act.wait_ge(e_nm, t)
                    act.activation(hb[1 - x][:, :], hb[1 - x][:, :], ACT.Identity, bias=sm[1 - x][:, 10:11],
                                   scale=sm[1 - x][:, 9:10]).then_inc(e_z, 1)
                if on(2):
                    act.wait_ge(e_scale2, t - 1)
                    act.activation(hb[x][:, :], hb[x][:, :], ACT.Copy, bias=MAGIC, scale=sm[x][:, 18:19]).then_inc(e_qm2, 1)
                if on(2):
                    act.wait_ge(e_qt2, t - 1)
                    act.activation(hqt[x][:, :, :].rearrange("p a b -> p (a b)"), turn2[:, :], ACT.Copy).then_inc(e_qtc2, 1)
                for n in LATENT.get(t, ()) if isinstance(t, int) else ():
                    latent_copy(n)

            for t in range(NT):
                act.activation(sga[:, t, :], xtok[:, t, :], ACT.Sigmoid).then_inc(e_sig, 1)
            skewed(act, steps)
            barrier(act, 2)

            def fsteps(t, x, on):
                o = 1 - x
                if on(0):
                    act.activation(fsg[x][:, :], pick(xtok, t, slice(0, C)), ACT.Sigmoid).then_inc(f_sig, 1)
                if on(1):
                    act.wait_ge(f_pc, t)
                    act.activation(junk[:, 0:QR], fp[o][:, 0:QR], ACT.Square, accum_out=fs[o][:, 0:1])
                    act.activation(junk[:, QR:QR + KVR], fp[o][:, QR:QR + KVR], ACT.Square, accum_out=fs[o][:, 1:2]).then_inc(f_sq, 1)
                if on(0):
                    act.wait_ge(f_yt, t + 1)
                    act.activation(fyhi[x][:, :, :].rearrange("p a b -> p (a b)"), fturn[x][:, 0:C], ACT.Copy).then_inc(f_hi, 1)
                if on(3):
                    act.wait_ge(f_t, t - 2)
                    cols = bass.ds((t - 3) * P, P)
                    act.activation(ikt[:, cols], fout[o][:, 3 * P:4 * P], ACT.Copy)
                    act.activation(qrhi[:, 0, cols], fout[o][:, 0:P], ACT.Copy, scale=lnw[:, 0:1])
                    act.activation(qrhi[0:QR - P, 1, cols], fout[o][0:QR - P, P:2 * P], ACT.Copy, scale=lnw[0:QR - P, 1:2])
                    act.drain().then_inc(f_hi2, 1)
                if on(1):
                    act.wait_ge(f_rstd, t)
                    act.activation(qrs[o][:, :], fp[o][:, 0:QR], ACT.Copy, scale=fs[o][:, 12:13]).then_inc(f_qrs, 1)
                    act.activation(pick(iw, t - 1, slice(0, H)), fp[o][:, 448:464], ACT.Copy, scale=H ** -0.5).then_inc(f_free, 1)
                    act.wait_ge(f_ki, t)
                    act.activation(pick(vl, t - 1, slice(0, KVR)), ki[o][:, 0:KVR], ACT.Copy).then_inc(f_vl, 1)

            skewed(act, fsteps)
            def split_q(n, x):
                act.wait_ge(in_q[x], (n - x) * 8 + 16)
                if not isinstance(n, int) or n >= 2:
                    act.wait_ge(q_chunk, n * 2 - 2)
                act.activation(wihi[x][:, :, :], wi[x][:, :, :], ACT.Copy).then_inc(q_whi, 1)

            split_q(0, 0)
            split_q(1, 1)
            barrier(act, 3)
            act.sem_inc(i_relu, 4)
            act.sem_inc(q_abs, 1)

            def stage_q(m, x):
                act.wait_ge(in_q[x], (m - x) * 8 + 16 + 8 * H)
                act.wait_ge(q_wlo, m + (H - 1))
                act.activation(wi[x][:, :, 0:KVR], pick_k(wabs, m), ACT.Copy).then_inc(q_abs, 1)
                act.wait_ge(q_abs, m + 2)
                split_q(m + H, x)

            def pick_k(t, m):
                return t[:, :, bass.ds(m * KVR, KVR)] if not isinstance(m, int) else t[:, :, m * KVR:(m + 1) * KVR]

            def relus(n, s):
                act.wait_ge(q_scores, n * 4 + (s + 1))
                act.wait_ge(i_acc, n * 8 + (2 * s + 2))
                act.activation(rl[s][:, :], iscore[s][:, 0:384], ACT.Relu).then_inc(i_relu, 1)

            with act.Fori(0, PAIRS - 1) as i:
                for h in range(2):
                    n = i * 2 + h
                    split_q(n + 2, h)
                    for s in range(4):
                        relus(n, s)
            def weight_abs(k):
                act.wait_ge(in_u, 16 * k + 16)
                act.activation(wt[k][:, :], ust[:, :], ACT.Abs, accum_out=wsum[:, 2 + k:3 + k]).then_inc(j_abs, 1)

            def weight_round(k):
                act.wait_ge(j_scale, k + 1)
                if k:
                    act.wait_ge(j_tern, k)
                act.activation(uround[:, :], ust[:, :], ACT.Copy, bias=MAGIC, scale=wrec[:, 2 + k:3 + k]).then_inc(j_round, 1)
                act.wait_ge(j_round, k + 1)
                act.activation(uround[:, :], uround[:, :], ACT.Relu, bias=clipc[:, 0:1]).then_inc(j_clip, 1)
                act.wait_ge(j_clip, 2 * k + 1)
                act.activation(uround[:, :], uround[:, :], ACT.Relu, bias=clipc[:, 1:2], scale=-1.0).then_inc(j_clip, 1)

            weight_abs(0)
            for s in range(4):
                relus(H - 2, s)
            stage_q(0, 0)
            for s in range(4):
                relus(H - 1, s)
            stage_q(1, 1)
            for k in range(3):
                if k:
                    weight_abs(k)
                weight_round(k)

            def exps1(u, x):
                act.wait_ge(a_negmax, u * 2 + 2)
                for q, cols in enumerate((slice(0, P), slice(P, 384))):
                    last = act.activation(p1[x][:, cols], score_bank[x][:, cols], ACT.Exp, bias=negm1[x][:, q:q + 1],
                                          accum_out=sums1[x][:, q:q + 1])
                    last.then_inc(a_exp, 1)

            exps1(0, 0)
            exps1(1, 1)

            def turned_copy(u, x):
                act.wait_ge(a_turn, u + 1)
                act.activation(pt1[x][:, :], turn_bank[:, 0:384], ACT.Copy).then_inc(a_pt, 1)

            def out_copy(u, h, s):
                rows = slice(h * 64, h * 64 + 64)
                act.wait_ge(a_pv, u + 1)
                act.activation(ot1[rows, s * T:(s + 1) * T], pv_bank[s % 2][rows, 0:T], ACT.Copy).then_inc(a_o, 1)

            def attention_body(i, first, last):
                for h in range(2):
                    for s in range(4):
                        u = i * 8 + (4 * h + s)
                        turned_copy(u, s % 2)
                        if not (last and h == 1 and s >= 2):
                            exps1(u + 2, s % 2)
                        if not (first and h == 0 and s == 0):
                            out_copy(u - 1, h if s else 1 - h, (s - 1) % 4)
                        if s == 1 and not last:
                            stage_q(i * 2 + (h + 2), h)

            attention_body(0, True, False)
            with act.Fori(1, PAIRS - 1) as i:
                attention_body(i, False, False)
            attention_body(PAIRS - 1, False, True)
            out_copy(8 * PAIRS - 1, 1, 3)
            act.drain().then_inc(phase, 1)
            for w in range(4):
                act.wait_ge(a_x, 4 * (PAIRS - 1) + w + 1)
                act.activation(jsg[:, 2 * w:2 * w + 2, :], xtok[:, 2 * w:2 * w + 2, :], ACT.Sigmoid).then_inc(j_sig, 1)
            for g in range(4):
                act.wait_ge(j_yt, g + 1)
                act.activation(yhi[:, :, g * T:(g + 1) * T], yturn[g][:, :].rearrange("p (c n) -> p c n", c=KC), ACT.Copy).then_inc(j_hi, 1)
            act.wait_ge(phase, 5 * 4)
            with act.Fori(0, 2) as n:
                for f in range(NF):
                    act.wait_ge(j_proj, n * NF + (f + 1))
                    act.activation(silu[f % 2][:, :], up_bank[f % 2][:, :], ACT.Silu, scale=wmean[:, 2:3]).then_inc(j_silu, 1)
                    act.wait_ge(j_h, n * NF + (f + 1))
                    act.activation(hhi[:, f, :], h32[f % 2][:, :], ACT.Copy).then_inc(j_hhi, 1)

        @block.vector
        def _(dve):
            ch = Chain(dve, dch)
            dve.wait_ge(in_k, 16)
            for c in range(KC):
                dve.tensor_scalar(ek[:, c, :], kt[:, c, :], 30.0, None, ALU.min).then_inc(s_kmin, 1)
            dve.wait_ge(in_par, 32)
            dve.tensor_reduce(tf[:, :], condb[:, :, :], AX.X, ALU.add).then_inc(s_tf, 1)
            dve.wait_ge(s_tf, 2)
            ch.step(dve.tensor_scalar(tf[:, :], tf[:, :], 1.0, None, ALU.add))
            ch.step(dve.reciprocal(tf[:, :], tf[:, :]))
            ch.did(dve.tensor_scalar(dfac[:, :], tf[:, :], 0.5, 0.5, ALU.mult, ALU.add))
            ch.did(dve.tensor_scalar(gate[:, :], tf[:, :], 0.2, 0.8, ALU.mult, ALU.add))
            ch.wait()
            dve.wait_ge(s_decay, 1)
            for b in range(B):
                ch.did(dve.tensor_scalar(decay[:, :, b], ew[:, :], dfac[:, b:b + 1], None, ALU.mult))
            for c in range(KC):
                dve.wait_ge(s_ek, c + 1)
                ch.did(dve.tensor_tensor(ekv[:, c, :], ek[:, c, :], kt[:, c, :], ALU.mult))
            ch.wait()

            def cols(t, ci, b, rev):
                s = slice((b + 1) * T - 1, b * T - 1 if b else None, -1) if rev else slice(b * T, (b + 1) * T)
                return pick(t, ci, s)

            def gate_scans(lc, ci, bh, batches=(0, 1), bufs=gbuf):
                nf, nb, df, db, euk, dd = bufs
                for j in batches:
                    b = 2 * bh + j
                    dk = pick(decay, lc, slice(b, b + 1)).broadcast_to([P, T])
                    fw = slice(j * T, (j + 1) * T)
                    bw = slice((j + 1) * T - 1, j * T - 1 if j else None, -1)
                    for src, f, r in ((ekv, nf, nb), (ek, df, db)):
                        dve.tensor_tensor_scan(f[:, fw], dk, cols(src, ci, b, False), 0.0, ALU.mult, ALU.add)
                        back = cols(src, ci, b, True) if isinstance(ci, int) else r[:, bw]
                        last = dve.tensor_tensor_scan(r[:, bw], dk, back, 0.0, ALU.mult, ALU.add)
                    last.then_inc(s_scan, 1)

            def gate_ukmin(lc, ci, bh, bufs=gbuf):
                euk = bufs[4]
                u = par[:, 1, lc:lc + 1] if isinstance(lc, int) else par[:, 1, bass.ds(lc, 1)]
                dve.tensor_scalar(euk[:, :], pick(kt, ci, slice(bh * HALF, (bh + 1) * HALF)), u, 30.0,
                                  ALU.add, ALU.min).then_inc(s_ukmin, 1)

            def gate_dd(gu, ci, bh, bufs=gbuf):
                euk, dd = bufs[4:]
                s = slice(bh * HALF, (bh + 1) * HALF)
                dve.wait_ge(s_euk, gu + 1)
                dve.tensor_tensor(dd[:, :], euk[:, :], pick(ek, ci, s), ALU.subtract).then_inc(s_dd, 1)

            def gate_den(gu, bufs=gbuf):
                df = bufs[2]
                dve.wait_ge(s_sums, gu + 1)
                ch.step(dve.tensor_scalar(df[:, :], df[:, :], 1e-8, None, ALU.max))

            def gate_reciprocal(j, bufs=gbuf):
                df = bufs[2]
                ch.step(dve.reciprocal(df[:, j * T:(j + 1) * T], df[:, j * T:(j + 1) * T]))

            def gate_factor(dst, bufs=gbuf):
                return dve.tensor_tensor(dst, bufs[0][:, :], bufs[2][:, :], ALU.mult)

            def rope_front(g, bank, w):
                dve.wait_ge(s_chunk, g + 1)
                dve.tensor_tensor(rt1[w][:, :], chunk_bank[bank][:, :], tabc[:, :], ALU.mult)
                dve.stream_shuffle(rsh[w][:, :], chunk_bank[bank][:, :], SWAP).then_inc(s_shuf, 1)
                dve.drain().then_inc(s_free[bank], 1)

            def gated_y(gu):
                bh, c = divmod(gu, KC)
                dve.wait_ge(s_sig, 1)
                for b in range(2 * bh, 2 * bh + 2):
                    cs = slice(b * T, (b + 1) * T)
                    dve.scalar_tensor_tensor(y32[:, c, cs], xt[:, c, cs], gate[:, b:b + 1], y32[:, c, cs], ALU.mult, ALU.mult)
                dve.drain().then_inc(s_y, 1)

            def lower_y(gu):
                bh, c = divmod(gu, KC)
                cs = slice(bh * HALF, (bh + 1) * HALF)
                dve.wait_ge(s_yhi, gu + 1)
                dve.tensor_tensor(ylo[:, c, cs], y32[:, c, cs], yhi[:, c, cs].bitcast(F32), ALU.subtract).then_inc(s_ylo, 1)

            for gu in range(2 * KC + 2):
                if gu < 2 * KC:
                    bh, c = divmod(gu, KC)
                    z = gate_buffers(gu, True)
                    gate_ukmin(c, c, bh, z)
                if gu > 1:
                    lower_y(gu - 2)
                if gu < 2 * KC:
                    gate_scans(c, c, bh, bufs=z)
                    gate_dd(gu, c, bh, z)
                if gu == 3:
                    dve.wait_ge(in_tab, 32)
                    rope_front(0, 0, 0)
                if 0 < gu <= 2 * KC:
                    bh, c = divmod(gu - 1, KC)
                    z = gate_buffers(gu - 1, True)
                    gate_den(gu - 1, z)
                    gate_reciprocal(0, z)
                    gate_reciprocal(1, z)
                    ch.step(gate_factor(y32[:, c, bh * HALF:(bh + 1) * HALF], z))
                    gated_y(gu - 1)

            def rope_back(rn, w):
                dve.wait_ge(s_t2, rn + w + 1)
                dve.tensor_tensor(rt1[w][:, :], rt1[w][:, :], rsh[w][:, :], ALU.add).then_inc(s_rsum, 1)

            def rope_lower(rn, x, w):
                dve.wait_ge(s_rhi, rn + w + 1)
                s = slice(w * HALF, (w + 1) * HALF)
                lo, hi = slice(0, DR), slice(DR, P)
                q_lower = rlow[hi, s] if x == 0 else qr[x][hi, s]
                k_lower = kr[x][lo, s] if x == 0 else rlow[lo, s]
                dve.tensor_tensor(q_lower, rt1[w][lo, :], qr[x][lo, s].bitcast(F32), ALU.subtract)
                dve.tensor_tensor(k_lower, rt1[w][hi, :], kr[x][hi, s].bitcast(F32), ALU.subtract)
                dve.drain().then_inc(s_rope, 1)

            def negmax(u, par_):
                dve.wait_ge(s_scores, u + 1)
                dve.tensor_reduce(negm[par_][:, :], score_bank[par_][:, :].rearrange("p (q k) -> p q k", q=2),
                                  AX.X, ALU.max, negate=True).then_inc(s_negmax, 1)

            def normalise(u, par_):
                dve.wait_ge(s_exp, u + 1)
                ch.step(dve.reciprocal(rsum[par_][:, :], sums[par_][:, :]))
                for q in range(2):
                    last = dve.tensor_scalar(pr[par_][:, q, :], pr[par_][:, q, :], rsum[par_][:, q:q + 1], None, ALU.mult)
                last.then_inc(s_norm, 1)

            rope_back(0, 0)
            rope_front(5, 1, 1)
            rope_lower(0, 0, 0)
            rope_back(0, 1)
            negmax(0, 0)
            rope_lower(0, 0, 1)
            normalise(0, 0)
            dve.sem_inc(s_x1, 1)
            dve.wait_ge(in_wo, 32)

            def ternary_scales():
                dve.wait_ge(s_tot, 1)
                for k in range(2):
                    ch.step(dve.tensor_scalar(wmean[:, k:k + 1], ps[7][:, k:k + 1], 1.0 / (C * F), 1e-5, ALU.mult, ALU.max))
                    dve.reciprocal(wrec[:, k:k + 1], wmean[:, k:k + 1]).then_inc(s_wscale, 1)

            def ternary_clip(k):
                dve.wait_ge(s_round, k + 1)
                ch.step(dve.tensor_scalar(wround[:, :], wround[:, :], -MAGIC, 1.0, ALU.add, ALU.min))
                dve.tensor_scalar((w1q, w2q)[k][:, :, :].rearrange("p a b -> p (a b)"), wround[:, :], -1.0, None, ALU.max).then_inc(s_tern, 1)

            def body(i, g, last):
                for h, (front, tail) in enumerate(chunks(g, last)):
                    rn = i * 4 + (2 + 2 * h)
                    ropes = ("r", 0) in front[0]
                    for s in range(4):
                        u = i * 8 + (4 * h + s)
                        more = not (last and h == 1 and s == 3)
                        if more:
                            negmax(u + 1, (s + 1) % 2)
                        if ropes and s == 0:
                            rope_front(chunk_at(i, h, "r", 0), bank_at(i, h, "r", 0), 0)
                        if g and s == 2:
                            gate_den(i * 2 + (4 + h))
                            gate_reciprocal(0)
                        if more:
                            normalise(u + 1, (s + 1) % 2)
                        if ropes and s == 0:
                            rope_front(chunk_at(i, h, "r", 1), bank_at(i, h, "r", 1), 1)
                        if ropes and s == 1:
                            rope_back(rn, 0)
                            rope_back(rn, 1)
                        if ropes and s >= 2:
                            rope_lower(rn, 1 - h, s - 2)
                        for kind, w in front[s] + tail[s]:
                            if kind == "o":
                                dve.wait_ge(s_out_chunk, i * 4 + (w + 1))
                                xs = xtok[:, 2 * w:2 * w + 2, :].rearrange("p a b -> p (a b)")
                                dve.tensor_tensor(xs, out_bank[:, :], xs, ALU.add).then_inc(s_x1, 1)
                        if last and h == 0 and s == 0:
                            ternary_scales()
                        if last and s == 3:
                            ternary_clip(h)
                        if g:
                            gu = i * 2 + (4 + h)
                            if s == 0:
                                gate_ukmin(i + 2, i % 2, h)
                                dve.wait_ge(s_rev, i * 2 + (1 + h))
                                gate_scans(i + 2, i % 2, h)
                                gate_dd(gu, i % 2, h)
                            elif s == 2:
                                gate_reciprocal(1)
                                dve.wait_ge(s_gtok, i * 2 + (1 + h))
                                gate_factor(gg[:, :]).then_inc(s_gg, 1)

            pairs(dve, body, ch, 14)
            barrier(dve, 1)
            dve.wait_ge(in_e, 64)

            def quant_scale(src, s_, at, done):
                ch.step(dve.tensor_reduce(s_[:, at:at + 1], src, AX.X, ALU.max, apply_absolute_value=True))
                ch.step(dve.tensor_scalar(s_[:, at + 1:at + 2], s_[:, at:at + 1], 1e-5, 1.0 / 127.0, ALU.max, ALU.mult))
                dve.reciprocal(s_[:, at + 2:at + 3], s_[:, at + 1:at + 2]).then_inc(done, 1)

            def gated(dst, src, t, L, b):
                gcol = gate[:, b:b + 1] if isinstance(b, int) else gate[:, bass.ds(b, 1)]
                fac = gtok[:, 2 * L:2 * L + 2, t:t + 1, :] if isinstance(t, int) else gtok[:, 2 * L:2 * L + 2, bass.ds(t, 1), :]
                return dve.scalar_tensor_tensor(dst.rearrange("p (l n) -> p l n", l=2), src.rearrange("p (l n) -> p l n", l=2), gcol,
                                                fac.rearrange("p l t n -> p l (t n)"), ALU.mult, ALU.mult)

            def steps(t, x, on):
                o = 1 - x
                if on(0):
                    dve.wait_ge(e_sig, t + 1)
                    ch.step(gated(y[x][:, :], pick(sga, t, slice(0, C)), t, 0, t // 2))
                    quant_scale(y[x][:, :], sm[x], 0, e_scale)
                if on(1):
                    dve.wait_ge(e_h, t)
                    ch.step(dve.tensor_scalar(sm[o][:, 3:4], sm[o][:, 1:2], wmean[:, 0:1], None, ALU.mult))
                    for n in range(2):
                        last = dve.scalar_tensor_tensor(hb[o][:, n * 512:(n + 1) * 512], ffn1[o][n][:, :], sm[o][:, 3:4],
                                                        b1b[:, n * 512:(n + 1) * 512], ALU.mult, ALU.add)
                    last.then_inc(e_hb, 1)
                if on(0):
                    dve.wait_ge(e_qm, t + 1)
                    dve.tensor_scalar(yq[x][:, :], y[x][:, :], -MAGIC, None, ALU.add).then_inc(e_q, 1)
                if on(1):
                    dve.wait_ge(e_gelu, t)
                    for n in range(2):
                        ch.did(dve.bn_stats(sm[o][:, 32 + 6 * n:38 + 6 * n], hb[o][:, n * 512:(n + 1) * 512]))
                    ch.wait()
                    dve.sem_inc(s_pause, 1)
                    ch.step(dve.bn_aggr(sm[o][:, 6:8], sm[o][:, 32:44]))
                    dve.tensor_scalar(sm[o][:, 8:9], sm[o][:, 7:8], 1e-5, None, ALU.add).then_inc(e_ve, 1)
                if on(3):
                    dve.wait_ge(e_y2, t - 2)
                    dve.wait_ge(e_xb, t - 2)
                    ch.wait()
                    dve.scalar_tensor_tensor(pick(xtok, t - 3, slice(0, C)), ffn2[o][:, 0:C], sm[o][:, 19:20], xb[o][:, :],
                                             ALU.mult, ALU.add).then_inc(e_x2, 1)
                if on(1):
                    dve.wait_ge(e_rstd, t)
                    dve.tensor_scalar(sm[o][:, 10:11], sm[o][:, 6:7], sm[o][:, 9:10], -1.0, ALU.mult, ALU.mult).then_inc(e_nm, 1)
                if on(2):
                    dve.wait_ge(e_beta, t - 1)
                    quant_scale(hb[x][:, :], sm[x], 16, e_scale2)
                if on(2):
                    dve.wait_ge(e_qm2, t - 1)
                    dve.tensor_scalar(hq[x][:, :], hb[x][:, :], -MAGIC, None, ALU.add).then_inc(e_q2, 1)
                    ch.did(dve.tensor_scalar(sm[x][:, 19:20], sm[x][:, 17:18], wmean[:, 1:2], None, ALU.mult))

            skewed(dve, steps, ch, 2 * 10)
            barrier(dve, 2)
            dve.wait_ge(in_f, 16 * 7)

            def fsteps(t, x, on):
                o = 1 - x
                if on(0):
                    dve.wait_ge(f_sig, t + 1)
                    gated(fy[x][:, :], fsg[x][:, :], t, 1, t // 2).then_inc(f_y, 1)
                if on(1):
                    s_ = fs[o]
                    dve.wait_ge(f_p, t)
                    dve.tensor_copy(fp[o][:, :], fproj[o][:, 0:464]).then_inc(f_pc, 1)
                    dve.wait_ge(f_pc, t)
                    ch.step(dve.bn_stats(s_[:, 16:22], fp[o][:, 320:448]))
                    dve.sem_inc(s_pause, 1)
                    ch.step(dve.bn_aggr(s_[:, 2:4], s_[:, 16:22]))
                    dve.wait_ge(f_sq, t)
                    ch.did(dve.tensor_scalar(s_[:, 8:9], s_[:, 0:1], 1.0 / QR, 1e-6, ALU.mult, ALU.add))
                    ch.did(dve.tensor_scalar(s_[:, 9:10], s_[:, 1:2], 1.0 / KVR, 1e-6, ALU.mult, ALU.add))
                    dve.tensor_scalar(s_[:, 10:11], s_[:, 3:4], 1e-6, None, ALU.add).then_inc(f_bn, 1)
                if on(0):
                    dve.wait_ge(f_hi, t + 1)
                    dve.tensor_tensor(fylo[x][:, :, :].rearrange("p a b -> p (a b)"), fturn[x][:, 0:C],
                                      fyhi[x][:, :, :].rearrange("p a b -> p (a b)").bitcast(F32), ALU.subtract).then_inc(f_lo, 1)
                if on(3):
                    dve.wait_ge(f_hi2, t - 2)
                    cols = bass.ds((t - 3) * P, P)
                    for k, rows in ((0, P), (1, QR - P)):
                        dve.scalar_tensor_tensor(qrlo[0:rows, k, cols], fout[o][0:rows, k * P:(k + 1) * P], lnw[0:rows, k:k + 1],
                                                 qrhi[0:rows, k, cols].bitcast(F32), ALU.mult, ALU.subtract)
                    ch.did(dve.tensor_copy(kct[:, cols], fout[o][:, 2 * P:3 * P]))
                if on(1):
                    s_, k_ = fs[o], ki[o]
                    dve.wait_ge(f_rstd, t)
                    ch.did(dve.tensor_scalar(k_[:, P:2 * P], fp[o][:, 320:448], s_[:, 2:3], s_[:, 14:15], ALU.subtract, ALU.mult))
                    ch.did(dve.tensor_copy(k_[:, KVR:P], fp[o][:, 256:320]))
                    ch.did(dve.scalar_tensor_tensor(k_[:, 0:KVR], fp[o][:, QR:QR + KVR], s_[:, 13:14], kvw[:, :], ALU.mult, ALU.mult))
                    ch.wait()
                    ch.step(dve.tensor_tensor(k_[:, P:2 * P], k_[:, P:2 * P], ikw[:, :], ALU.mult))
                    ch.step(dve.tensor_tensor(k_[:, P:2 * P], k_[:, P:2 * P], ikb[:, :], ALU.add))
                    kv = k_[:, :].rearrange("p (s r g h f) -> p s r g h f", s=2, r=2, g=2, h=2)[:, :, 1, :, :, :]
                    ra, rb = kv[:, :, :, 0, :], kv[:, :, :, 1, :]
                    tab = [tb[:, o, :].rearrange("p (s g f) -> p s g f", s=2, g=2) for tb in (ropec, ropes)]
                    r4 = [rp[:, n, :].rearrange("p (s g f) -> p s g f", s=2, g=2) for n in range(4)]
                    for n, (src, tb) in enumerate(((ra, 0), (rb, 1), (ra, 1), (rb, 0))):
                        ch.did(dve.tensor_tensor(r4[n], src, tab[tb], ALU.mult))
                    ch.wait()
                    dve.tensor_tensor(ra, r4[0], r4[1], ALU.subtract)
                    dve.tensor_tensor(rb, r4[2], r4[3], ALU.add).then_inc(f_ki, 1)

            skewed(dve, fsteps, ch, 2 * 14)
            barrier(dve, 3)
            dve.sem_inc(i_acc, 8)

            def front_q(n, w, tab, first=False):
                dve.wait_ge(q_chunk, n * 2 + (w + 1))
                if not first:
                    dve.wait_ge(q_ready, n * 2 + w - 1)
                dve.tensor_tensor(it1[w][:, :], chunk_bank[w][:, :], tab[:, :], ALU.mult).then_inc(q_front, 1)
                dve.stream_shuffle(ish[w][:, :], chunk_bank[w][:, :], SWAP).then_inc(q_front, 1)

            def accumulate(n, s):
                dve.wait_ge(i_relu, n * 4 + (s + 5))
                dve.wait_ge(i_acc, n * 8 + (2 * s + 2))
                for q, (cols, width) in enumerate(((slice(0, P), P), (slice(P, 384), T))):
                    tt = 2 * s + q
                    wcol = iw[:, tt, n:n + 1] if isinstance(n, int) else iw[:, tt, bass.ds(n, 1)]
                    dve.scalar_tensor_tensor(acc[:, tt, 0:width], rl[s][:, cols], wcol, acc[:, tt, 0:width],
                                             ALU.mult, ALU.add).then_inc(i_acc, 1)

            dve.wait_ge(in_i, 32)
            for w in range(2):
                front_q(0, w, tabc1, True)
            dve.wait_ge(i_init, 4)
            with dve.Fori(0, PAIRS - 1) as i:
                for h in range(2):
                    n = i * 2 + h
                    for s in range(4):
                        if s % 2 == 0:
                            front_q(n + 1, s // 2, tabc1)
                        accumulate(n, s)
            dve.wait_ge(in_i2, 32)
            for h in range(2):
                n = H - 2 + h
                for s in range(4):
                    if s % 2 == 0:
                        front_q(n + 1, s // 2, tabc2 if h else tabc1)
                    accumulate(n, s)
            dve.wait_ge(i_acc, 8 + 8 * H)
            widths = [(P, T)[tt % 2] for tt in range(NT)]
            for r in range(TOPK // 8):
                for tt in range(NT):
                    ch.did(dve.max(top8[:, tt, :], acc[:, tt, 0:widths[tt]]))
                ch.wait()
                for tt in range(NT):
                    ch.did(dve.match_replace(acc[:, tt, 0:widths[tt]], top8[:, tt, :], acc[:, tt, 0:widths[tt]], -3.3e38))
                ch.wait()
                if r % 3 == 0:
                    k = r // 3
                    c0 = slice(2 + k, 3 + k)
                    dve.wait_ge(j_tot, k + 1)
                    ch.step(dve.tensor_scalar(wmean[:, c0], out_bank[:, c0], 1.0 / (C * F), 1e-8, ALU.mult, ALU.add))
                    dve.reciprocal(wrec[:, c0], wmean[:, c0]).then_inc(j_scale, 1)
            for tt in range(NT):
                w_ = widths[tt]
                ch.step(dve.tensor_scalar(biasb[:, tt, 0:w_], acc[:, tt, 0:w_], -3.25e38, -1e9, ALU.is_gt, ALU.mult))
                dve.tensor_tensor(biasb[:, tt, 0:w_], biasb[:, tt, 0:w_], causb[:, tt % 2, 0:w_], ALU.min).then_inc(a_bias, 1)

            def negmax1(u, x):
                dve.wait_ge(q_scores, u + (4 * H + 1))
                for q, cols in enumerate((slice(0, P), slice(P, 384))):
                    dve.tensor_reduce(negm1[x][:, q:q + 1], score_bank[x][:, cols], AX.X, ALU.max, negate=True).then_inc(a_negmax, 1)

            def normalise1(u, x):
                dve.wait_ge(a_exp, u * 2 + 2)
                ch.step(dve.reciprocal(rsum1[x][:, :], sums1[x][:, :]))
                for q, cols in enumerate((slice(0, P), slice(P, 384))):
                    dve.tensor_scalar(p1[x][:, cols], p1[x][:, cols], rsum1[x][:, q:q + 1], None, ALU.mult).then_inc(a_norm, 1)

            negmax1(0, 0)
            negmax1(1, 1)
            normalise1(0, 0)

            def add_out(i, w, bank=out_bank):
                dve.wait_ge(a_out, i * 4 + (w + 1))
                xs = xtok[:, 2 * w:2 * w + 2, :].rearrange("p a b -> p (a b)")
                dve.tensor_tensor(xs, bank[:, :], xs, ALU.add).then_inc(a_x, 1)

            def attention_body(i, first, last):
                for h in range(2):
                    n = i * 2 + (H + h)
                    for s in range(4):
                        u = i * 8 + (4 * h + s)
                        if not (last and h == 1 and s == 3):
                            normalise1(u + 1, (s + 1) % 2)
                        if not (last and h == 1 and s >= 2):
                            negmax1(u + 2, s % 2)
                        if s < 2 and not (last and h):
                            front_q(n + 1, s, tabc2)
                        if h == 1 and s >= 2:
                            add_out(i, s - 2)
                        if h == 0 and s < 2 and not first:
                            add_out(i - 1, s + 2)

            attention_body(0, True, False)
            with dve.Fori(1, PAIRS - 1) as i:
                ch.loop(i, 1, 8)
                attention_body(i, False, False)
                ch.close(PAIRS - 2)
            attention_body(PAIRS - 1, False, True)
            for w in (2, 3):
                add_out(PAIRS - 1, w, LAST_OUT[w])
            dve.drain().then_inc(phase, 1)

            def gated_batch(w):
                dve.wait_ge(j_sig, w + 1)
                for t in (2 * w, 2 * w + 1):
                    gated(jy[:, t, :], jsg[:, t, :], t, 2, w).then_inc(j_y, 1)

            def lower_batch(g):
                dve.wait_ge(j_hi, g + 1)
                cols = slice(g * T, (g + 1) * T)
                dve.tensor_tensor(ylo[:, :, cols], yturn[g][:, :].rearrange("p (c n) -> p c n", c=KC),
                                  yhi[:, :, cols].bitcast(F32), ALU.subtract).then_inc(j_lo, 1)

            for w in range(4):
                gated_batch(w)
                if w >= 2:
                    lower_batch(w - 2)
            for g in (2, 3):
                lower_batch(g)
            dve.wait_ge(phase, 5 * 4)
            dve.sem_inc(j_x, 1)
            with dve.Fori(0, 2) as n:
                for f in range(NF):
                    dve.wait_ge(j_silu, n * NF + (f + 1))
                    dve.scalar_tensor_tensor(h32[f % 2][:, :], gate_bank[f % 2][:, :], wmean[:, 3:4], silu[f % 2][:, :],
                                             ALU.mult, ALU.mult).then_inc(j_h, 1)
                    dve.wait_ge(j_hhi, n * NF + (f + 1))
                    dve.tensor_tensor(hlo[:, f, :], h32[f % 2][:, :], hhi[:, f, :].bitcast(F32), ALU.subtract).then_inc(j_hlo, 1)
                for x in range(2):
                    dve.wait_ge(j_down, n * 2 + (x + 1))
                    dve.wait_ge(j_out[x], n * 16 + 16)
                    xs = xtok[:, bass.ds(n * 4 + 2 * x, 2), :].rearrange("p t c -> p (t c)")
                    dve.scalar_tensor_tensor(xo[x][:, :], down_bank[x][:, :], wmean[:, 4:5], xs, ALU.mult, ALU.add).then_inc(j_x, 1)

        @block.tensor
        def _(pe):
            pe.sem_inc(s_free[0], 1)
            pe.sem_inc(s_free[1], 1)
            pe.sem_inc(s_gtok, 1)
            pe.wait_ge(s_const, 2)
            PASSES = ((whi, yhi), (wlo, yhi), (whi, ylo))

            def project(g, bank, uses, x, kind, w, pair=None):
                if kind == "o":
                    pe.wait_ge(s_x1, pair * 4 + (w + 1))
                    out_ = out_bank
                else:
                    pe.wait_ge(s_free[bank], uses + 1)
                    out_ = chunk_bank[bank]
                if kind in "qkr":
                    mt = "qkr".index(kind)
                    n = 0
                    for c in range(KC):
                        for wt, yt in PASSES:
                            last = pe.matmul(out_[:, :], wt[x][:, c, mt * P:(mt + 1) * P], yt[:, c, w * HALF:(w + 1) * HALF],
                                             start=(n == 0), stop=(n == 5))
                            n += 1
                elif kind == "v":
                    for j in range(2):
                        tt = 2 * w + j
                        n = 0
                        for c in range(KC):
                            for wt, yt in ((wvhi, yhi), (wvlo, yhi), (wvhi, ylo)):
                                last = pe.matmul(out_[:, j * 256:(j + 1) * 256], yt[:, c, tt * P:(tt + 1) * P], wt[:, c, :],
                                                 start=(n == 0), stop=(n == 5))
                                n += 1
                elif kind == "o":
                    for j in range(2):
                        tt = 2 * w + j
                        for h in range(2):
                            wh = pick(wo, pair * 2 + h, slice(0, C))
                            last = pe.matmul(out_[:, j * 256:(j + 1) * 256], ot[:, h, tt * P:(tt + 1) * P], wh,
                                             start=(h == 0), stop=(h == 1))
                else:
                    for q in range(4):
                        last = pe.transpose(out_[:, q * P:(q + 1) * P], gg[:, q * P:(q + 1) * P], ident[:, :])
                last.then_inc(s_out_chunk if kind == "o" else s_chunk, 1)

            def scores(u, hd, x, b):
                pe.wait_ge(s_qk, hd * 4 + (2 if b < 2 else 4))
                pe.wait_ge(s_rope, hd * 2 + (1 if b < 2 else 2))
                bank = score_bank[b % 2]
                for q in range(2):
                    qs = slice(b * T + q * P, b * T + (q + 1) * P)
                    ks = slice(b * T, (b + 1) * T)
                    pe.matmul(bank[:, q * T:(q + 1) * T], qn[x][:, qs], kn[x][:, ks], start=True, stop=False)
                    pe.matmul(bank[:, q * T:(q + 1) * T], qr[x][:, qs], kr[x][:, ks], start=False, stop=False)
                    low = (rlow[DR:P, qs], kr[x][DR:P, ks]) if x == 0 else (qr[x][0:DR, qs], rlow[0:DR, ks])
                    last = pe.matmul(bank[:, q * T:(q + 1) * T], low[0], low[1], start=False, stop=True)
                last.then_inc(s_scores, 1)

            def turn(u, par_):
                pe.wait_ge(s_norm, u + 1)
                pe.wait_ge(s_pt, u + 1)
                for k in range(2):
                    for q in range(2):
                        last = pe.transpose(turn_bank[:, k * T + q * P:k * T + (q + 1) * P],
                                            pr[par_][:, q, k * P:(k + 1) * P], ident[:, :])
                last.then_inc(s_turn, 1)

            def pv(u, pair, h, b):
                pe.wait_ge(s_pt, u + 2)
                pe.wait_ge(s_v, pair * 4 + (b + 1))
                for k in range(2):
                    last = pe.matmul(pv_bank[b % 2][:, 0:T], v[:, 2 * b + k, h * DN:(h + 1) * DN],
                                     pt[b % 2][:, k, :], start=(k == 0), stop=(k == 1))
                last.then_inc(s_pv, 1)

            pe.wait_ge(s_wlo, 1)
            pe.wait_ge(s_wvlo, 1)
            for n, (kind, w) in enumerate(FIRST_CHUNKS):
                pe.wait_ge(s_ylo, KC * (w if kind in "rqk" else w // 2) + KC)
                if n == 8:
                    scores(0, 0, 0, 0)
                project(n, n % 2, n // 2, 0, kind, w)

            def chunk(i, h, kind, w):
                if (kind, w) == ("r", 0):
                    pe.wait_ge(s_wlo, i * 2 + (2 + h))
                if (kind, w) == ("v", 0):
                    pe.wait_ge(s_wvlo, i + 2)
                if kind == "o":
                    pe.wait_ge(s_o, i * 8 + (4 + w + 1))
                if kind == "g":
                    pe.wait_ge(s_gg, i * 2 + (1 + h))
                if kind == "o":
                    project(0, None, None, None, kind, w, i)
                else:
                    project(0, bank_at(i, h, kind, w), uses_at(i, h, kind, w), 1 - h, kind, w, i)

            def body(i, g, last):
                if last:
                    pe.wait_ge(s_abs, 2)
                    pe.wait_ge(s_ones, 1)
                    pe.wait_ge(s_x1, 4 * i + 1)
                    pe.matmul(ps[7][:, 0:2], ones0[:, :], wsum[:, 0:2], start=True, stop=True).then_inc(s_tot, 1)
                for h, (front, tail) in enumerate(chunks(g, last)):
                    for s in range(4):
                        u = i * 8 + (4 * h + s)
                        if s < 3:
                            scores(u + 1, i * 2 + h, h, s + 1)
                        elif not (last and h == 1):
                            scores(u + 1, i * 2 + (h + 1), 1 - h, 0)
                        turn(u, s % 2)
                        for kind, w in front[s]:
                            chunk(i, h, kind, w)
                        pv(u, i, h, s)
                        for kind, w in tail[s]:
                            chunk(i, h, kind, w)

            pairs(pe, body)
            barrier(pe, 1)
            def latent_products(n):
                pe.wait_ge(in_hw, 16)
                if n >= 2:
                    pe.wait_ge(s_hwc, n - 1)
                bank = ps[n % 2]
                if n < 4:
                    k, g8 = n % 2, n // 2
                    rows = P if k == 0 else QR - P
                    for j in range(8):
                        hd = 8 * g8 + j
                        last = pe.matmul(bank[0:rows, j * 64:(j + 1) * 64], hw[:, hd, k * P:k * P + rows], hw[:, hd, QR:QR + 64],
                                         start=True, stop=True)
                else:
                    for j in range(2):
                        for h in range(2):
                            hd = 4 * (n - 4) + 2 * j + h
                            last = pe.matmul(bank[h * 64:(h + 1) * 64, j * C:(j + 1) * C], hw[:, hd, 256:320], hw[:, hd, 320:576],
                                             start=True, stop=True)
                last.then_inc(s_hw, 1)

            def steps(t, x, on):
                if on(0):
                    pe.wait_ge(e_q, t + 1)
                    for c in range(KC):
                        last = pe.transpose(qturn[x][:, c * P:(c + 1) * P], yq[x][:, c * P:(c + 1) * P], identb[:, :])
                    last.then_inc(e_qt, 1)
                if on(0):
                    pe.wait_ge(e_qtc, t + 1)
                    for n in range(2):
                        for c in range(KC):
                            last = pe.matmul(ffn1[x][n][:, :], yqt[x][:, c, :], w1q[:, c, n * 512:(n + 1) * 512], start=(c == 0), stop=(c == 1))
                    last.then_inc(e_h, 1)
                if on(2):
                    pe.wait_ge(e_q2, t - 1)
                    for f in range(NF):
                        last = pe.transpose(turn2[:, f * P:(f + 1) * P], hq[x][:, f * P:(f + 1) * P], identb[:, :])
                    last.then_inc(e_qt2, 1)
                if on(2):
                    pe.wait_ge(e_qtc2, t - 1)
                    for f in range(NF):
                        last = pe.matmul(ffn2[x][:, 0:C], hqt[x][:, f, :], w2q[:, f, :], start=(f == 0), stop=(f == NF - 1))
                    last.then_inc(e_y2, 1)
                for n in LATENT.get(t, ()) if isinstance(t, int) else ():
                    latent_products(n)

            skewed(pe, steps)
            barrier(pe, 2)
            pe.wait_ge(f_wlo, 1)

            def fsteps(t, x, on):
                if on(0):
                    pe.wait_ge(f_y, t + 1)
                    for c in range(KC):
                        last = pe.transpose(fturn[x][:, c * P:(c + 1) * P], fy[x][:, c * P:(c + 1) * P], ident[:, :])
                    last.then_inc(f_yt, 1)
                if on(0):
                    pe.wait_ge(f_lo, t + 1)
                    n = 0
                    for c in range(KC):
                        for yt, wt_ in ((fyhi, wfhi), (fylo, wfhi), (fyhi, wflo)):
                            last = pe.matmul(fproj[x][:, 0:464], yt[x][:, c, :], wt_[:, c, :], start=(n == 0), stop=(n == 5))
                            n += 1
                    last.then_inc(f_p, 1)
                if on(2):
                    pe.wait_ge(f_qrs, t - 1)
                    pe.wait_ge(f_ki, t - 1)
                    pe.transpose(fout[x][:, 0:P], qrs[x][:, 0:P], ident[:, :])
                    pe.transpose(fout[x][0:QR - P, P:2 * P], qrs[x][:, P:QR], ident[:, :])
                    for j in range(2):
                        last = pe.transpose(fout[x][:, (2 + j) * P:(3 + j) * P], ki[x][:, j * P:(j + 1) * P], ident[:, :])
                    last.then_inc(f_t, 1)

            skewed(pe, fsteps)
            barrier(pe, 3)
            def project_q(n, x, w, first=False):
                pe.wait_ge(q_wlo, n + 1)
                if not first:
                    pe.wait_ge(q_front, n * 4 + (2 * w - 2))
                cols = slice(w * HALF, (w + 1) * HALF)
                k = 0
                for c, rows in ((0, P), (1, QR - P)):
                    for wt_, qt_ in ((wihi, qrhi), (wilo, qrhi), (wihi, qrlo)):
                        last = pe.matmul(chunk_bank[w][:, :], wt_[x][0:rows, c, :], qt_[0:rows, c, cols], start=(k == 0), stop=(k == 5))
                        k += 1
                last.then_inc(q_chunk, 1)

            def index_scores(n, x, s):
                pe.wait_ge(q_ready, n * 2 + (1 if s < 2 else 2))
                pe.wait_ge(i_relu, n * 4 + (s + 1))
                bank = iscore[s]
                pe.matmul(bank[:, 0:P], iq[x][:, s * T:s * T + P], ikt[:, s * T:s * T + P], start=True, stop=True)
                pe.matmul(bank[:, P:384], iq[x][:, s * T + P:(s + 1) * T], ikt[:, s * T:(s + 1) * T], start=True,
                          stop=True).then_inc(q_scores, 1)

            for w in range(2):
                project_q(0, 0, w, True)
            with pe.Fori(0, PAIRS - 1) as i:
                for h in range(2):
                    n = i * 2 + h
                    for s in range(4):
                        if s % 2 == 0:
                            project_q(n + 1, 1 - h, s // 2)
                        index_scores(n, h, s)
            for h in range(2):
                n = H - 2 + h
                for s in range(4):
                    if s % 2 == 0:
                        project_q(n + 1, 1 - h, s // 2)
                    index_scores(n, h, s)

            def scores1(u, n, x, s, first=False):
                pe.wait_ge(q_ready, n * 2 + (1 if s < 2 else 2))
                if first:
                    pe.wait_ge(a_bias, 2 * s + 2)
                bank = score_bank[s % 2]
                for q, (c0, width) in enumerate(((0, P), (P, T))):
                    pe.matmul(bank[:, c0:c0 + width], iq[x][:, s * T + q * P:s * T + (q + 1) * P], kct[:, s * T:s * T + width],
                              start=True, stop=False)
                    last = pe.matmul(bank[:, c0:c0 + width], identb[:, :], biasb[:, 2 * s + q, 0:width], start=False, stop=True)
                last.then_inc(q_scores, 1)

            for k in range(3):
                pe.wait_ge(j_abs, k + 1)
                pe.wait_ge(s_ones, 2)
                pe.matmul(out_bank[:, 2 + k:3 + k], ones1[:, :], wsum[:, 2 + k:3 + k], start=True, stop=True).then_inc(j_tot, 1)
            for s in range(2):
                scores1(s, H, 0, s, True)

            def pv1(u, h, s):
                rows = slice(h * 64, h * 64 + 64)
                bank = pv_bank[s % 2]
                pe.matmul(bank[rows, 0:T], vl[:, 2 * s, :], pt1[s % 2][:, 0:T], start=True, stop=False)
                pe.matmul(bank[rows, P:T], vl[:, 2 * s + 1, :], pt1[s % 2][:, T:384], start=False, stop=True).then_inc(a_pv, 1)

            def attention_body(i, first, last):
                for h in range(2):
                    n = i * 2 + (H + h)
                    for s in range(4):
                        u = i * 8 + (4 * h + s)
                        pe.wait_ge(a_norm, u * 2 + 2)
                        before = not (first and h == 0 and s == 0)
                        if before:
                            pe.wait_ge(a_pt, u)
                        for c, cols in enumerate((slice(0, P), slice(P, T), slice(T, 384))):
                            t_ = pe.transpose(turn_bank[:, c * P:(c + 1) * P], p1[s % 2][:, cols], ident[:, :])
                        t_.then_inc(a_turn, 1)
                        if s < 2:
                            scores1(u + 2, n, h, s + 2, first and h == 0)
                        elif not (last and h == 1):
                            scores1(u + 2, n + 1, 1 - h, s - 2)
                        if s < 2 and not (last and h):
                            project_q(n + 1, 1 - h, s)
                        if h == 1 and s >= 2:
                            project_out(i, s - 2)
                        if h == 0 and s < 2 and not first:
                            project_out(i - 1, s + 2)
                        if before:
                            pv1(u - 1, h if s else 1 - h, (s - 1) % 4)

            def project_out(i, w, bank=out_bank):
                pe.wait_ge(a_o, i * 8 + (4 + w + 1))
                if bank is out_bank and not (isinstance(i, int) and i == 0 and w == 0):
                    pe.wait_ge(a_x, i * 4 + w)
                for j in range(2):
                    tt = 2 * w + j
                    last = pe.matmul(bank[:, j * C:(j + 1) * C], ot1[:, tt * P:(tt + 1) * P], pick(wvo, i, slice(0, C)),
                                     start=True, stop=True)
                last.then_inc(a_out, 1)

            attention_body(0, True, False)
            with pe.Fori(1, PAIRS - 1) as i:
                attention_body(i, False, False)
            attention_body(PAIRS - 1, False, True)
            pe.wait_ge(a_pt, 8 * PAIRS)
            pv1(8 * PAIRS - 1, 1, 3)
            for w in (2, 3):
                project_out(PAIRS - 1, w, LAST_OUT[w])
            pe.drain().then_inc(phase, 1)
            for g in range(4):
                for j in range(2):
                    pe.wait_ge(j_y, 2 * g + j + 1)
                    for c in range(KC):
                        last = pe.transpose(yturn[g][:, c * T + j * P:c * T + (j + 1) * P], jy[:, 2 * g + j, c * P:(c + 1) * P], ident[:, :])
                last.then_inc(j_yt, 1)
            pe.wait_ge(j_tern, 3)
            pe.wait_ge(phase, 5 * 4)
            def down(n, f):
                pe.wait_ge(j_hlo, n * NF + (f + 1))
                if f == 0:
                    pe.wait_ge(j_x, n * 2 + 1)
                for j in range(4):
                    cols = slice((j % 2) * C, (j % 2 + 1) * C)
                    for ht in (hhi, hlo):
                        last = pe.matmul(down_bank[j // 2][:, cols], ht[:, f, j * P:(j + 1) * P], wt[2][:, f * C:(f + 1) * C],
                                         start=(f == 0 and ht is hhi and j % 2 == 0),
                                         stop=(f == NF - 1 and ht is hlo and j % 2 == 1))
                    if f == NF - 1 and j % 2:
                        last.then_inc(j_down, 1)

            with pe.Fori(0, 2) as n:
                pe.wait_ge(j_lo, n * 2 + 2)
                for f in range(NF):
                    if f >= 2:
                        pe.wait_ge(j_h, n * NF + (f - 1))
                    for k, bank in ((0, up_bank), (1, gate_bank)):
                        m = 0
                        for c in range(KC):
                            for yt in (yhi, ylo):
                                last = pe.matmul(bank[f % 2][:, :], wt[k][:, c * F + f * P:c * F + (f + 1) * P],
                                                 yt[:, c, bass.ds(n * HALF, HALF)], start=(m == 0), stop=(m == 3))
                                m += 1
                    last.then_inc(j_proj, 1)
                    if f >= 2:
                        down(n, f - 2)
                for f in (NF - 2, NF - 1):
                    down(n, f)


_P64 = np.concatenate([np.arange(0, 16), np.arange(32, 48), np.arange(16, 32), np.arange(48, 64)])
_FREQ = np.concatenate([np.arange(0, 16), np.arange(0, 16), np.arange(16, 32), np.arange(16, 32)])
_SIGN = np.concatenate([-np.ones(16), np.ones(16), -np.ones(16), np.ones(16)]).astype(np.float32)


def _angles():
    inv = (1.0 / 10000.0 ** (np.arange(0, 64, 2, dtype=np.float32) / 64)).astype(np.float32)
    f = np.arange(T, dtype=np.float32)[:, None] * inv[None, :]
    return np.cos(f).astype(np.float32), np.sin(f).astype(np.float32)


def _chan(x):
    return np.ascontiguousarray(np.asarray(x).T.reshape(2, P, -1).transpose(1, 0, 2))


def host_arrays(i):
    g = {k: np.asarray(v) for k, v in i.items()}
    r = {}
    x = g["x"].reshape(N, C)
    r["xt"], r["kt"] = _chan(x), _chan(g["fside_BxSxS_0"].reshape(N, C))
    r["xtok"] = np.ascontiguousarray(x.reshape(NT, P, C).transpose(1, 0, 2))
    names = ["L0_cond", "L0_cond2", "L1_cond", "L1_cond2"]
    r["par"] = np.ascontiguousarray(np.stack([np.stack([g[n + s].reshape(2, P) for n in names]) for s in ("_w", "_u")])
                                    .transpose(3, 0, 1, 2).reshape(P, 2, 8))
    r["cond"] = np.ascontiguousarray(np.broadcast_to(g["cond_512"][None], (P, B, 64)))
    wq, wk = g["L0_attn_Wq"], g["L0_attn_Wk"]
    heads = []
    for h in range(H):
        rows = np.concatenate([wq[h * DN:(h + 1) * DN], wk[h * DN:(h + 1) * DN],
                               wq[H * DN + h * DR:H * DN + (h + 1) * DR][_P64],
                               wk[H * DN + h * DR:H * DN + (h + 1) * DR][_P64]])
        heads.append(_chan(rows))
    r["wqk0"] = np.stack(heads)
    r["wv0"] = np.stack([_chan(g["L0_attn_Wv"][p * 256:(p + 1) * 256]) for p in range(PAIRS)])
    r["wo0"] = np.ascontiguousarray(g["L0_attn_Wo"].T.reshape(H, DN, C).transpose(1, 0, 2))
    cos, sin = _angles()
    cr, sr = cos.T[_FREQ], sin.T[_FREQ] * _SIGN[:, None]
    q8 = np.float32(DR ** -0.5)
    r["tabc0"] = np.tile(np.concatenate([cr * q8, cr]), (1, 2)).astype(np.float32)
    r["tabs0"] = np.tile(np.concatenate([sr * q8, sr]), (1, 2)).astype(np.float32)
    r["w12"] = np.stack([_chan(g["L0_ffn_w1"]).reshape(P, 2048),
                         g["L0_ffn_w2"].T.reshape(NF, P, C).transpose(1, 0, 2).reshape(P, 2048)])

    def rows(v):
        return np.ascontiguousarray(np.broadcast_to(v[None], (P,) + v.shape))

    r["b1"], r["gamma"], r["beta"], r["b2"] = (rows(g["L0_ffn_" + n]) for n in ("b1", "gamma", "beta", "b2"))
    qb = g["L1_attn_q_b_w"].reshape(H, DN + DR, QR)
    kvb = g["L1_attn_kv_b_w"].reshape(H, 2 * DN, KVR)
    ow = g["L1_attn_o_w"].T.reshape(H, DN, C)
    r["hw"] = np.ascontiguousarray(np.concatenate([qb[:, :DN], kvb[:, :DN], kvb[:, DN:], ow], axis=2).transpose(1, 0, 2))
    kva, ikw_ = g["L1_attn_kv_a_w"], g["L1_attn_idx_wk_w"]
    order = np.concatenate([np.arange(64, 128), _P64])
    r["wf"] = _chan(np.concatenate([g["L1_attn_q_a_w"], kva[:KVR], kva[KVR:][_P64], ikw_[order], g["L1_attn_idx_wproj_w"]]))
    fc = np.concatenate([np.arange(0, 16), np.arange(16, 32)])
    c4, s4 = (np.tile(v[:, fc], (1, 2)).reshape(2, P, 64).transpose(1, 0, 2) for v in (cos, sin))
    r["ropec"], r["ropes"] = np.ascontiguousarray(c4), np.ascontiguousarray(s4)
    r["ikw"], r["ikb"] = rows(g["L1_attn_idx_kn_w"][order]), rows(g["L1_attn_idx_kn_b"][order])
    r["kvw"] = rows(g["L1_attn_kv_a_ln_w"])
    iqb = g["L1_attn_idx_wq_b_w"].reshape(H, P, QR)[:, order]
    qpe = qb[:, DN:][:, _P64]

    def padded(w):
        z = np.zeros((H, 2 * P, w.shape[1]), np.float32)
        z[:, :QR] = w.transpose(0, 2, 1)
        return np.ascontiguousarray(z.reshape(H, 2, P, -1).transpose(0, 2, 1, 3))

    r["wi"], r["wq1"] = padded(iqb), padded(qpe)
    one, zero = np.ones((DR, T), np.float32), np.zeros((DR, T), np.float32)
    sc = np.float32((DN + DR) ** -0.5)
    tc, ts = np.tile(np.concatenate([one, cr]), (1, 2)), np.tile(np.concatenate([zero, sr]), (1, 2))
    r["tabc1"], r["tabs1"] = tc.astype(np.float32), ts.astype(np.float32)
    r["tabc2"], r["tabs2"] = (tc * sc).astype(np.float32), (ts * sc).astype(np.float32)
    r["w3"] = np.stack([_chan(g["L1_ffn_W_up"]).reshape(P, 2048), _chan(g["L1_ffn_W_gate"]).reshape(P, 2048),
                        g["L1_ffn_W_down"].T.reshape(NF, P, C).transpose(1, 0, 2).reshape(P, 2048)])
    ln = np.zeros(256, np.float32)
    ln[:QR] = g["L1_attn_q_a_ln_w"]
    r["lnw"] = np.ascontiguousarray(ln.reshape(2, P).T)
    return r


def kernel(**inputs):
    import concourse.bacc as bacc
    from concourse.bass_utils import run_bass_kernel_spmd

    arrays = host_arrays(inputs)
    nc = bacc.Bacc("TRN2", target_bir_lowering=False, num_devices=1)
    aps = {k: nc.dram_tensor("in_" + k, v.shape, mybir.dt.from_np(v.dtype), kind="ExternalInput").ap()
           for k, v in arrays.items()}
    out = nc.dram_tensor("out_x", (P, NT, C), F32, kind="ExternalOutput").ap()
    adaln_block(nc, aps, out)
    r = run_bass_kernel_spmd(nc, [{"in_" + k: v for k, v in arrays.items()}], core_ids=[0])
    return r.results[0]["out_x"].transpose(1, 0, 2).reshape(B, T, C)
```
